# Optimizing a Trainium2 kernel written in Bass

```python
import numpy as np
import jax
import jax.numpy as jnp

def _softmax(x, axis=-1):
    return jax.nn.softmax(x, axis=axis)

def _gelu(x):
    return jax.nn.gelu(x, approximate=True)

def _silu(x):
    return jax.nn.silu(x)

def _sigmoid(x):
    return jax.nn.sigmoid(x)

def _layernorm(x, axis=-1, eps=1e-05):
    m = jnp.mean(x, axis=axis, keepdims=True)
    v = jnp.var(x, axis=axis, keepdims=True)
    return (x - m) / jnp.sqrt(v + eps)

def _scatter_add(tgt, idx, src, axis=0):
    return tgt.at[idx].add(src)

def _segment_sum(src, seg, n):
    return jax.ops.segment_sum(src, seg, n)
kernel_name = 'mk_hybrid_d1_jaxref_r8_0edd76'

def setup_inputs(seed: int=0):
    np.random.seed(seed)
    _w = jnp.asarray

    def _L0_attn_a_setup():
        import math
        import jax, jax.numpy as jnp
        import numpy as np
        NUM_HEADS = 32
        HIDDEN = 512
        HEAD_DIM = HIDDEN // NUM_HEADS
        NEG_INF = -1e+30

        def _alibi_slopes(n: int) -> jnp.ndarray:
            cp2 = 2 ** math.floor(math.log2(n))
            base = 2.0 ** (-2.0 ** (-(math.log2(cp2) - 3)))
            slopes = base ** np.arange(1, cp2 + 1, dtype=np.float64)
            if cp2 != n:
                extra_base = 2.0 ** (-2.0 ** (-(math.log2(2 * cp2) - 3)))
                rem = min(cp2, n - cp2)
                extra = extra_base ** np.arange(1, 1 + 2 * rem, 2, dtype=np.float64)
                slopes = np.concatenate([slopes, extra])
            return jnp.asarray(slopes, dtype=jnp.float32)
        key = jax.random.key(seed)
        k1, k2, k3 = jax.random.split(key, 3)
        B, S = (2, 256)
        hidden_states = jax.random.normal(k1, (B, S, HIDDEN), dtype=jnp.float32)
        Wqkv = jax.random.normal(k2, (HIDDEN, NUM_HEADS * HEAD_DIM + 2 * HEAD_DIM), dtype=jnp.float32) * 0.02
        Wo = jax.random.normal(k3, (HIDDEN, HIDDEN), dtype=jnp.float32) * 0.02
        return {'hidden_states': hidden_states, 'Wqkv': Wqkv, 'Wo': Wo}
    _L0_attn_a_in = _L0_attn_a_setup()

    def _L0_attn_b_setup():
        import jax, jax.numpy as jnp
        import numpy as np
        HIDDEN = 512
        HEAD_DIM = 128
        N_Q_HEADS = 32
        N_KV_HEADS = 8
        SLIDING_WINDOW = 128
        ROPE_THETA = 10000.0
        BATCH, SEQ = (1, 256)

        def _rope(t, pos):
            d = t.shape[-1]
            half = d // 2
            inv_freq = ROPE_THETA ** (-jnp.arange(half, dtype=jnp.float32) / half)
            ang = pos[:, None].astype(jnp.float32) * inv_freq[None, :]
            cos = jnp.cos(ang)[None, :, None, :]
            sin = jnp.sin(ang)[None, :, None, :]
            t1, t2 = (t[..., :half], t[..., half:])
            return jnp.concatenate([t1 * cos - t2 * sin, t1 * sin + t2 * cos], axis=-1)
        key = jax.random.key(seed)
        ks = jax.random.split(key, 5)
        w_scale = HIDDEN ** (-0.5)
        return {'x': jax.random.normal(ks[0], (BATCH, SEQ, HIDDEN), jnp.float32), 'wq': jax.random.normal(ks[1], (HIDDEN, N_Q_HEADS * HEAD_DIM), jnp.float32) * w_scale, 'wk': jax.random.normal(ks[2], (HIDDEN, N_KV_HEADS * HEAD_DIM), jnp.float32) * w_scale, 'wv': jax.random.normal(ks[3], (HIDDEN, N_KV_HEADS * HEAD_DIM), jnp.float32) * w_scale, 'wo': jax.random.normal(ks[4], (N_Q_HEADS * HEAD_DIM, HIDDEN), jnp.float32) * w_scale}
    _L0_attn_b_in = _L0_attn_b_setup()

    def _L0_ffn_setup():
        import jax, jax.numpy as jnp
        import numpy as np
        DIM = 512
        INTER = 1792
        SPARSITY = 32
        RANK = 16
        key = jax.random.key(seed)
        ks = jax.random.split(key, 5)
        B, T = (32, 1)
        x = jax.random.normal(ks[0], (B, T, DIM), dtype=jnp.float32)
        c1_w = jax.random.normal(ks[1], (RANK, DIM), dtype=jnp.float32) * (1.0 / np.sqrt(DIM))
        c2_w = jax.random.normal(ks[2], (INTER, RANK), dtype=jnp.float32) * (1.0 / np.sqrt(RANK))
        w1 = jax.random.normal(ks[3], (INTER, DIM), dtype=jnp.float32) * (1.0 / np.sqrt(DIM))
        w2t = jax.random.normal(ks[4], (INTER, DIM), dtype=jnp.float32) * (1.0 / np.sqrt(INTER))
        return {'x': x, 'c1_w': c1_w, 'c2_w': c2_w, 'w1': w1, 'w2t': w2t}
    _L0_ffn_in = _L0_ffn_setup()
    _d = {'L0_attn_a_hidden_states': _L0_attn_a_in['hidden_states'], 'L0_attn_a_Wqkv': _L0_attn_a_in['Wqkv'], 'L0_attn_a_Wo': _L0_attn_a_in['Wo'], 'L0_attn_b_wq': _L0_attn_b_in['wq'], 'L0_attn_b_wk': _L0_attn_b_in['wk'], 'L0_attn_b_wv': _L0_attn_b_in['wv'], 'L0_attn_b_wo': _L0_attn_b_in['wo'], 'L0_ffn_c1_w': _L0_ffn_in['c1_w'], 'L0_ffn_c2_w': _L0_ffn_in['c2_w'], 'L0_ffn_w1': _L0_ffn_in['w1'], 'L0_ffn_w2t': _L0_ffn_in['w2t']}
    _x0 = _d['L0_attn_a_hidden_states']
    _d['L0_attn_a_hidden_states'] = jax.random.normal(jax.random.fold_in(jax.random.key(seed), 1), (4, 512, 512), dtype=_x0.dtype)
    del _x0
    return _d

def reference(L0_attn_a_hidden_states, L0_attn_a_Wqkv, L0_attn_a_Wo, L0_attn_b_wq, L0_attn_b_wk, L0_attn_b_wv, L0_attn_b_wo, L0_ffn_c1_w, L0_ffn_c2_w, L0_ffn_w1, L0_ffn_w2t):

    def _L0_attn_a_ref(hidden_states, Wqkv, Wo):
        import math
        import jax, jax.numpy as jnp
        import numpy as np
        NUM_HEADS = 32
        HIDDEN = 512
        HEAD_DIM = HIDDEN // NUM_HEADS
        NEG_INF = -1e+30

        def _alibi_slopes(n: int) -> jnp.ndarray:
            cp2 = 2 ** math.floor(math.log2(n))
            base = 2.0 ** (-2.0 ** (-(math.log2(cp2) - 3)))
            slopes = base ** np.arange(1, cp2 + 1, dtype=np.float64)
            if cp2 != n:
                extra_base = 2.0 ** (-2.0 ** (-(math.log2(2 * cp2) - 3)))
                rem = min(cp2, n - cp2)
                extra = extra_base ** np.arange(1, 1 + 2 * rem, 2, dtype=np.float64)
                slopes = np.concatenate([slopes, extra])
            return jnp.asarray(slopes, dtype=jnp.float32)
        B, S, H = hidden_states.shape
        nH, d = (NUM_HEADS, HEAD_DIM)
        scale = d ** (-0.5)
        qkv = hidden_states @ Wqkv
        q = qkv[..., :nH * d].reshape(B, S, nH, d)
        k = qkv[..., nH * d:nH * d + d]
        v = qkv[..., nH * d + d:]
        scores = jnp.einsum('bqhd,bkd->bhqk', q, k) * scale
        pos_q = jnp.arange(S)[:, None]
        pos_k = jnp.arange(S)[None, :]
        slopes = _alibi_slopes(nH)
        alibi = slopes[:, None, None] * (pos_k - pos_q).astype(jnp.float32)
        causal = pos_k <= pos_q
        scores = jnp.where(causal[None, None], scores + alibi[None], NEG_INF)
        probs = jax.nn.softmax(scores, axis=-1)
        attn = jnp.einsum('bhqk,bkd->bqhd', probs, v).reshape(B, S, H)
        return attn @ Wo

    def _L0_attn_b_ref(x, wq, wk, wv, wo):
        import jax, jax.numpy as jnp
        import numpy as np
        HIDDEN = 512
        HEAD_DIM = 128
        N_Q_HEADS = 32
        N_KV_HEADS = 8
        SLIDING_WINDOW = 128
        ROPE_THETA = 10000.0
        BATCH, SEQ = (1, 256)

        def _rope(t, pos):
            d = t.shape[-1]
            half = d // 2
            inv_freq = ROPE_THETA ** (-jnp.arange(half, dtype=jnp.float32) / half)
            ang = pos[:, None].astype(jnp.float32) * inv_freq[None, :]
            cos = jnp.cos(ang)[None, :, None, :]
            sin = jnp.sin(ang)[None, :, None, :]
            t1, t2 = (t[..., :half], t[..., half:])
            return jnp.concatenate([t1 * cos - t2 * sin, t1 * sin + t2 * cos], axis=-1)
        B, S, _ = x.shape
        G = N_Q_HEADS // N_KV_HEADS
        sm_scale = HEAD_DIM ** (-0.5)
        q = (x @ wq).reshape(B, S, N_Q_HEADS, HEAD_DIM)
        k = (x @ wk).reshape(B, S, N_KV_HEADS, HEAD_DIM)
        v = (x @ wv).reshape(B, S, N_KV_HEADS, HEAD_DIM)
        pos = jnp.arange(S)
        q = _rope(q, pos)
        k = _rope(k, pos)
        qg = q.reshape(B, S, N_KV_HEADS, G, HEAD_DIM)
        scores = jnp.einsum('bqhgd,bshd->bhgqs', qg, k) * sm_scale
        i = pos[:, None]
        j = pos[None, :]
        allowed = (j <= i) & (j > i - SLIDING_WINDOW)
        neg = jnp.finfo(scores.dtype).min
        scores = jnp.where(allowed[None, None, None], scores, neg)
        attn = jax.nn.softmax(scores, axis=-1)
        out = jnp.einsum('bhgqs,bshd->bqhgd', attn, v).reshape(B, S, N_Q_HEADS * HEAD_DIM)
        return out @ wo

    def _L0_ffn_ref(x, c1_w, c2_w, w1, w2t):
        import jax, jax.numpy as jnp
        import numpy as np
        DIM = 512
        INTER = 1792
        SPARSITY = 32
        RANK = 16
        B, T, M = x.shape
        xf = x.reshape(B * T, M)
        inter = xf @ c1_w.T @ c2_w.T
        n_blocks = INTER // SPARSITY
        blk = inter.reshape(B * T, n_blocks, SPARSITY)
        idx = jnp.argmax(blk, axis=-1) + jnp.arange(0, INTER, SPARSITY)
        w1_g = w1[idx]
        w2_g = w2t[idx]
        h = jax.nn.relu(jnp.einsum('bkm,bm->bk', w1_g, xf))
        out = jnp.einsum('bk,bkm->bm', h, w2_g)
        return out.reshape(B, T, M)
    x = L0_attn_a_hidden_states
    x = x + _L0_attn_a_ref(_layernorm(x, axis=-1), L0_attn_a_Wqkv, L0_attn_a_Wo)
    x = x + _L0_ffn_ref(_layernorm(x, axis=-1), L0_ffn_c1_w, L0_ffn_c2_w, L0_ffn_w1, L0_ffn_w2t)
    x = x + _L0_attn_b_ref(_layernorm(x, axis=-1), L0_attn_b_wq, L0_attn_b_wk, L0_attn_b_wv, L0_attn_b_wo)
    x = x + _L0_ffn_ref(_layernorm(x, axis=-1), L0_ffn_c1_w, L0_ffn_c2_w, L0_ffn_w1, L0_ffn_w2t)
    return x

_drawn_inputs = setup_inputs


def setup_inputs(seed=0):
    import zlib

    import numpy as np

    out = dict(_drawn_inputs(seed))
    spreads = {}
    factors = {}
    for name, (base, spread) in spreads.items():
        noise = np.random.default_rng([zlib.crc32(name.encode()), seed]).standard_normal(out[name].shape)
        drawn = base * np.exp(spread * noise) if base else spread * noise
        out[name] = jnp.asarray(drawn.astype(out[name].dtype))
    for name, factor in factors.items():
        out[name] = (out[name] * factor).astype(out[name].dtype)
    return out
```

```python
from contextlib import ExitStack

import concourse.bass as bass
import numpy as np
from concourse import mybir

F32 = mybir.dt.float32
F32R = mybir.dt.float32r
BF16 = mybir.dt.bfloat16
ALU = mybir.AluOpType
ACT = mybir.ActivationFunctionType
AX = mybir.AxisListType

P = 128
NB, S, D = 4, 512, 512
DT = D // P
ST = S // P
TOK = NB * S
LN_EPS = 1e-5

INTER, SPARSE, RANK = 1792, 32, 16
IT = INTER // P
CH = 256
NCH = INTER // CH
CBLK = 2 * CH // SPARSE
CROWS = 96


def f32(ap):
    return ap.bitcast(F32)


def sb_in(nc, stack):
    return lambda name, shape, dt=F32: stack.enter_context(nc.sbuf_tensor(name, shape, dt))


def ps_in(nc, stack):
    return lambda name, shape, dt=F32: stack.enter_context(nc.psum_tensor(name, shape, dt))


def sem_in(nc, tag=""):
    return lambda name: nc.alloc_semaphore(name=tag + name)


def load_x(nc, x, xt, ident):
    with ExitStack() as st:
        sb, ps, sem = sb_in(nc, st), ps_in(nc, st), sem_in(nc)
        rows = sb("x_rows", [P, NB, ST, D])
        pt = [ps(f"x_turned{i}", [P, DT, P]) for i in range(8)]
        landed = [sem(f"x_landed{b}") for b in range(NB)]
        turned = sem("x_tile_turned")
        kept = [sem("x_kept_even"), sem("x_kept_odd")]
        xv = x.rearrange("b (t p) d -> b p t d", p=P)
        block = st.enter_context(nc.Block())

        @block.sync
        def _(e):
            for b in range(NB):
                e.dma_start(rows[:, b], xv[b]).then_inc(landed[b], 16)

        @block.tensor
        def _(e):
            for n in range(NB * ST):
                b, t = divmod(n, ST)
                if t == 0:
                    e.wait_ge(landed[b], 16)
                if n >= 8:
                    e.wait_ge(kept[n % 2], n // 2 - 3)
                for d in range(DT):
                    mm = e.transpose(pt[n % 8][:, d], rows[:, b, t, d * P:(d + 1) * P], ident[:, :])
                mm.then_inc(turned, 1)

        def keep(e, n, op):
            e.wait_ge(turned, n + 1)
            op(xt[:, :, n * P:(n + 1) * P], pt[n % 8][:, :, :]).then_inc(kept[n % 2], 1)

        @block.vector
        def _(e):
            for n in range(0, NB * ST, 2):
                keep(e, n, e.tensor_copy)

        @block.scalar
        def _(e):
            for n in range(1, NB * ST, 2):
                keep(e, n, e.copy)


def store_x(nc, out, xt, ident):
    with ExitStack() as st:
        sb, ps, sem = sb_in(nc, st), ps_in(nc, st), sem_in(nc)
        rows = sb("out_rows", [P, NB * ST, D])
        pt = [ps(f"out_turned{i}", [P, D]) for i in range(8)]
        turned = sem("out_tile_turned")
        kept = [sem("out_kept_even"), sem("out_kept_odd")]
        stored = sem("out_stored")
        ov = out.rearrange("b (t p) d -> p (b t) d", p=P)
        block = st.enter_context(nc.Block())

        @block.tensor
        def _(e):
            for n in range(NB * ST):
                if n >= 8:
                    e.wait_ge(kept[n % 2], n // 2 - 3)
                for d in range(DT):
                    mm = e.transpose(pt[n % 8][:, d * P:(d + 1) * P], xt[:, d, n * P:(n + 1) * P], ident[:, :])
                mm.then_inc(turned, 1)

        def keep(e, n, op):
            e.wait_ge(turned, n + 1)
            op(rows[:, n], pt[n % 8][:, :]).then_inc(kept[n % 2], 1)

        @block.vector
        def _(e):
            for n in range(0, NB * ST, 2):
                keep(e, n, e.tensor_copy)

        @block.scalar
        def _(e):
            for n in range(1, NB * ST, 2):
                keep(e, n, e.copy)

        @block.sync
        def _(e):
            for n in range(0, NB * ST, 2):
                e.wait_ge(kept[0], n // 2 + 1)
                e.wait_ge(kept[1], n // 2 + 1)
                e.dma_start(ov[:, n:n + 2], rows[:, n:n + 2]).then_inc(stored, 16)
            e.wait_ge(stored, 16 * NB * ST // 2)


class Chain:

    def __init__(self, e, sem, before=0):
        self.e, self.sem, self.before, self.n = e, sem, before, 0

    def __call__(self, instruction):
        self.n += 1
        instruction.then_inc(self.sem, 1)
        self.e.wait_ge(self.sem, self.before + self.n)


def ffn(nc, tag, drams, xt, consts):
    c1_w, c2_w, w1, w2t = drams
    ident, identb, ones, rev = consts
    with ExitStack() as st:
        sb, ps, sem = sb_in(nc, st), ps_in(nc, st), sem_in(nc)
        with ExitStack() as early:
            w1_raw, w2_raw = sb_in(nc, early)(f"{tag}w1_raw", [P, DT, INTER]), sb_in(nc, early)(f"{tag}w2_raw", [P, IT, D])
        w1l, w2l = sb(f"{tag}w1_low", [P, DT, INTER], F32R), sb(f"{tag}w2_low", [P, IT, D], F32R)
        w1h, w2h = sb(f"{tag}w1_high", [P, DT, INTER], F32R), sb(f"{tag}w2_high", [P, IT, D], F32R)
        c1h, c1l = (sb(f"{tag}c1_{x}", [P, DT, CROWS], F32R) for x in ("high", "low"))
        c2s = sb(f"{tag}c2_stacked", [CROWS, INTER], F32R)
        zh, zl = (sb(f"{tag}z_{x}", [P, DT, S], F32R) for x in ("high", "low"))
        zf = sb(f"{tag}z", [P, DT, S])
        tmp = [sb(f"{tag}ln_tmp{i}", [P, S]) for i in range(3)]
        ts = sb(f"{tag}t_stacked", [CROWS, S], F32R)
        eq = sb(f"{tag}is_max", [P, CBLK, SPARSE], BF16)
        mx = sb(f"{tag}block_max", [P, CBLK])
        first = sb(f"{tag}first_max", [P, CBLK], BF16)
        mask = sb(f"{tag}mask", [P, 2, ST, CH], BF16)
        mts = sb(f"{tag}mask_turned", [P, 2, 2, S], BF16)
        hm = sb(f"{tag}hidden", [P, S])
        with ExitStack() as early:
            c2_raw = [sb_in(nc, early)(f"{tag}c2_raw{i}", [P, 2 * S]) for i in range(2)]
        hh, hl = (sb(f"{tag}hidden_{x}", [P, 2, S], F32R) for x in ("high", "low"))
        acc = ps(f"{tag}acc", [P, DT, S])
        hp = [ps(f"{tag}hidden_sum{i}", [P, S]) for i in range(2)]
        aux = [ps(f"{tag}aux{i}", [P, S]) for i in range(2)]
        HALF_IT = IT // 2
        c1r = hm[0:CROWS, :]
        c2r = [x[:, 0:HALF_IT * CROWS].rearrange("p (t r) -> p t r", t=HALF_IT) for x in c2_raw]
        banks = [acc[:, d] for d in range(DT)] + [x[:, :] for x in hp]
        groups = [(g, min(4, IT - g)) for g in range(0, IT, 4)]
        jobs = [("c1", 0, 0, DT)] + [("c2", 0, g, n) for g, n in groups] + \
               [("w1", d, g, n) for g, n in groups for d in range(DT)]
        ROUTER = range(1 + len(groups))
        W1 = [range(ROUTER.stop + DT * i, ROUTER.stop + DT * (i + 1)) for i in range(len(groups))]

        def places(j):
            (what, d, g, n), b = jobs[j], banks[j % len(banks)]
            cols = slice(g * P, (g + n) * P)
            if what == "c1":
                src = b[:, 0:DT * CROWS].rearrange("p (k r) -> p k r", k=DT)
                return src, c1h[:, :, :], src, c1l[:, :, :], c1h[:, :, :]
            if what == "c2":
                rest = c2s[64:CROWS, cols]
                return b[0:CROWS, 0:n * P], c2s[:, cols], b[64:CROWS, 0:n * P], rest, rest
            return b[:, 0:n * P], w1h[:, d, cols], b[:, 0:n * P], w1l[:, d, cols], w1h[:, d, cols]

        cleared, c_in = sem(f"{tag}c_rows_cleared"), sem(f"{tag}c_landed")
        w1_in = [sem(f"{tag}w1_landed{i}") for i in range(len(groups))]
        w2_in = [sem(f"{tag}w2_landed{i}") for i in range(NCH)]
        turned, w_high, w_low = (sem(f"{tag}weights_{x}") for x in ("turned", "high_ready", "low_ready"))
        w2_high, w2_low = sem(f"{tag}w2_high_ready"), sem(f"{tag}w2_low_ready")
        aux_full = [sem(f"{tag}aux_full{i}") for i in range(2)]
        aux_free = [sem(f"{tag}aux_free{i}") for i in range(2)]
        t_high = sem(f"{tag}t_high_written")
        dve_step, pool_step, act_step = sem(f"{tag}dve_step"), sem(f"{tag}pool_step"), sem(f"{tag}act_step")
        mask_ready = sem(f"{tag}mask_half_ready")
        h_full, h_masked = sem(f"{tag}hidden_sum_full"), sem(f"{tag}hidden_masked")
        hh_ready, hl_ready = sem(f"{tag}hidden_high_ready"), sem(f"{tag}hidden_low_ready")
        h_used, acc_added = sem(f"{tag}hidden_used"), sem(f"{tag}acc_added")
        x_summed, sq_ready, sq_added = sem(f"{tag}x_summed"), sem(f"{tag}square_ready"), sem(f"{tag}square_added")
        y0_ready, z_ready = sem(f"{tag}rsqrt_seed_ready"), sem(f"{tag}z_ready")
        zh_ready, zl_ready = sem(f"{tag}z_high_ready"), sem(f"{tag}z_low_ready")

        order = [("I", 0), ("I", 1)]
        for c in range(NCH):
            order += [("M", c)] + ([("I", 2 * c + 2), ("I", 2 * c + 3)] if c + 1 < NCH else [])
            order += [("mean", 0)] * (c == 1) + [("var", 0)] * (c == 4)
        order += [("T", 0)]
        BEFORE = ["mean", "var", "T"]
        HALF = len(order) // 2
        assert len(order) % 2 == 0

        def use(it, what, i=0):
            n = BEFORE.index(what) if it is None else order.index((what, i)) + len(BEFORE)
            return n % 2, (0 if it is None else it * HALF) + n // 2 + 1

        def aux_write(e, it, what, i=0):
            k, n = use(it, what, i)
            if not isinstance(n, int) or n > 1:
                e.wait_ge(aux_free[k], n - 1)
            return aux[k], aux_full[k]

        def aux_read(e, it, what, i=0):
            k, n = use(it, what, i)
            e.wait_ge(aux_full[k], n)
            return aux[k], aux_free[k]

        def aux_done(e, it, what, i=0):
            k, n = use(it, what, i)
            e.wait_ge(aux_free[k], n)

        def first_batch(it):
            return isinstance(it, int) and it == 0

        def of_ln(it, per):
            return 0 if it is None else (it + 1) * per

        def batch_after(it):
            return 0 if it is None else (it + 1) % NB

        def loop(e, body):
            body(0, True)
            with e.Fori(1, NB) as it:
                body(it, False)

        block = st.enter_context(nc.Block())

        @block.sync
        def _(e):
            e.wait_ge(cleared, 3)
            for r in range(CROWS // 32):
                rows = slice(32 * r, 32 * r + RANK)
                e.dma_start(c1r[rows, :], c1_w).then_inc(c_in, 16)
                for half in range(2):
                    e.dma_start(c2r[half][:, :, rows], c2_w.rearrange("(h t p) r -> h p t r", h=2, p=P)[half])\
                        .then_inc(c_in, 16)
            w1v = w1.rearrange("(t p) (d k) -> t p d k", p=P, k=P)
            for i, (g, n) in enumerate(groups):
                for t in range(g, g + n):
                    e.dma_start(w1_raw[:, :, t * P:(t + 1) * P], w1v[t]).then_inc(w1_in[i], 16)
            w2v = w2t.rearrange("(t p) d -> p t d", p=P)
            for i in range(NCH):
                e.dma_start(w2_raw[:, 2 * i:2 * i + 2], w2v[:, 2 * i:2 * i + 2]).then_inc(w2_in[i], 16)

        @block.tensor
        def _(e):
            def turn_weights(which):
                for j in which:
                    what, d, g, n = jobs[j]
                    if j == 0:
                        e.wait_ge(c_in, 16 * CROWS // 32 * 3)
                    if what == "w1" and d == 0:
                        e.wait_ge(w1_in[g // 4], 16 * n)
                    if j >= len(banks):
                        e.wait_ge(w_low, j - len(banks) + 1)
                    b = banks[j % len(banks)]
                    for k in range(n):
                        t = g + k
                        if what == "c1":
                            mm = e.transpose(b[:, k * CROWS:(k + 1) * CROWS], c1r[:, k * P:(k + 1) * P],
                                             ident[0:CROWS, 0:CROWS])
                        elif what == "c2":
                            mm = e.transpose(b[0:CROWS, k * P:(k + 1) * P], c2r[t // HALF_IT][:, t % HALF_IT, :],
                                             ident[:, :])
                        else:
                            mm = e.transpose(b[:, k * P:(k + 1) * P], w1_raw[:, d, t * P:(t + 1) * P], ident[:, :])
                    mm.then_inc(turned, 1)

            def mean(it):
                bank, full = aux_write(e, it, "mean")
                e.wait_ge(x_summed, of_ln(it, 1) + 1)
                e.matmul(bank[:, :], ones[:, :], tmp[2][:, :], start=True, stop=True).then_inc(full, 1)

            def var(it):
                bank, full = aux_write(e, it, "var")
                e.wait_ge(sq_added, of_ln(it, 3) + 3)
                e.matmul(bank[:, :], ones[:, :], tmp[2][:, :], start=True, stop=True).then_inc(full, 1)

            def router_first(it):
                e.wait_ge(zh_ready, of_ln(it, DT) + DT)
                e.wait_ge(zl_ready, of_ln(it, DT) + DT)
                bank, full = aux_write(e, it, "T")
                for n, (w, z) in enumerate([(c1h, zh), (c1h, zl), (c1l, zh)]):
                    for d in range(DT):
                        mm = e.matmul(bank[0:CROWS, :], w[:, d, :], z[:, d, :],
                                      start=n == 0 and d == 0, stop=n == 2 and d == DT - 1)
                mm.then_inc(full, 1)

            def router_scores(it, c, halves=(0, 1)):
                if c == 0:
                    aux_done(e, it - 1 if not first_batch(it) else None, "T")
                for half in halves:
                    bank, full = aux_write(e, it, "I", 2 * c + half)
                    for k in range(2):
                        t = 2 * half + k
                        mm = e.matmul(bank[:, k * CH:(k + 1) * CH], ts[:, t * P:(t + 1) * P],
                                      c2s[:, c * CH:(c + 1) * CH], start=True, stop=True)
                    mm.then_inc(full, 1)

            def turn_masks(it, c):
                e.wait_ge(mask_ready, it * 2 * NCH + 2 * c + 2)
                bank, full = aux_write(e, it, "M", c)
                turned = bank[:, :].bitcast(BF16).rearrange("p (j t) -> p j t", j=2)
                for j in range(2):
                    for t in range(ST):
                        mm = e.transpose(turned[:, j, t * P:(t + 1) * P],
                                         mask[:, c % 2, t, j * P:(j + 1) * P], identb[:, :])
                mm.then_inc(full, 1)

            def up(it, j):
                e.wait_ge(h_masked, it * IT + j + 1)
                for d in range(DT):
                    for n, (w, z) in enumerate([(w1h, zh), (w1h, zl), (w1l, zh)]):
                        mm = e.matmul(hp[j % 2][:, :], w[:, d, j * P:(j + 1) * P], z[:, d, :],
                                      start=d == 0 and n == 0, stop=d == DT - 1 and n == 2)
                mm.then_inc(h_full, 1)

            def down(it, j):
                if j == 0 and not first_batch(it):
                    e.wait_ge(acc_added, it)
                e.wait_ge(hh_ready, it * IT + j + 1)
                e.wait_ge(hl_ready, it * IT + j + 1)
                if first_batch(it):
                    e.wait_ge(w2_low, j // 2 + 1)
                for d in range(DT):
                    for n, (w, h) in enumerate([(w2h, hh), (w2h, hl), (w2l, hh)]):
                        mm = e.matmul(acc[:, d, :], w[:, j, d * P:(d + 1) * P], h[:, j % 2, :],
                                      start=j == 0 and n == 0, stop=j == IT - 1 and n == 2)
                mm.then_inc(h_used, 1)

            def body(it, first):
                router_scores(it, 0)
                for c in range(NCH):
                    up(it, 2 * c)
                    if c == 0:
                        up(it, 1)
                    else:
                        if c == 1:
                            router_scores(it, 1, [1])
                        down(it, 2 * c - 2)
                    turn_masks(it, c)
                    if c + 1 < NCH:
                        router_scores(it, c + 1, [0])
                    if c:
                        up(it, 2 * c + 1)
                        if c + 1 < NCH:
                            router_scores(it, c + 1, [1])
                        down(it, 2 * c - 1)
                    if c == 1:
                        mean(it)
                    if c == 4:
                        var(it)
                down(it, IT - 2)
                router_first(it)
                down(it, IT - 1)

            e.sem_inc(h_used, 2)
            mean(None)
            turn_weights(ROUTER)
            var(None)
            for i in range(3):
                turn_weights(W1[i])
            router_first(None)
            turn_weights(W1[3])
            e.wait_ge(w_low, len(jobs))
            loop(e, body)

        @block.vector
        def _(e):
            def centre(it):
                bank, free = aux_read(e, it, "mean")
                e.tensor_tensor(zf[:, :, :], xt[:, :, bass.ts(batch_after(it), S)],
                                bank[:, :].unsqueeze(1).broadcast_to([P, DT, S]), ALU.subtract).then_inc(free, 1)

            def variance(it):
                bank, free = aux_read(e, it, "var")
                e.tensor_scalar(tmp[0][:, :], bank[:, :], LN_EPS, None, ALU.add).then_inc(free, 1)

            def normalise(it, chain):
                e.wait_ge(y0_ready, of_ln(it, 1) + 1)
                chain(e.scalar_tensor_tensor(tmp[2][:, :], tmp[0][:, :], -0.5, tmp[1][:, :], ALU.mult, ALU.mult))
                chain(e.tensor_tensor(tmp[2][:, :], tmp[2][:, :], tmp[1][:, :], ALU.mult))
                chain(e.scalar_tensor_tensor(tmp[0][:, :], tmp[2][:, :], 1.5, tmp[1][:, :], ALU.add, ALU.mult))
                e.tensor_tensor(zf[:, :, :], zf[:, :, :], tmp[0][:, :].unsqueeze(1).broadcast_to([P, DT, S]),
                                ALU.mult).then_inc(z_ready, 1)

            def low_z(it):
                for d in range(DT):
                    e.wait_ge(zh_ready, of_ln(it, DT) + d + 1)
                    e.tensor_tensor(zl[:, d], zf[:, d], f32(zh[:, d]), ALU.subtract).then_inc(zl_ready, 1)

            def stack_t(it):
                e.wait_ge(t_high, of_ln(it, 1) + 1)
                bank, free = aux_read(e, it, "T")
                e.tensor_tensor(ts[32:64, :], bank[32:64, :], f32(ts[32:64, :]), ALU.subtract).then_inc(free, 1)

            def find_max(it, c, half, chain):
                bank, free = aux_read(e, it, "I", 2 * c + half)
                scores = bank[:, :].rearrange("p (g k) -> p g k", k=SPARSE)
                chain(e.tensor_reduce(mx[:, :], scores, AX.X, ALU.max))
                e.tensor_tensor(eq[:, :, :], scores, mx[:, :].unsqueeze(2).broadcast_to([P, CBLK, SPARSE]),
                                ALU.is_equal).then_inc(free, 1)
                aux_done(e, it, "I", 2 * c + half)
                chain(e.tensor_tensor(eq[:, :, :], eq[:, :, :],
                                      rev[:, :].unsqueeze(1).broadcast_to([P, CBLK, SPARSE]), ALU.mult))
                chain(e.tensor_reduce(first[:, :], eq[:, :, :], AX.X, ALU.max))
                if c >= 2:
                    k, n = use(it, "M", c - 2)
                    e.wait_ge(aux_full[k], n)
                out = mask[:, c % 2, 2 * half:2 * half + 2, :].rearrange("p t (g k) -> p (t g) k", k=SPARSE)
                e.tensor_tensor(out, eq[:, :, :], first[:, :].unsqueeze(2).broadcast_to([P, CBLK, SPARSE]),
                                ALU.is_equal).then_inc(mask_ready, 1)

            def keep_hidden(it, j):
                aux_done(e, it, "M", j // 2)
                e.wait_ge(h_full, it * IT + j + 1)
                e.wait_ge(hl_ready, it * IT + j)
                e.scalar_tensor_tensor(hm[:, :], hp[j % 2][:, :], 0.0, mts[:, j // 2 % 2, j % 2, :],
                                       ALU.max, ALU.mult).then_inc(h_masked, 1)

            def add_out(it):
                e.wait_ge(h_used, it * IT + IT + 2)
                here = xt[:, :, bass.ts(it, S)]
                e.tensor_tensor(here, here, acc[:, :, :], ALU.add).then_inc(acc_added, 1)

            def body(it, first):
                chain = Chain(e, dve_step, it * (3 * 2 * NCH + 3) + 3)
                find_max(it, 0, 0, chain)
                find_max(it, 0, 1, chain)
                if not first:
                    add_out(it - 1)
                for c in range(NCH):
                    if c == 2:
                        centre(it)
                    if c == 5:
                        variance(it)
                    for half in range(2):
                        keep_hidden(it, 2 * c + half)
                        if c + 1 < NCH:
                            find_max(it, c + 1, half, chain)
                    if c == 5:
                        normalise(it, chain)
                low_z(it)
                stack_t(it)

            def low_weights(which):
                for j in which:
                    _, _, src, lo, hi = places(j)
                    e.wait_ge(w_high, j + 1)
                    e.tensor_tensor(lo, src, f32(hi), ALU.subtract).then_inc(w_low, 1)

            e.sem_inc(h_masked, 2)
            centre(None)
            low_weights(ROUTER)
            variance(None)
            low_weights(W1[0])
            normalise(None, Chain(e, dve_step))
            low_weights(W1[1])
            low_z(None)
            low_weights(W1[2])
            low_weights(W1[3])
            stack_t(None)
            loop(e, body)
            add_out(NB - 1)

        @block.scalar
        def _(e):
            def square(it, d):
                if d == 0:
                    aux_done(e, it, "mean")
                if d == 2:
                    e.wait_ge(sq_added, of_ln(it, 3) + 1)
                if d == 3:
                    e.wait_ge(sq_added, of_ln(it, 3) + 1)
                e.activation(tmp[d % 2][:, :], zf[:, d], ACT.Square).then_inc(sq_ready, 1)

            def seed(it):
                k, n = use(it, "var")
                aux_done(e, it, "var")
                e.activation(tmp[1][:, :], tmp[0][:, :], ACT.Ln).then_inc(act_step, 1)
                e.wait_ge(act_step, of_ln(it, 1) + 1)
                e.activation(tmp[1][:, :], tmp[1][:, :], ACT.Exp, scale=-0.5).then_inc(y0_ready, 1)

            def high_z(it):
                e.wait_ge(z_ready, of_ln(it, 1) + 1)
                if it is not None:
                    e.wait_ge(h_full, it * IT + IT)
                for d in range(DT):
                    e.copy(zh[:, d], zf[:, d]).then_inc(zh_ready, 1)

            def high_w2(i):
                e.wait_ge(w2_in[i], 16)
                e.copy(w2h[:, 2 * i:2 * i + 2], w2_raw[:, 2 * i:2 * i + 2]).then_inc(w2_high, 1)

            def high_t(it):
                bank, _ = aux_read(e, it, "T")
                e.copy(ts[:, :], bank[0:CROWS, :]).then_inc(t_high, 1)

            def body(it, first):
                for c in range(NCH):
                    e.wait_ge(h_masked, it * IT + max(2 * c, 0))
                    bank, free = aux_read(e, it, "M", c)
                    e.copy(mts[:, c % 2], bank[:, :].bitcast(BF16).rearrange("p (j t) -> p j t", j=2))\
                        .then_inc(free, 1)
                    for j in (2 * c, 2 * c + 1):
                        e.wait_ge(h_masked, it * IT + j + 3)
                        e.wait_ge(h_used, it * IT + j + 1)
                        e.copy(hh[:, j % 2], hm[:, :]).then_inc(hh_ready, 1)
                    if first and c + 1 < NCH:
                        high_w2(c + 1)
                    if c == 2:
                        square(it, 0)
                        square(it, 1)
                    if c == 3:
                        square(it, 2)
                        square(it, 3)
                    if c == 5:
                        seed(it)
                high_z(it)
                high_t(it)

            def high_weights(which):
                for j in which:
                    src, hi, _, _, _ = places(j)
                    e.wait_ge(turned, j + 1)
                    e.copy(hi, src).then_inc(w_high, 1)

            for d in range(DT):
                square(None, d)
            high_weights(ROUTER)
            seed(None)
            high_weights(W1[0])
            high_weights(W1[1])
            high_z(None)
            high_weights(W1[2])
            high_weights(W1[3])
            high_t(None)
            high_w2(0)
            loop(e, body)

        @block.gpsimd
        def _(e):
            def sum_x(it, chain):
                if it is not None:
                    e.wait_ge(z_ready, it + 1)
                    if not first_batch(it):
                        e.wait_ge(acc_added, it - 1)
                here = xt[:, :, bass.ts(batch_after(it), S)]
                chain(e.tensor_tensor(tmp[2][:, :], here[:, 0], here[:, 1], ALU.add))
                chain(e.tensor_tensor(tmp[2][:, :], tmp[2][:, :], here[:, 2], ALU.add))
                e.tensor_tensor(tmp[2][:, :], tmp[2][:, :], here[:, 3], ALU.add).then_inc(x_summed, 1)

            def sum_squares(it, n):
                e.wait_ge(sq_ready, of_ln(it, DT) + n + 2)
                if n:
                    e.wait_ge(sq_added, of_ln(it, 3) + n)
                e.tensor_tensor(tmp[2][:, :], tmp[0][:, :] if n == 0 else tmp[2][:, :], tmp[(n + 1) % 2][:, :],
                                ALU.add).then_inc(sq_added, 1)

            def low_hidden(it, j):
                e.wait_ge(hh_ready, it * IT + j + 1)
                e.tensor_tensor(hl[:, j % 2], hm[:, :], f32(hh[:, j % 2]), ALU.subtract).then_inc(hl_ready, 1)

            def body(it, first):
                sum_x(it, Chain(e, pool_step, it * 2 + 2))
                for c in range(NCH):
                    low_hidden(it, 2 * c)
                    low_hidden(it, 2 * c + 1)
                    if first and c + 1 < NCH:
                        low_w2(c + 1)
                    if c == 2:
                        sum_squares(it, 0)
                    if c == 3:
                        sum_squares(it, 1)
                        sum_squares(it, 2)

            def low_w2(i):
                e.wait_ge(w2_high, i + 1)
                e.tensor_tensor(w2l[:, 2 * i:2 * i + 2], w2_raw[:, 2 * i:2 * i + 2], f32(w2h[:, 2 * i:2 * i + 2]), ALU.subtract).then_inc(w2_low, 1)

            e.memset(c1r, 0.0).then_inc(cleared, 1)
            for x in c2r:
                e.memset(x, 0.0).then_inc(cleared, 1)
            sum_x(None, Chain(e, pool_step))
            for n in range(3):
                sum_squares(None, n)
            low_w2(0)
            loop(e, body)


AH, AD = 32, 16
PAIRS = AH // 2
HG = AH // 4
KV = 48
VROWS = 80
R_QHI, R_QLO, R_BIAS, R_MAX, R_QHI2, R_ZERO = 0, 16, 32, 38, 40, 56
LAG = 3


def unit_base(qt):
    return HG * qt * (qt + 1) // 2


def load_attention_a(nc, drams, raw, parts, kan, vn):
    wqkv, wo, q_rows, k_rows, q_dram, k_dram = drams
    w_raw, wo_raw = raw
    wh, wl, wkvh, wkvl, woh, wol = parts
    with ExitStack() as st:
        sem = sem_in(nc)
        w_in, wo_in, q_in, k_in, k_back = (sem(f"a_load_{n}") for n in ("w", "wo", "q_rows", "k_rows", "k_back"))
        cleared, high = sem("a_load_cleared"), sem("a_load_high")
        NQ = AH * AD
        splits = [(w_raw[:, :, 0:NQ], wh[:, :, :], wl[:, :, :]),
                  (w_raw[:, :, NQ + AD:], wkvh[:, :, 0:AD], wkvl[:, :, 0:AD]),
                  (w_raw[:, :, NQ:NQ + AD], wkvh[:, :, 32:KV], wkvl[:, :, 32:KV]),
                  (wo_raw[:, :, :], woh[:, :, :], wol[:, :, :])]
        block = st.enter_context(nc.Block())

        @block.sync
        def _(e):
            e.dma_start(w_raw[:, :, :], wqkv.rearrange("(t p) n -> p t n", p=P)).then_inc(w_in, 16)
            e.dma_start(wo_raw[:, :, :], wo.rearrange("(t p) n -> p t n", p=P)).then_inc(wo_in, 16)
            e.dma_start(k_dram, k_rows).then_inc(k_in, 16)
            e.dma_start(q_dram[:, R_BIAS:R_QHI2], q_rows[:, 0:8]).then_inc(q_in, 16)
            e.dma_start(q_dram[:, R_ZERO:64], q_rows[:, 8:16]).then_inc(q_in, 16)
            e.wait_ge(k_in, 16)
            for half in range(2):
                e.dma_start(f32(kan[half][:, :]), k_dram[half]).then_inc(k_back, 16)
            e.wait_ge(k_back, 32)
            e.wait_ge(q_in, 32)

        @block.gpsimd
        def _(e):
            for x in (wkvh, wkvl):
                e.memset(f32(x[:, :, AD:32]), 0.0)
            e.memset(f32(vn[:, :, 0:64]), 0.0)
            e.memset(f32(vn[:, :, 64:VROWS]), 1.0)

        @block.scalar
        def _(e):
            for i, (raw, hi, _) in enumerate(splits):
                e.wait_ge(w_in if i < 3 else wo_in, 16)
                e.copy(hi, raw).then_inc(high, 1)

        @block.vector
        def _(e):
            for i, (raw, hi, lo) in enumerate(splits):
                e.wait_ge(high, i + 1)
                e.tensor_tensor(lo, raw, f32(hi), ALU.subtract)


def causal_attention(nc, drams, xt, consts, tables):
    ident, identb, ones = consts[:3]
    below, above, q_rows, k_rows = tables
    wqkv, wo = drams
    with ExitStack() as st:
        sb, ps, sem = sb_in(nc, st), ps_in(nc, st), sem_in(nc)
        q_dram = nc.dram_tensor("a_q_stacked", [2, 64, PAIRS, S], F32).ap()
        k_dram = nc.dram_tensor("a_k_stacked", [2, P, S], F32).ap()
        o_dram = nc.dram_tensor("a_out_parts", [NB, 2, AH * AD, S], F32).ap()
        sums_dram, inv_dram = (nc.dram_tensor(f"a_exp_{x}", [NB, AH, S], F32).ap() for x in ("sums", "inverses"))
        wh, wl = (sb(f"a_wq_{x}", [P, DT, AH * AD], F32R) for x in ("high", "low"))
        wkvh, wkvl = (sb(f"a_wkv_{x}", [P, DT, KV], F32R) for x in ("high", "low"))
        woh, wol = (sb(f"a_wo_{x}", [P, DT, D], F32R) for x in ("high", "low"))
        ka = [sb(f"a_keys{i}", [P, S], F32R) for i in range(2)]
        kan = [sb(f"a_keys_next{i}", [P, S], F32R) for i in range(2)]
        vs, vn = sb("a_values", [P, ST, VROWS], F32R), sb("a_values_next", [P, ST, VROWS], F32R)
        with ExitStack() as early:
            sbe = sb_in(nc, early)
            w_raw, wo_raw = sbe("a_wqkv_raw", [P, DT, AH * AD + 2 * AD]), sbe("a_wo_raw", [P, DT, D])
            load_attention_a(nc, (wqkv, wo, q_rows, k_rows, q_dram, k_dram), (w_raw, wo_raw),
                             (wh, wl, wkvh, wkvl, woh, wol), kan, vn)
        qa = sb("a_queries", [P, PAIRS, S], F32R)
        zh, zl = (sb(f"a_z_{x}", [P, DT, S], F32R) for x in ("high", "low"))
        zf = sb("a_z", [P, DT, S])
        tmp = [sb(f"a_ln_tmp{i}", [P, S]) for i in range(3)]
        pf = sb("a_probs", [P, 4, S])
        ph, pl = (sb(f"a_probs_{x}", [P, 4, S], F32R) for x in ("high", "low"))
        ot = sb("a_out", [VROWS, 2, 2, 4, P])
        qsh, qsl = (sb(f"a_q_part_{x}", [P, 2, S], F32R) for x in ("high", "low"))
        kxh, kxl = (sb(f"a_k_part_{x}", [KV, S], F32R) for x in ("high", "low"))
        vt = sb("a_v_by_dim", [AD, S])
        at = zf[:, 0:3]
        sums = sb("a_sums_tile", [P, AH * S // P])
        ath, atl = (sb(f"a_out_{x}", [P, DT, S], F32R) for x in ("high", "low"))
        mx = sb("a_max", [P, 2, AH])
        mh, ml = (sb(f"a_minus_max_{x}", [AH, 2, P], F32R) for x in ("high", "low"))

        mbank = [ps(f"a_max_scores{i}", [P, S]) for i in range(2)]
        sbank = [ps(f"a_scores{i}", [P, S]) for i in range(2)]
        obank = [ps(f"a_o_sum{i}", [P, S]) for i in range(2)]
        misc = [ps(f"a_misc{i}", [P, S]) for i in range(2)]

        names = ("max_full", "max_read", "scores_full", "exp_done", "low_by_vector", "low_by_pool", "pv_done", "o_copied",
                 "misc_used", "m_high", "m_low", "kv_high", "kv_low", "vt_copied", "v_high", "v_low", "q_high", "q_low",
                 "k_landed", "keys_kept", "x_summed", "sq_ready", "sq_added", "centred", "seed", "z_ready", "zh_ready", "zl_ready",
                 "pool_step", "act_step", "dve_step", "at_ready", "at_high", "at_low", "wo_added", "out_landed",
                 "sums_landed", "inv_ready", "inv_stored")
        s = {n: sem(f"a_{n}") for n in names}
        misc_full, misc_free = [sem(f"a_misc_full{i}") for i in range(2)], [sem(f"a_misc_free{i}") for i in range(2)]
        q_stored = [sem(f"a_q_stored{i}") for i in range(2)]
        q_landed = [sem(f"a_q_landed{t}") for t in range(ST)]
        m_landed, o_stored = [sem(f"a_m_landed{i}") for i in range(2)], [sem(f"a_o_stored{i}") for i in range(2)]

        MEAN, VAR, TURNS, KEYS, OUT = 1, 11, (18, 42, 57, 74), 23, 50
        prepare = [("KV", 0), ("Vt", 0)] + [("Q", m) for m in range(DT)]
        small = {MEAN: ("mean", 0), VAR: ("var", 0)}
        small |= {KEYS + 2 * n: x for n, x in enumerate(prepare)}
        small |= {OUT + 14 + 3 * d: ("Wo", d) for d in range(DT)}
        small |= {n: ("mT", qt) for n, qt in zip(TURNS, range(2, ST + 2))}
        searches = [(0, 17, 2), (19, 41, 3), (43, 56, 4), (58, 73, 5)]
        assert len(small) == 8 + 2 * DT
        ahead_only = {("mean", 0), ("var", 0), ("mT", 4), ("mT", 5), *prepare}
        BEFORE = [("mean", 0), ("var", 0), *prepare, ("mT", 4), ("mT", 5)]

        class Batch:

            def __init__(self, it, first=False, last=False):
                self.it, self.first, self.last = it, first, last
                self.small = {k: x for k, x in sorted(small.items())
                              if not (first and x[0] == "Wo") and not (last and x in ahead_only)}
                self.order = list(self.small.values())

            def misc(self, x):
                if self.it is None:
                    n = BEFORE.index(x)
                    return n % 2, n // 2 + 1
                n = self.order.index(x) + (len(BEFORE) if self.first else len(BEFORE) - DT)
                full = len(small) // 2
                return n % 2, (0 if self.first else self.it * full) + n // 2 + 1

            def ahead(self):
                return 0 if self.it is None else self.it + 1

            def steps(self):
                for g in range(UB):
                    yield "scores", g
                    for since, until, tile in searches:
                        if since <= g < until and not (self.last and tile >= ST):
                            for j in range(AH * (g - since) // (until - since), AH * (g + 1 - since) // (until - since)):
                                yield "max", tile, j
                    if g >= LAG:
                        yield "pv", g - LAG
                    if g in self.small:
                        yield ("small", *self.small[g])
                    if g - 1 in self.small:
                        yield ("read", *self.small[g - 1])
                for g in range(UB - LAG, UB):
                    yield "pv", g

        assert len(small) % 2 == 0

        UB = unit_base(ST)

        def place(g):
            qt = max(t for t in range(ST) if unit_base(t) <= g)
            return (qt, *divmod(g - unit_base(qt), qt + 1))

        def group_end(g):
            qt, hg, kt = place(g)
            return qt * HG + hg if kt == qt else None

        def split_by(b, g):
            on_vector = g % 4 == 1
            same = [x for x in range(UB) if (x % 4 == 1) == on_vector]
            return s["low_by_vector" if on_vector else "low_by_pool"], b.it * len(same) + same.index(g) + 1

        def wait(e, sem, value):
            if not (isinstance(value, int) and value <= 0):
                e.wait_ge(sem, value)

        def batches(e, body):
            body(Batch(0, first=True))
            with e.Fori(1, NB - 1) as it:
                body(Batch(it))
            body(Batch(NB - 1, last=True))

        class Finish(Batch):

            def __init__(self):
                self.it = NB

            def misc(self, x):
                n = NB * len(small) + len(BEFORE) - DT + x[1] - len(ahead_only)
                return n % 2, n // 2 + 1

        def step_of(b, qt):
            base = -ST if b.it is None else b.it * ST
            return base + qt, qt % 2

        block = st.enter_context(nc.Block())

        @block.tensor
        def _(e):
            def take(b, x):
                k, n = b.misc(x)
                wait(e, misc_free[k], n - 1)
                return misc[k], misc_full[k]

            def three(out, w, z, first, last):
                for n, (x, y) in enumerate([(w[0], z[0]), (w[0], z[1]), (w[1], z[0])]):
                    mm = e.matmul(out, x, y, start=first and n == 0, stop=last and n == 2)
                return mm

            def small_product(b, kind, i):
                bank, full = take(b, (kind, i))
                if kind in ("mean", "var"):
                    wait(e, s["x_summed"] if kind == "mean" else s["sq_added"],
                         b.ahead() * (1 if kind == "mean" else 3) + (1 if kind == "mean" else 3))
                    mm = e.matmul(bank[:, :], ones[:, :], tmp[2][:, :], start=True, stop=True)
                elif kind in ("KV", "Q"):
                    e.wait_ge(s["zl_ready"], (b.ahead() + 1) * DT)
                    w = (wkvh, wkvl) if kind == "KV" else [x[:, :, i * P:(i + 1) * P] for x in (wh, wl)]
                    out = bank[0:KV, :] if kind == "KV" else bank[:, :]
                    for d in range(DT):
                        mm = three(out, [x[:, d, :] for x in w], [z[:, d, :] for z in (zh, zl)], d == 0, d == DT - 1)
                elif kind == "Vt":
                    e.wait_ge(s["vt_copied"], b.ahead() + 1)
                    for t in range(ST):
                        mm = e.matmul(bank[:, t * AD:(t + 1) * AD], vt[:, t * P:(t + 1) * P], ident[0:AD, 0:AD], start=True,
                                      stop=True)
                elif kind == "mT":
                    step, par = step_of(b, i)
                    e.wait_ge(s["max_read"], (step + 1) * AH)
                    mm = e.transpose(bank[0:AH, 0:P], mx[:, par, :], ident[:, :])
                else:
                    e.wait_ge(s["at_low"], b.it * DT)
                    for m in range(DT):
                        mm = three(bank[:, :], [x[:, m, i * P:(i + 1) * P] for x in (woh, wol)],
                                   [x[:, m, :] for x in (ath, atl)], m == 0, m == DT - 1)
                mm.then_inc(full, 1)

            def max_scores(b, qt, j):
                step, _ = step_of(b, qt)
                pair, half = divmod(j, 2)
                t, keys = qt % ST, kan if qt >= ST else ka
                if j == 0:
                    e.wait_ge(q_landed[t], 16 * (b.ahead() + (1 if qt >= ST else 0)) if b.it is not None else 16)
                    if qt >= ST:
                        e.wait_ge(s["k_landed"], 96 * (b.ahead() + 1))
                wait(e, s["max_read"], step * AH + j - 1)
                n = (t + 1) * P
                e.matmul(mbank[half][:, 0:n], qa[:, pair, t * P:n], keys[half][:, 0:n], start=True, stop=False,
                         skip_group_check=True)
                e.matmul(mbank[half][:, t * P:n], identb[:, :], below[:, :], start=False, stop=True,
                         skip_group_check=True).then_inc(s["max_full"], 1)

            def score(b, g):
                qt, hg, kt = place(g)
                if g == 0:
                    e.wait_ge(s["keys_kept"], (b.it + 1) * 3)
                if g == unit_base(qt):
                    e.wait_ge(m_landed[qt % 2], 64 * (b.it * 2 + qt // 2 + 1))
                wait(e, s["exp_done"], b.it * UB + g - 1)
                half, head = divmod(4 * hg, PAIRS)
                diagonal = kt == qt
                mm = e.matmul(sbank[g % 2][:, :], ka[half][:, kt * P:(kt + 1) * P],
                              qa[:, head:head + 4, qt * P:(qt + 1) * P], start=True, stop=not diagonal,
                              skip_group_check=True)
                if diagonal:
                    mm = e.matmul(sbank[g % 2][:, :], identb[:, :], above[:, :], start=False, stop=True,
                                  skip_group_check=True)
                mm.then_inc(s["scores_full"], 1)

            def weigh(b, g):
                qt, hg, kt = place(g)
                if kt == 0:
                    wait(e, s["o_copied"], b.it * ST * HG + qt * HG + hg - 1)
                e.wait_ge(*split_by(b, g))
                for x in (ph, pl):
                    mm = e.matmul(obank[hg % 2][0:VROWS, :], vs[:, kt, :], x[:, g % 4, :], start=kt == 0 and x is ph,
                                  stop=kt == qt and x is pl)
                mm.then_inc(s["pv_done"], 1)

            def body(b):
                for kind, *x in b.steps():
                    if kind != "read":
                        {"scores": score, "max": max_scores, "pv": weigh, "small": small_product}[kind](b, *x)

            first = Batch(None)
            for x in BEFORE:
                for j in range(AH) if x[0] == "mT" else ():
                    max_scores(first, x[1], j)
                small_product(first, *x)
            batches(e, body)
            for d in range(DT):
                small_product(Finish(), "Wo", d)

        @block.vector
        def _(e):
            def read_small(b, kind, i, chain):
                k, n = b.misc((kind, i))
                bank, free = misc[k], misc_free[k]
                if kind == "mean":
                    pass
                elif kind == "var":
                    e.wait_ge(misc_full[k], n)
                    e.tensor_scalar(tmp[0][:, :], bank[:, :], LN_EPS, None, ALU.add).then_inc(free, 1)
                elif kind == "KV":
                    e.wait_ge(s["kv_high"], b.ahead() + 1)
                    e.scalar_tensor_tensor(kxl[32:KV, :], bank[32:KV, :], AD ** -0.5, f32(kxh[32:KV, :]), ALU.mult,
                                           ALU.subtract).then_inc(s["kv_low"], 1)
                    e.wait_ge(s["kv_low"], b.ahead() + 1)
                    e.sem_inc(free, 1)
                elif kind == "Vt":
                    e.wait_ge(s["v_high"], b.ahead() + 1)
                    e.tensor_tensor(vn[:, :, 32:32 + AD], bank[:, 0:ST * AD].rearrange("p (t d) -> p t d", t=ST),
                                    f32(vn[:, :, 0:AD]), ALU.subtract).then_inc(s["v_low"], 1)
                    e.wait_ge(s["v_low"], b.ahead() + 1)
                    e.sem_inc(free, 1)
                elif kind == "Q":
                    e.wait_ge(s["q_high"], b.ahead() * DT + i + 1)
                    e.tensor_tensor(qsl[:, i % 2], bank[:, :], f32(qsh[:, i % 2]), ALU.subtract).then_inc(s["q_low"], 1)
                    e.wait_ge(s["q_low"], b.ahead() * DT + i + 1)
                    e.sem_inc(free, 1)
                elif kind == "mT":
                    step, par = step_of(b, i)
                    e.wait_ge(s["m_high"], step + 1)
                    e.scalar_tensor_tensor(ml[:, par], bank[0:AH, 0:P], -1.0, f32(mh[:, par]), ALU.mult,
                                           ALU.subtract).then_inc(s["m_low"], 1)
                    e.wait_ge(s["m_low"], step + 1)
                    e.sem_inc(free, 1)
                else:
                    e.wait_ge(misc_full[k], n)
                    here = xt[:, i, bass.ds((b.it - 1) * S, S)]
                    e.tensor_tensor(here, here, bank[:, :], ALU.add).then_inc(free, 1)

            def centre(b, d):
                k, n = b.misc(("mean", 0))
                if d == 0:
                    e.wait_ge(misc_full[k], n)
                    wait(e, s["zl_ready"], b.ahead() * DT)
                    if b.it is not None and not b.first:
                        e.wait_ge(s["at_low"], (b.it - 1) * DT)
                e.tensor_tensor(zf[:, d], xt[:, d, bass.ts(0 if b.it is None else b.it + 1, S)], misc[k][:, :],
                                ALU.subtract).then_inc(s["centred"], 1)
                if d == DT - 1:
                    e.wait_ge(s["centred"], (b.ahead() + 1) * DT)
                    e.sem_inc(misc_free[k], 1)

            def inverse_std(b, chain):
                e.wait_ge(s["seed"], b.ahead() + 1)
                chain(e.scalar_tensor_tensor(tmp[2][:, :], tmp[0][:, :], -0.5, tmp[1][:, :], ALU.mult, ALU.mult))
                chain(e.tensor_tensor(tmp[2][:, :], tmp[2][:, :], tmp[1][:, :], ALU.mult))
                chain(e.scalar_tensor_tensor(tmp[0][:, :], tmp[2][:, :], 1.5, tmp[1][:, :], ALU.add, ALU.mult))

            def normalise(b, d):
                e.tensor_tensor(zf[:, d], zf[:, d], tmp[0][:, :], ALU.mult).then_inc(s["z_ready"], 1)

            def find_max(b, qt, j):
                step, par = step_of(b, qt)
                pair, half = divmod(j, 2)
                e.wait_ge(s["max_full"], step * AH + j + 1)
                if j == 0:
                    wait(e, s["m_high"], step - 1)
                head = half * PAIRS + pair
                e.tensor_reduce(mx[:, par, head:head + 1], mbank[half][:, 0:(qt % ST + 1) * P], AX.X,
                                ALU.max).then_inc(s["max_read"], 1)

            def low_probs(b, g):
                e.wait_ge(s["exp_done"], b.it * UB + g + 1)
                e.tensor_tensor(pl[:, g % 4], pf[:, g % 4], f32(ph[:, g % 4]), ALU.subtract)\
                    .then_inc(s["low_by_vector"], 1)

            def invert_sums(b):
                e.wait_ge(s["sums_landed"], 16 * (b + 1))
                e.reciprocal(sums[:, :], sums[:, :]).then_inc(s["inv_ready"], 1)

            def out_tile(count, chain):
                e.wait_ge(s["out_landed"], 32 * (count + 1))
                chain(e.tensor_tensor(at[:, 0], at[:, 0], at[:, 1], ALU.add))
                e.tensor_tensor(at[:, 0], at[:, 0], at[:, 2], ALU.mult).then_inc(s["at_ready"], 1)

            def low_out(m, count):
                e.wait_ge(s["at_high"], count + 1)
                e.tensor_tensor(atl[:, m], at[:, 0], f32(ath[:, m]), ALU.subtract).then_inc(s["at_low"], 1)

            def keep_keys(b):
                e.wait_ge(s["k_landed"], 96 * (b.it + 1))
                wait(e, s["pv_done"], b.it * UB)
                e.tensor_copy(ka[0][:, :], kan[0][:, :]).then_inc(s["keys_kept"], 1)
                e.tensor_copy(ka[1][:, :], kan[1][:, :]).then_inc(s["keys_kept"], 1)
                e.wait_ge(s["v_low"], b.it + 1)
                e.tensor_copy(vs[:, :, :], vn[:, :, :]).then_inc(s["keys_kept"], 1)

            def body(b):
                chain = Chain(e, s["dve_step"], 3 if b.first else b.it * 7 - 1)
                keep_keys(b)
                for kind, *x in b.steps():
                    if kind == "max":
                        find_max(b, *x)
                    elif kind == "scores":
                        g = x[0]
                        if not b.last:
                            if MEAN < g <= MEAN + DT:
                                centre(b, g - MEAN - 1)
                            if g == VAR + 3:
                                inverse_std(b, chain)
                            if VAR + 3 < g <= VAR + 3 + DT:
                                normalise(b, g - VAR - 4)
                        if not b.first:
                            if g == 8:
                                invert_sums(b.it - 1)
                            if OUT <= g < OUT + 4 * DT and (g - OUT) % 4 == 0:
                                out_tile((b.it - 1) * DT + (g - OUT) // 4, chain)
                            if OUT < g <= OUT + 4 * DT and (g - OUT) % 4 == 1:
                                m = (g - OUT) // 4
                                low_out(m, (b.it - 1) * DT + m)
                    elif kind == "read":
                        read_small(b, *x, chain)
                    if kind == "scores" and x[0] % 4 == 2:
                        low_probs(b, x[0] - 1)

            first = Batch(None)
            chain = Chain(e, s["dve_step"])
            for x in BEFORE:
                for j in range(AH) if x[0] == "mT" else ():
                    find_max(first, x[1], j)
                read_small(first, *x, chain)
                for d in range(DT):
                    if x[0] == "mean":
                        centre(first, d)
                    if x[0] == "var":
                        if d == 0:
                            inverse_std(first, chain)
                        normalise(first, d)
            batches(e, body)
            chain = Chain(e, s["dve_step"], 7 * NB - 4)
            invert_sums(NB - 1)
            for m in range(DT):
                out_tile((NB - 1) * DT + m, chain)
                low_out(m, (NB - 1) * DT + m)
            for d in range(DT):
                read_small(Finish(), "Wo", d, chain)

        @block.scalar
        def _(e):
            def read_small(b, kind, i):
                k, n = b.misc((kind, i))
                bank = misc[k]
                if kind == "var":
                    e.wait_ge(misc_free[k], n)
                    e.activation(tmp[1][:, :], tmp[0][:, :], ACT.Ln).then_inc(s["act_step"], 1)
                    e.wait_ge(s["act_step"], b.ahead() + 1)
                    e.activation(tmp[1][:, :], tmp[1][:, :], ACT.Exp, scale=-0.5).then_inc(s["seed"], 1)
                elif kind == "KV":
                    e.wait_ge(misc_full[k], n)
                    wait(e, s["k_landed"], 96 * b.ahead())
                    e.copy(vt[:, :], bank[0:AD, :]).then_inc(s["vt_copied"], 1)
                    e.activation(kxh[32:KV, :], bank[32:KV, :], ACT.Copy, scale=AD ** -0.5).then_inc(s["kv_high"], 1)
                elif kind == "Vt":
                    e.wait_ge(misc_full[k], n)
                    wait(e, s["keys_kept"], 3 * b.ahead())
                    e.copy(vn[:, :, 0:AD], bank[:, 0:ST * AD].rearrange("p (t d) -> p t d", t=ST)).then_inc(s["v_high"], 1)
                elif kind == "Q":
                    e.wait_ge(misc_full[k], n)
                    wait(e, q_stored[i % 2], 48 * (DT // 2 * b.ahead() + i // 2))
                    e.copy(qsh[:, i % 2], bank[:, :]).then_inc(s["q_high"], 1)
                elif kind == "mT":
                    step, par = step_of(b, i)
                    e.wait_ge(misc_full[k], n)
                    wait(e, m_landed[par], 64 * (((-1 if b.it is None else b.it) * 2) + i // 2))
                    e.activation(mh[:, par], bank[0:AH, 0:P], ACT.Copy, scale=-1.0).then_inc(s["m_high"], 1)

            def square(b, d):
                e.wait_ge(s["centred"], b.ahead() * DT + d + 1)
                if d >= 2:
                    e.wait_ge(s["sq_added"], b.ahead() * 3 + 1)
                e.activation(tmp[d % 2][:, :], zf[:, d], ACT.Square).then_inc(s["sq_ready"], 1)

            def high_z(b, d):
                e.wait_ge(s["z_ready"], b.ahead() * DT + d + 1)
                e.copy(zh[:, d], zf[:, d]).then_inc(s["zh_ready"], 1)

            def exps(b, g):
                e.wait_ge(s["scores_full"], b.it * UB + g + 1)
                if g >= 4 or not b.first:
                    before = (b, g - 4) if g >= 4 else (Batch(b.it - 1), g - 4 + UB)
                    e.wait_ge(*split_by(*before))
                e.activation(pf[:, g % 4], sbank[g % 2][:, :], ACT.Exp)
                wait(e, s["pv_done"], b.it * UB + g - 3)
                e.activation(ph[:, g % 4], sbank[g % 2][:, :], ACT.Exp).then_inc(s["exp_done"], 1)

            def copy_out(b, g):
                group = b.it * ST * HG + group_end(g)
                hg = place(g)[1]
                e.wait_ge(s["pv_done"], b.it * UB + g + 1)
                if hg % 2 == 0:
                    wait(e, o_stored[hg // 2 % 2], 48 * (b.it * 2 * ST + group_end(g) // 4))
                e.copy(ot[:, hg // 2 % 2, hg % 2], obank[hg % 2][0:VROWS, :].rearrange("p (h q) -> p h q", h=4))\
                    .then_inc(s["o_copied"], 1)

            def high_out(m, count):
                e.wait_ge(s["at_ready"], count + 1)
                e.copy(ath[:, m], at[:, 0]).then_inc(s["at_high"], 1)

            def body(b):
                for kind, *x in b.steps():
                    if kind == "scores":
                        g = x[0]
                        exps(b, g)
                        if not b.last:
                            if MEAN + 1 < g <= MEAN + 1 + DT:
                                square(b, g - MEAN - 2)
                            if VAR + 4 < g <= VAR + 4 + DT:
                                high_z(b, g - VAR - 5)
                        if not b.first and OUT <= g < OUT + 4 * DT and (g - OUT) % 4 == 0:
                            m = (g - OUT) // 4
                            high_out(m, (b.it - 1) * DT + m)
                    elif kind == "pv" and group_end(x[0]) is not None:
                        copy_out(b, x[0])
                    elif kind == "small":
                        read_small(b, *x)

            first = Batch(None)
            for x in BEFORE:
                read_small(first, *x)
                for d in range(DT):
                    if x[0] == "mean":
                        square(first, d)
                    if x[0] == "var":
                        high_z(first, d)
            batches(e, body)
            for m in range(DT):
                high_out(m, (NB - 1) * DT + m)

        @block.gpsimd
        def _(e):
            def sum_x(b, chain):
                wait(e, s["z_ready"], b.ahead() * DT)
                here = xt[:, :, bass.ts(0 if b.it is None else b.it + 1, S)]
                chain(e.tensor_tensor(tmp[2][:, :], here[:, 0], here[:, 1], ALU.add))
                chain(e.tensor_tensor(tmp[2][:, :], tmp[2][:, :], here[:, 2], ALU.add))
                e.tensor_tensor(tmp[2][:, :], tmp[2][:, :], here[:, 3], ALU.add).then_inc(s["x_summed"], 1)

            def sum_squares(b, n):
                e.wait_ge(s["sq_ready"], b.ahead() * DT + n + 2)
                if n:
                    e.wait_ge(s["sq_added"], b.ahead() * 3 + n)
                e.tensor_tensor(tmp[2][:, :], tmp[0][:, :] if n == 0 else tmp[2][:, :], tmp[(n + 1) % 2][:, :],
                                ALU.add).then_inc(s["sq_added"], 1)

            def low_z(b, d):
                e.wait_ge(s["zh_ready"], b.ahead() * DT + d + 1)
                e.tensor_tensor(zl[:, d], zf[:, d], f32(zh[:, d]), ALU.subtract).then_inc(s["zl_ready"], 1)

            def low_probs(b, g):
                e.wait_ge(s["exp_done"], b.it * UB + g + 1)
                e.tensor_tensor(pl[:, g % 4], pf[:, g % 4], f32(ph[:, g % 4]), ALU.subtract)\
                    .then_inc(s["low_by_pool"], 1)

            def body(b):
                if not b.last:
                    sum_x(b, Chain(e, s["pool_step"], b.it * 2 + 2))
                for kind, *x in b.steps():
                    if kind == "scores":
                        g = x[0]
                        if g % 4 != 1:
                            low_probs(b, g)
                        if b.last:
                            continue
                        if g in (MEAN + 4, MEAN + 6, MEAN + 7):
                            sum_squares(b, (MEAN + 4, MEAN + 6, MEAN + 7).index(g))
                        if VAR + 5 < g <= VAR + 5 + DT:
                            low_z(b, g - VAR - 6)

            first = Batch(None)
            sum_x(first, Chain(e, s["pool_step"]))
            for n in range(3):
                sum_squares(first, n)
            for d in range(DT):
                low_z(first, d)
            batches(e, body)

        @block.sync
        def _(e):
            def send_keys(b):
                e.wait_ge(s["kv_low"], b.ahead() + 1)
                wait(e, s["keys_kept"], 3 * b.ahead())
                for half in range(2):
                    for row, part in ((R_QHI, kxh), (R_QLO, kxh), (R_QHI2, kxl)):
                        r = 64 * half + row
                        e.dma_start(f32(kan[half][r:r + AD, :]), f32(part[32:KV, :])).then_inc(s["k_landed"], 16)

            def send_queries(b, m):
                if m == 0:
                    for t in range(ST):
                        wait(e, q_landed[t], 16 * b.ahead())
                e.wait_ge(s["q_low"], b.ahead() * DT + m + 1)
                half, head = divmod(8 * m, PAIRS)
                for row, part in ((R_QHI, qsh), (R_QLO, qsl), (R_QHI2, qsh)):
                    to = q_dram[half, row:row + AD, head:head + 8, :].rearrange("d h t -> h d t")
                    e.dma_start(to, f32(part[:, m % 2])).then_inc(q_stored[m % 2], 16)

            def load_queries(b, t, used=True):
                if used:
                    e.wait_ge(s["scores_full"], b.it * UB + unit_base(t + 1))
                e.dma_start(f32(qa[:, :, t * P:(t + 1) * P]),
                            q_dram[:, :, :, t * P:(t + 1) * P].rearrange("a r h t -> (a r) h t")).then_inc(q_landed[t], 16)

            def queries_stored(b):
                for k in range(2):
                    e.wait_ge(q_stored[k], 48 * DT // 2 * (b.ahead() + 1))

            def send_max(b, i):
                step, par = step_of(b, i)
                e.wait_ge(s["m_low"], step + 1)
                t = i % ST * P
                for half in range(2):
                    for row, part in ((R_MAX, mh), (R_MAX + 1, ml)):
                        r = 64 * half + row
                        e.dma_start(f32(qa[r:r + 1, :, t:t + P]), f32(part[half * PAIRS:(half + 1) * PAIRS, par, :]))\
                            .then_inc(m_landed[par], 16)

            def store_out(b, g):
                qt, hg, _ = place(g)
                tile = hg // 2
                e.wait_ge(s["o_copied"], b.it * ST * HG + group_end(g) + 1)
                for c in range(2):
                    to = o_dram[bass.ds(b.it, 1), c, tile * P:(tile + 1) * P, qt * P:(qt + 1) * P]\
                        .rearrange("b (h d) q -> d (b h) q", d=AD)
                    e.dma_start(to, ot[32 * c:32 * c + AD, tile % 2].rearrange("p a h q -> p (a h) q"))\
                        .then_inc(o_stored[tile % 2], 16)
                e.dma_start(sums_dram[bass.ds(b.it, 1), 8 * tile:8 * tile + 8, qt * P:(qt + 1) * P],
                            ot[64:65, tile % 2].rearrange("p a h q -> p (a h) q")).then_inc(o_stored[tile % 2], 16)

            def load_sums(b):
                for k in range(2):
                    e.wait_ge(o_stored[k], 48 * 2 * ST * (b + 1))
                e.dma_start(sums[:, :], sums_dram[bass.ds(b, 1)].rearrange("b h (c q) -> (b h c) q", c=ST))\
                    .then_inc(s["sums_landed"], 16)

            def store_inverses(b):
                e.wait_ge(s["inv_ready"], b + 1)
                e.dma_start(inv_dram[bass.ds(b, 1)].rearrange("b h (c q) -> (b h c) q", c=ST), sums[:, :])\
                    .then_inc(s["inv_stored"], 16)

            def load_out(b, m):
                if m == 0:
                    e.wait_ge(s["inv_stored"], 16 * (b + 1))
                else:
                    wait(e, s["at_low"], b * DT + m)
                e.dma_start(at[:, 0:2, :], o_dram[bass.ds(b, 1), :, m * P:(m + 1) * P, :].rearrange("b c p t -> p (b c) t"))\
                    .then_inc(s["out_landed"], 16)
                heads = P // AD
                e.dma_start(at[:, 2, :], inv_dram[bass.ds(b, 1), heads * m:heads * (m + 1)].rearrange("b h t -> (b h) t")
                            .unsqueeze(1).broadcast_to([heads, AD, S])).then_inc(s["out_landed"], 16)

            def body(b):
                for kind, *x in b.steps():
                    if kind == "scores" and not b.first:
                        g = x[0]
                        if g == 2:
                            load_sums(b.it - 1)
                        if g == 14:
                            store_inverses(b.it - 1)
                        if OUT - 6 <= g < OUT + 4 * DT - 6 and (g - OUT + 6) % 4 == 0:
                            load_out(b.it - 1, (g - OUT + 6) // 4)
                    if kind == "scores" and x[0] == unit_base(3) + 1 and not b.last:
                        load_queries(b, 2)
                    if kind == "pv" and group_end(x[0]) is not None and group_end(x[0]) % 2:
                        store_out(b, x[0])
                    if kind != "small":
                        continue
                    if x[0] == "mT":
                        send_max(b, x[1])
                    if x[0] == "KV":
                        send_keys(b)
                    if x[0] == "Q":
                        send_queries(b, x[1])
                        if x[1] == DT - 1:
                            queries_stored(b)
                            load_queries(b, 0)
                            load_queries(b, 1)
                if not b.last:
                    load_queries(b, 3)

            first = Batch(None)
            send_keys(first)
            for m in range(DT):
                send_queries(first, m)
            queries_stored(first)
            for t in range(ST):
                load_queries(first, t, used=False)
            send_max(first, ST)
            send_max(first, ST + 1)
            batches(e, body)
            load_sums(NB - 1)
            store_inverses(NB - 1)
            for m in range(DT):
                load_out(NB - 1, m)


QH, KVH, HD = 32, 8, 128
GRP = QH // KVH
WINDOW = 128
SM_SCALE = HD ** -0.5
HALF = HD // 2
UNITS = 2 * GRP
BELOW_ALL = -3.0e38


def window_attention(nc, drams, xt, consts, tables):
    ident, ones = consts[0], consts[2]
    cos, sin, mask = tables
    wq, wk, wv, wo = drams
    with ExitStack() as st:
        sb, ps, sem = sb_in(nc, st), ps_in(nc, st), sem_in(nc)
        yh, yl = (sb(f"y_{x}", [P, DT, 2 * S], F32R) for x in ("high", "low"))
        wqh, wql = (sb(f"wq_{x}", [P, DT, GRP * HD], F32R) for x in ("high", "low"))
        wkvh, wkvl = (sb(f"wkv_{x}", [P, 2, DT, HD], F32R) for x in ("high", "low"))
        woh, wol = (sb(f"wo_{x}", [P, GRP, D], F32R) for x in ("high", "low"))
        wq_raw, wkv_raw = sb("wq_raw", [P, DT, 2 * HD]), sb("wkv_raw", [P, 2, DT, HD])
        wo_raw = sb("wo_raw", [P, GRP, D])
        qh, ql = (sb(f"q_{x}", [P, 2, S], F32R) for x in ("high", "low"))
        kh, kl = (sb(f"k_{x}", [P, 2, S], F32R) for x in ("high", "low"))
        vh, vl = (sb(f"v_{x}", [P, 2, ST, HD], F32R) for x in ("high", "low"))
        vt = sb("v_by_dim", [P, S])
        ra, rb = sb("rope_straight", [P, 2, S]), sb("rope_crossed", [P, 2, S])
        probs = sb("probs", [P, 2, ST, 2 * P])
        top, bias = sb("score_max", [P, 2, ST]), sb("exp_bias", [P, 2, ST])
        nothing = sb("nothing", [1, 1])
        total, share = sb("exp_sum", [P, 2, ST]), sb("exp_sum_inverse", [P, 2, ST])
        with ExitStack() as early:
            sbe = sb_in(nc, early)
            zf, sq = sbe("y_centred", [P, DT, S]), sbe("y_squares", [P, DT, S])
            tmp = [sbe(f"y_tmp{i}", [P, S]) for i in range(3)]
        oh, ol = (sb(f"o_{x}", [P, 2, GRP, S], F32R) for x in ("high", "low"))
        pth, ptl = (sb(f"probs_turned_{x}", [P, ST * 2 * P - P], F32R) for x in ("high", "low"))

        ring = [ps(f"proj{i}", [P, S]) for i in range(2)]
        scores = ps("scores", [P, ST, 2 * P])
        pt = ps("probs_turned", [P, 2 * S])
        obank, wbank = ps("o_sum", [P, S]), ps("w_sum", [P, S])

        ring_full, ring_free = [sem(f"b_proj_full{i}") for i in range(2)], [sem(f"b_proj_free{i}") for i in range(2)]
        o_full, w_full, w_free = (sem(f"b_{n}") for n in ("o_full", "w_full", "w_free"))
        ln_mean, ln_centred, ln_squared, ln_var, ln_vare, ln_seed, ln_z, ln_yh, ln_yl = (
            sem(f"b_ln_{n}") for n in ("mean", "centred", "squared", "var", "var_read", "seed", "z", "yh", "yl"))
        act_step, dve_step = sem("b_act_step"), sem("b_dve_step")
        raw_in = {n: sem(f"b_{n}_raw_landed") for n in ("wo", "wkv", "wq")}
        w_high, w_low = ({n: sem(f"b_{n}_{x}_ready") for n in ("wo", "wkv", "wq")} for x in ("high", "low"))
        crossed, roped, rope_high, rope_low = (sem(f"b_{n}") for n in ("rope_products", "roped", "rope_high", "rope_low"))
        vt_ready, v_high, v_low = sem("b_v_by_dim"), sem("b_v_high"), sem("b_v_low")
        s_full, s_max, bias_ready, exp_done, p_ready = (
            sem(f"b_{n}") for n in ("scores_full", "scores_max", "bias_ready", "exp_done", "probs_ready"))
        pt_full, pt_high, pt_low, pv_done = (sem(f"b_{n}") for n in ("turned_full", "turned_high", "turned_low", "pv_done"))
        o_high, o_low = sem("b_o_high"), sem("b_o_low")

        proj = [("Q", 2), ("Q", 3), ("Q", 4), ("K", 1), ("Q", 5), ("V", 1), ("N", 1), ("Q", 6), ("Q", 7),
                ("Q", 8), ("K", 2), ("Q", 9), ("V", 2), ("N", 2)]
        ropes = [x for x in proj if x[0] in "QK"]
        FIRST = proj[-5:]
        AHEAD, AHEAD_R = 5, 3

        def bank_of(it, kind, n):
            i = proj.index((kind, n)) + AHEAD
            return i % 2, it * (len(proj) // 2) + i // 2 + 1

        def rope_of(it, kind, n):
            i = ropes.index((kind, n)) + AHEAD_R
            return i % 2, it * len(ropes) + i + 1

        def quarter_of(it, u):
            return it * UNITS + u - GRP, (u // GRP - 1) % 2, u % GRP

        def groups(e, before, body, after=None):
            with e.Fori(0, NB // 2) as pair:
                before(pair)
                body(pair, 0, pair * KVH, True, False)
                with e.Fori(1, KVH - 1) as g:
                    body(pair, g, pair * KVH + g, False, False)
                body(pair, KVH - 1, pair * KVH + (KVH - 1), False, True)
                if after:
                    after(pair, pair * KVH + KVH)

        def head(i):
            return slice(i * HD, (i + 1) * HD)

        def prepare(u, last):
            steps = {0: [("Q", 2)], 1: [("Q", 3)], 2: [("Q", 4), ("K", 1)], 3: [("Q", 5), ("V", 1), ("N", 1)],
                     4: [("Q", 6)], 5: [("Q", 7)], 6: [("Q", 8), ("K", 2)], 7: [("Q", 9), ("V", 2), ("N", 2)]}[u]
            return [x for x in steps if not (last and u >= 6)]

        block = st.enter_context(nc.Block())

        @block.sync
        def _(e):
            def load_qkv(g, it):
                e.wait_ge(w_low["wkv"], it)
                cols = bass.ds(g * HD, HD)
                for i, w in enumerate((wk, wv)):
                    e.dma_start(wkv_raw[:, i], w[:, cols].rearrange("(t p) n -> p t n", p=P)).then_inc(raw_in["wkv"], 16)
                for two in range(GRP // 2):
                    e.wait_ge(w_low["wq"], it * GRP + 2 * two)
                    e.dma_start(wq_raw[:, :, :], wq[:, bass.ds((g * GRP + 2 * two) * HD, 2 * HD)]
                                .rearrange("(t p) n -> p t n", p=P)).then_inc(raw_in["wq"], 16)

            def load_wo(g, it):
                e.wait_ge(w_low["wo"], it * DT)
                e.dma_start(wo_raw[:, :, :], wo[bass.ds(g * GRP * HD, GRP * HD), :]
                            .rearrange("(t p) n -> p t n", p=P)).then_inc(raw_in["wo"], 16)

            def before(pair):
                load_qkv(0, pair * KVH)
                load_wo(0, pair * KVH)

            def body(pair, g, it, first, last):
                if not last:
                    load_qkv(g + 1, it + 1)
                    load_wo(g + 1, it + 1)

            groups(e, before, body)

        @block.tensor
        def _(e):
            def layernorm_sums(b):
                for d in range(DT):
                    mm = e.matmul(ring[0][:, :], ones[:, :], xt[:, d, bass.ds(b * S, S)], start=d == 0, stop=d == DT - 1)
                mm.then_inc(ln_mean, 1)
                e.wait_ge(ln_squared, b + 1)
                for d in range(DT):
                    mm = e.matmul(ring[1][:, :], ones[:, :], sq[:, d, :], start=d == 0, stop=d == DT - 1)
                mm.then_inc(ln_var, 1)
                e.wait_ge(ln_vare, b + 1)

            def three(out, w, z, first, last, **kw):
                for n, (a, b) in enumerate([(w[0], z[0]), (w[0], z[1]), (w[1], z[0])]):
                    mm = e.matmul(out, a, b, start=first and n == 0, stop=last and n == 2, **kw)
                return mm

            def project(it, kind, n):
                k, count = bank_of(it, kind, n)
                e.wait_ge(ring_free[k], count - 1)
                if kind == "Q":
                    i, b = n % GRP, n // GRP % 2
                    e.wait_ge(w_low["wq"], it * GRP + (GRP if n >= UNITS else 0) + i + 1)
                    w = [x[:, :, head(i)] for x in (wqh, wql)]
                elif kind in "KV":
                    b = n % 2
                    e.wait_ge(w_low["wkv"], it + (1 if n >= 2 else 0) + 1)
                    w = [x[:, 0 if kind == "K" else 1] for x in (wkvh, wkvl)]
                if kind == "N":
                    e.wait_ge(vt_ready, it * 2 + n + 1)
                    for t in range(ST):
                        mm = e.transpose(ring[k][:, t * HD:(t + 1) * HD], vt[:, t * P:(t + 1) * P], ident[:, :])
                else:
                    for d in range(DT):
                        mm = three(ring[k][:, :], [x[:, d, :] for x in w],
                                   [y[:, d, b * S:(b + 1) * S] for y in (yh, yl)], d == 0, d == DT - 1)
                mm.then_inc(ring_full[k], 1)

            def score(it, n):
                before = rope_of(it, "Q", n) if n > 1 else rope_of(it - 1, "Q", 9)
                e.wait_ge(rope_low, before[1] + 2)
                if n % GRP == 0:
                    e.wait_ge(rope_low, rope_of(it, "K", n // GRP)[1] + 2)
                e.wait_ge(s_max, (it * UNITS + n) * ST)
                for t in range(ST):
                    keys = slice(max(t - 1, 0) * P, (t + 1) * P)
                    mm = three(scores[:, t, (P if t == 0 else 0):], [x[:, n % 2, t * P:(t + 1) * P] for x in (qh, ql)],
                               [x[:, n // GRP % 2, keys] for x in (kh, kl)], True, True)
                mm.then_inc(s_full, 1)

            def turn(it, u):
                e.wait_ge(p_ready, it * UNITS + u + 1)
                e.wait_ge(pt_low, it * UNITS + u)
                for k in range(ST):
                    mm = e.transpose(pt[:, 2 * k * P:(2 * k + 1) * P], probs[:, u % 2, k, P:2 * P], ident[:, :])
                    if k + 1 < ST:
                        e.transpose(pt[:, (2 * k + 1) * P:(2 * k + 2) * P], probs[:, u % 2, k + 1, 0:P], ident[:, :])
                mm.then_inc(pt_full, 1)

            def weigh(it, u):
                b = u // GRP
                e.wait_ge(pt_low, it * UNITS + u + 1)
                e.wait_ge(v_low, it * 2 + b + 1)
                e.wait_ge(o_low, it * UNITS + u)
                for k in range(ST):
                    q = slice(k * P, min(k + 2, ST) * P)
                    cols = slice(2 * k * P, min(2 * k + 2, 2 * ST - 1) * P)
                    mm = three(obank[:, q], [x[:, b, k, :] for x in (vh, vl)], [x[:, cols] for x in (pth, ptl)],
                               k == 0, k == ST - 1, skip_group_check=True)
                mm.then_inc(o_full, 1)

            def project_out(it, u):
                n, half, d = quarter_of(it, u)
                if d == 0:
                    e.wait_ge(o_low, n + GRP)
                if half == 0:
                    e.wait_ge(w_low["wo"], it * DT + d + 1)
                e.wait_ge(w_free, n)
                for i in range(GRP):
                    mm = three(wbank[:, :], [x[:, i, d * P:(d + 1) * P] for x in (woh, wol)],
                               [x[:, half, i, :] for x in (oh, ol)], i == 0, i == GRP - 1)
                mm.then_inc(w_full, 1)

            def before(pair):
                for k in range(2):
                    e.wait_ge(ring_free[k], pair * KVH * (len(proj) // 2))
                for b in range(2):
                    layernorm_sums(pair * 2 + b)
                e.wait_ge(ln_yl, pair * 2 + 2)
                for kind, n in FIRST:
                    project(pair * KVH - 1, kind, n)
                score(pair * KVH - 1, UNITS)

            def body(pair, g, it, first, last):
                for u in range(UNITS):
                    steps = prepare(u, last)
                    for kind, n in steps[:1]:
                        project(it, kind, n)
                    turn(it, u)
                    if not (last and u == UNITS - 1):
                        score(it, u + 1)
                    if not (first and u < GRP):
                        project_out(it, u)
                    for kind, n in steps[1:]:
                        if kind != "N":
                            project(it, kind, n)
                    weigh(it, u)
                    for kind, n in steps[1:]:
                        if kind == "N":
                            project(it, kind, n)

            def after(pair, it):
                for u in range(GRP):
                    project_out(it, u)

            groups(e, before, body, after)

        @block.vector
        def _(e):
            def layernorm(b, half, chain):
                e.wait_ge(ln_mean, b + 1)
                e.wait_ge(ln_yl, b)
                e.tensor_tensor(zf[:, :, :], xt[:, :, bass.ts(b, S)],
                                ring[0][:, :].unsqueeze(1).broadcast_to([P, DT, S]), ALU.subtract).then_inc(ln_centred, 1)
                e.wait_ge(ln_var, b + 1)
                e.tensor_scalar(tmp[0][:, :], ring[1][:, :], LN_EPS, None, ALU.add).then_inc(ln_vare, 1)
                e.wait_ge(ln_seed, b + 1)
                chain(e.scalar_tensor_tensor(tmp[2][:, :], tmp[0][:, :], -0.5, tmp[1][:, :], ALU.mult, ALU.mult))
                chain(e.tensor_tensor(tmp[2][:, :], tmp[2][:, :], tmp[1][:, :], ALU.mult))
                chain(e.scalar_tensor_tensor(tmp[0][:, :], tmp[2][:, :], 1.5, tmp[1][:, :], ALU.add, ALU.mult))
                e.tensor_tensor(zf[:, :, :], zf[:, :, :], tmp[0][:, :].unsqueeze(1).broadcast_to([P, DT, S]),
                                ALU.mult).then_inc(ln_z, 1)
                e.wait_ge(ln_yh, b + 1)
                cols = slice(half * S, (half + 1) * S)
                e.tensor_tensor(yl[:, :, cols], zf[:, :, :], f32(yh[:, :, cols]), ALU.subtract).then_inc(ln_yl, 1)

            def find_max(it, n):
                e.wait_ge(s_full, it * UNITS + n + 1)
                e.memset(nothing[:, :], 0.0)
                for t in range(ST):
                    k = slice(P if t == 0 else 0, 2 * P)
                    e.tensor_tensor_reduce(probs[:, n % 2, t, k], scores[:, t, k], mask[:, k], 1.0, BELOW_ALL,
                                           ALU.add, ALU.max, top[:, n % 2, t:t + 1]).then_inc(s_max, 1)
                e.wait_ge(s_max, (it * UNITS + n + 1) * ST)
                e.tensor_scalar(bias[:, n % 2], top[:, n % 2], -SM_SCALE, None, ALU.mult).then_inc(bias_ready, 1)

            def normalise(it, n, chain):
                e.wait_ge(exp_done, (it * UNITS + n + 1) * ST)
                chain(e.reciprocal(share[:, n % 2], total[:, n % 2]))
                for t in range(ST):
                    part = probs[:, n % 2, t, (P if t == 0 else 0):]
                    last = e.tensor_scalar(part, part, share[:, n % 2, t:t + 1], None, ALU.mult)
                last.then_inc(p_ready, 1)

            def rope(it, kind, n):
                k, count = bank_of(it, kind, n)
                slot, r = rope_of(it, kind, n)
                e.wait_ge(ring_full[k], count)
                e.wait_ge(rope_low, r)
                e.tensor_tensor(ra[:, slot], ring[k][:, :], cos[:, :], ALU.mult)
                e.tensor_tensor(rb[0:HALF, slot], ring[k][HALF:, :], sin[HALF:, :], ALU.mult)
                e.tensor_tensor(rb[HALF:, slot], ring[k][0:HALF, :], sin[0:HALF, :], ALU.mult).then_inc(ring_free[k], 1)

            def low_values(it, n):
                k, count = bank_of(it, "N", n)
                e.wait_ge(v_high, it * 2 + n + 1)
                bank = ring[k][:, :].rearrange("p (t d) -> p t d", t=ST)
                e.tensor_tensor(vl[:, n % 2], bank, f32(vh[:, n % 2]), ALU.subtract).then_inc(v_low, 1)
                e.wait_ge(v_low, it * 2 + n + 1)
                e.sem_inc(ring_free[k], 1)

            def low_probs(it, u):
                e.wait_ge(pt_high, it * UNITS + u + 1)
                e.tensor_tensor(ptl[:, :], pt[:, 0:(2 * ST - 1) * P], f32(pth[:, :]), ALU.subtract).then_inc(pt_low, 1)

            def low_out(it, u):
                e.wait_ge(o_high, it * UNITS + u + 1)
                slot = u // GRP, u % GRP
                e.tensor_tensor(ol[:, slot[0], slot[1]], obank[:, :], f32(oh[:, slot[0], slot[1]]), ALU.subtract)\
                    .then_inc(o_low, 1)

            def add_out(pair, it, u):
                n, half, d = quarter_of(it, u)
                here = xt[:, d, bass.ds((pair * 2 + half) * S, S)]
                e.wait_ge(w_full, n + 1)
                e.tensor_tensor(here, here, wbank[:, :], ALU.add).then_inc(w_free, 1)

            def before(pair):
                for half in range(2):
                    layernorm(pair * 2 + half, half, Chain(e, dve_step, pair * (6 + KVH * UNITS) + 3 * half))
                it = pair * KVH - 1
                for kind, n in FIRST:
                    if kind in "QK":
                        rope(it, kind, n)
                    if kind == "N":
                        low_values(it, n)
                find_max(it, UNITS)
                normalise(it, UNITS, Chain(e, dve_step, pair * (6 + KVH * UNITS) + 6))

            def body(pair, g, it, first, last):
                chain = Chain(e, dve_step, pair * (6 + KVH * UNITS) + 7 + g * UNITS)
                for u in range(UNITS):
                    more = not (last and u == UNITS - 1)
                    steps = prepare(u, last)
                    for kind, n in steps[:1]:
                        rope(it, kind, n)
                    low_probs(it, u)
                    if more:
                        find_max(it, u + 1)
                    if not (first and u < GRP):
                        add_out(pair, it, u)
                    for kind, n in steps[1:]:
                        if kind == "K":
                            rope(it, kind, n)
                    if more:
                        normalise(it, u + 1, chain)
                    low_out(it, u)
                    for kind, n in steps[1:]:
                        if kind == "N":
                            low_values(it, n)

            def after(pair, it):
                for u in range(GRP):
                    add_out(pair, it, u)

            groups(e, before, body, after)

        @block.scalar
        def _(e):
            def layernorm(b, half):
                e.wait_ge(ln_centred, b + 1)
                e.activation(sq[:, :, :], zf[:, :, :], ACT.Square).then_inc(ln_squared, 1)
                e.wait_ge(ln_vare, b + 1)
                e.activation(tmp[1][:, :], tmp[0][:, :], ACT.Ln).then_inc(act_step, 1)
                e.wait_ge(act_step, b + 1)
                e.activation(tmp[1][:, :], tmp[1][:, :], ACT.Exp, scale=-0.5).then_inc(ln_seed, 1)
                e.wait_ge(ln_z, b + 1)
                e.copy(yh[:, :, half * S:(half + 1) * S], zf[:, :, :]).then_inc(ln_yh, 1)

            def exps(it, n):
                e.wait_ge(bias_ready, it * UNITS + n + 1)
                for t in range(ST):
                    part = probs[:, n % 2, t, (P if t == 0 else 0):]
                    e.activation(part, part, ACT.Exp, bias=bias[:, n % 2, t:t + 1], scale=SM_SCALE,
                                 accum_out=total[:, n % 2, t:t + 1]).then_inc(exp_done, 1)

            def high_rope(it, kind, n):
                slot, r = rope_of(it, kind, n)
                e.wait_ge(roped, r)
                to = (qh if kind == "Q" else kh)[:, n % 2]
                e.copy(to, ra[:, slot]).then_inc(rope_high, 1)

            def keep_values(it, n):
                k, count = bank_of(it, "V", n)
                e.wait_ge(ring_full[k], count)
                e.copy(vt[:, :], ring[k][:, :]).then_inc(vt_ready, 1)
                e.wait_ge(vt_ready, it * 2 + n + 1)
                e.sem_inc(ring_free[k], 1)

            def high_values(it, n):
                k, count = bank_of(it, "N", n)
                e.wait_ge(ring_full[k], count)
                e.copy(vh[:, n % 2], ring[k][:, :].rearrange("p (t d) -> p t d", t=ST)).then_inc(v_high, 1)

            def split_wkv(it):
                e.wait_ge(raw_in["wkv"], 32 * it + 32)
                e.copy(wkvh[:, :], wkv_raw[:, :]).then_inc(w_high["wkv"], 1)

            def split_wq(it, i):
                if i % 2 == 0:
                    e.wait_ge(raw_in["wq"], 32 * it + 8 * i + 16)
                e.copy(wqh[:, :, head(i)], wq_raw[:, :, head(i % 2)]).then_inc(w_high["wq"], 1)

            def split_wo(it, d, first):
                if d == 0:
                    e.wait_ge(raw_in["wo"], 16 * it + 16)
                if not first:
                    e.wait_ge(w_full, quarter_of(it, d)[0] + 1)
                cols = slice(d * P, (d + 1) * P)
                e.copy(woh[:, :, cols], wo_raw[:, :, cols]).then_inc(w_high["wo"], 1)

            def before(pair):
                for half in range(2):
                    layernorm(pair * 2 + half, half)
                split_wkv(pair * KVH)
                for i in range(GRP):
                    split_wq(pair * KVH, i)
                it = pair * KVH - 1
                for kind, n in FIRST:
                    if kind in "QK":
                        high_rope(it, kind, n)
                    elif kind == "V":
                        keep_values(it, n)
                    else:
                        high_values(it, n)
                exps(it, UNITS)

            def body(pair, g, it, first, last):
                for u in range(UNITS):
                    e.wait_ge(pt_full, it * UNITS + u + 1)
                    e.copy(pth[:, :], pt[:, 0:(2 * ST - 1) * P]).then_inc(pt_high, 1)
                    steps = prepare(u, last)
                    for kind, n in steps[:1]:
                        high_rope(it, kind, n)
                    if not (last and u == UNITS - 1):
                        exps(it, u + 1)
                    for kind, n in steps[1:]:
                        if kind == "K":
                            high_rope(it, kind, n)
                        elif kind == "V":
                            keep_values(it, n)
                    if u < DT:
                        split_wo(it, u, first)
                    if u == 4 and not last:
                        split_wkv(it + 1)
                    e.wait_ge(o_full, it * UNITS + u + 1)
                    if u == 0:
                        e.wait_ge(w_full, it * UNITS - (0 if first else GRP))
                    e.copy(oh[:, u // GRP, u % GRP], obank[:, :]).then_inc(o_high, 1)
                    for kind, n in steps[1:]:
                        if kind == "N":
                            high_values(it, n)
                    if 3 <= u <= 6 and not last:
                        split_wq(it + 1, u - 3)

            groups(e, before, body)

        @block.gpsimd
        def _(e):
            def rope(it, kind, n):
                slot, r = rope_of(it, kind, n)
                k, count = bank_of(it, kind, n)
                e.wait_ge(ring_free[k], count)
                e.tensor_tensor(ra[:, slot], ra[:, slot], rb[:, slot], ALU.add).then_inc(roped, 1)
                e.wait_ge(rope_high, r)
                hi, lo = [x[:, n % 2] for x in ((qh, ql) if kind == "Q" else (kh, kl))]
                e.tensor_tensor(lo, ra[:, slot], f32(hi), ALU.subtract).then_inc(rope_low, 1)

            def split(name, it, lo, raw, hi):
                e.wait_ge(w_high[name], it + 1)
                e.tensor_tensor(lo, raw, f32(hi), ALU.subtract).then_inc(w_low[name], 1)

            def split_wq(it, i):
                split("wq", it * GRP + i, wql[:, :, head(i)], wq_raw[:, :, head(i % 2)], wqh[:, :, head(i)])

            def before(pair):
                split("wkv", pair * KVH, wkvl[:, :], wkv_raw[:, :], wkvh[:, :])
                for i in range(GRP):
                    split_wq(pair * KVH, i)
                for kind, n in FIRST:
                    if kind in "QK":
                        rope(pair * KVH - 1, kind, n)

            def body(pair, g, it, first, last):
                for u in range(UNITS):
                    for kind, n in prepare(u, last):
                        if kind in "QK":
                            rope(it, kind, n)
                    if u < DT:
                        cols = slice(u * P, (u + 1) * P)
                        split("wo", it * DT + u, wol[:, :, cols], wo_raw[:, :, cols], woh[:, :, cols])
                    if u == 4 and not last:
                        split("wkv", it + 1, wkvl[:, :], wkv_raw[:, :], wkvh[:, :])
                    if 3 <= u <= 6 and not last:
                        split_wq(it + 1, u - 3)

            e.sem_inc(rope_low, 2)
            groups(e, before, body)


def rounded(x):
    bits = x.astype(np.float32).view(np.int32)
    return ((bits + 0x7FF + ((bits >> 12) & 1)) & ~0xFFF).view(np.float32)


def alibi_rows():
    slope = ((2.0 ** -0.25) ** np.arange(1, AH + 1, dtype=np.float64)).astype(np.float32).reshape(2, PAIRS, 1)
    pos = np.arange(S, dtype=np.float32)
    high = rounded(slope)
    low = slope - high
    q = np.zeros((2, 16, PAIRS, S), np.float32)
    q[:, 0], q[:, 3] = high, low
    for row, part in ((1, -high * pos), (4, -low * pos)):
        q[:, row] = rounded(part)
        q[:, row + 1] = rounded(part - q[:, row])
    k = np.zeros((2, P, S), np.float32)
    for half in range(2):
        r = 64 * half + R_BIAS
        k[half, r], k[half, r + 3] = pos, pos
        k[half, [r + 1, r + 2, r + 4, r + 5, r + 6, r + 7]] = 1.0
    return q, k


def constants():
    eye = np.eye(P, dtype=np.float32)
    rank = np.broadcast_to(np.arange(SPARSE, 0, -1, dtype=np.float32), (P, SPARSE))
    inv_freq = np.float32(10000.0) ** (-np.arange(HALF, dtype=np.float32) / np.float32(HALF))
    angle = inv_freq[:, None] * np.arange(S, dtype=np.float32)[None, :]
    cos, sin = np.cos(angle), np.sin(angle)
    q, k = np.arange(P)[:, None], np.arange(P)[None, :]
    window = np.where(np.concatenate([k > q, k <= q], axis=1), 0.0, -1.0e30).astype(np.float32)
    after = np.where(k > q, -1.0e30, 0.0).astype(np.float32)
    q_rows, k_rows = alibi_rows()
    return {"q_rows": q_rows, "k_rows": k_rows, "after": after, "before": np.tile(after.T, (1, 4)),
            "cos": np.concatenate([cos, cos]), "sin": np.concatenate([sin, -sin]), "window": window, "eye": eye, "ones": np.full((P, P), 1.0 / D, np.float32), "rank": np.ascontiguousarray(rank)}


def load_constants(nc, st, ins):
    sb, sem = sb_in(nc, st), sem_in(nc)
    ident, ones, rank = sb("ident", [P, P]), sb("ones", [P, P]), sb("rank", [P, SPARSE])
    identb, rankb = sb("identb", [P, P], BF16), sb("rankb", [P, SPARSE], BF16)
    landed = sem("constants_landed")
    with nc.Block() as block:
        @block.sync
        def _(e):
            for to, name in ((ident, "eye"), (ones, "ones"), (rank, "rank")):
                e.dma_start(to[:, :], ins[name]).then_inc(landed, 16)

        @block.vector
        def _(e):
            e.wait_ge(landed, 48)
            e.tensor_copy(identb[:, :], ident[:, :])
            e.tensor_copy(rankb[:, :], rank[:, :])
    return ident, identb, ones, rankb


def load_tables(nc, st, ins):
    sb, sem = sb_in(nc, st), sem_in(nc)
    cos, sin, window = sb("cos_table", [P, S]), sb("sin_table", [P, S]), sb("window_mask", [P, 2 * P])
    landed = sem("tables_landed")
    with nc.Block() as block:
        @block.sync
        def _(e):
            for to, name in ((cos, "cos"), (sin, "sin"), (window, "window")):
                e.dma_start(to[:, :], ins[name]).then_inc(landed, 16)
            e.wait_ge(landed, 48)
    return cos, sin, window


def load_causal_masks(nc, st, ins):
    below, above = sb_in(nc, st)("below_mask", [P, P], BF16), sb_in(nc, st)("above_mask", [P, 4 * P], BF16)
    with ExitStack() as early:
        sb, landed = sb_in(nc, early), sem_in(nc)("causal_masks_landed")
        below_raw, above_raw = sb("below_raw", [P, P]), sb("above_raw", [P, 4 * P])
        with nc.Block() as block:
            @block.sync
            def _(e):
                e.dma_start(below_raw[:, :], ins["after"]).then_inc(landed, 16)
                e.dma_start(above_raw[:, :], ins["before"]).then_inc(landed, 16)

            @block.vector
            def _(e):
                e.wait_ge(landed, 32)
                e.tensor_copy(below[:, :], below_raw[:, :])
                e.tensor_copy(above[:, :], above_raw[:, :])
    return below, above


def program(nc, ins, out, stages=("a", "f1", "b", "f2")):
    with ExitStack() as st:
        consts = load_constants(nc, st, ins)
        xt = st.enter_context(nc.sbuf_tensor("xt", [P, DT, TOK], F32))
        ffn_w = [ins[f"L0_ffn_{n}"] for n in ("c1_w", "c2_w", "w1", "w2t")]
        with nc.cleanup_on_exit():
            load_x(nc, ins["L0_attn_a_hidden_states"], xt, consts[0])
        if "a" in stages:
            with nc.cleanup_on_exit(), ExitStack() as tables_st:
                below, above = load_causal_masks(nc, tables_st, ins)
                causal_attention(nc, [ins[f"L0_attn_a_{n}"] for n in ("Wqkv", "Wo")], xt, consts,
                                 (below, above, ins["q_rows"], ins["k_rows"]))
        if "f1" in stages:
            with nc.cleanup_on_exit():
                ffn(nc, "f1_", ffn_w, xt, consts)
        if "b" in stages:
            with nc.cleanup_on_exit(), ExitStack() as tables_st:
                window_attention(nc, [ins[f"L0_attn_b_{n}"] for n in ("wq", "wk", "wv", "wo")], xt, consts,
                                 load_tables(nc, tables_st, ins))
        if "f2" in stages:
            with nc.cleanup_on_exit():
                ffn(nc, "f2_", ffn_w, xt, consts)
        with nc.cleanup_on_exit():
            store_x(nc, out, xt, consts[0])


_INS = ["L0_attn_a_hidden_states", "L0_attn_a_Wqkv", "L0_attn_a_Wo", "L0_attn_b_wq", "L0_attn_b_wk",
        "L0_attn_b_wv", "L0_attn_b_wo", "L0_ffn_c1_w", "L0_ffn_c2_w", "L0_ffn_w1", "L0_ffn_w2t"]


def kernel(**inputs):
    import concourse.bacc as _bacc
    from concourse.bass_utils import run_bass_kernel_spmd as _run

    nc = _bacc.Bacc("TRN2", target_bir_lowering=False, num_devices=1)
    arrays, aps = {}, {}
    for name, a in [(n, inputs[n]) for n in _INS] + list(constants().items()):
        a = np.ascontiguousarray(a)
        arrays[f"in_{name}"] = a
        aps[name] = nc.dram_tensor(f"in_{name}", a.shape, mybir.dt.from_np(a.dtype), kind="ExternalInput").ap()
    out = nc.dram_tensor("out", (NB, S, D), F32, kind="ExternalOutput").ap()
    program(nc, aps, out)
    r = _run(nc, [arrays], core_ids=[0])
    return r.results[0]["out"]
```

```python
from contextlib import ExitStack

import concourse.bass as bass
import numpy as np
from concourse import mybir

F32 = mybir.dt.float32
F32R = mybir.dt.float32r
BF16 = mybir.dt.bfloat16
ALU = mybir.AluOpType
ACT = mybir.ActivationFunctionType
AX = mybir.AxisListType

P = 128
NB, S, D = 4, 512, 512
DT = D // P
ST = S // P
TOK = NB * S
LN_EPS = 1e-5

INTER, SPARSE, RANK = 1792, 32, 16
IT = INTER // P
CH = 256
NCH = INTER // CH
CBLK = 2 * CH // SPARSE
CROWS = 96


def f32(ap):
    return ap.bitcast(F32)


def sb_in(nc, stack):
    return lambda name, shape, dt=F32: stack.enter_context(nc.sbuf_tensor(name, shape, dt))


def ps_in(nc, stack):
    return lambda name, shape, dt=F32: stack.enter_context(nc.psum_tensor(name, shape, dt))


def sem_in(nc, tag=""):
    return lambda name: nc.alloc_semaphore(name=tag + name)


def load_x(nc, ins, x, xt, consts):
    ident, identb, ones, rankb = consts
    with ExitStack() as st:
        sb, ps, sem = sb_in(nc, st), ps_in(nc, st), sem_in(nc)
        rows, rank = sb("x_rows", [P, NB, ST, D]), sb("rank", [P, SPARSE])
        pt = [ps(f"x_turned{i}", [P, DT, P]) for i in range(8)]
        landed = [sem(f"x_landed{b}") for b in range(NB)]
        eye_in, rest_in = sem("eye_landed"), sem("ones_and_rank_landed")
        turned = sem("x_tile_turned")
        kept = [sem("x_kept_even"), sem("x_kept_odd")]
        xv = x.rearrange("b (t p) d -> b p t d", p=P)
        block = st.enter_context(nc.Block())

        @block.sync
        def _(e):
            e.dma_start(ident[:, :], ins["eye"]).then_inc(eye_in, 16)
            for b in range(NB):
                e.dma_start(rows[:, b], xv[b]).then_inc(landed[b], 16)
            for to, name in ((ones, "ones"), (rank, "rank")):
                e.dma_start(to[:, :], ins[name]).then_inc(rest_in, 16)

        @block.tensor
        def _(e):
            e.wait_ge(eye_in, 16)
            for n in range(NB * ST):
                b, t = divmod(n, ST)
                if t == 0:
                    e.wait_ge(landed[b], 16)
                if n >= 8:
                    e.wait_ge(kept[n % 2], n // 2 - 3)
                for d in range(DT):
                    mm = e.transpose(pt[n % 8][:, d], rows[:, b, t, d * P:(d + 1) * P], ident[:, :])
                mm.then_inc(turned, 1)

        def keep(e, n, op):
            e.wait_ge(turned, n + 1)
            op(xt[:, :, n * P:(n + 1) * P], pt[n % 8][:, :, :]).then_inc(kept[n % 2], 1)

        @block.vector
        def _(e):
            e.wait_ge(eye_in, 16)
            e.tensor_copy(identb[:, :], ident[:, :])
            for n in range(0, NB * ST, 2):
                keep(e, n, e.tensor_copy)
            e.wait_ge(rest_in, 32)
            e.tensor_copy(rankb[:, :], rank[:, :])

        @block.scalar
        def _(e):
            for n in range(1, NB * ST, 2):
                keep(e, n, e.copy)


def store_x(nc, out, xt, ident):
    with ExitStack() as st:
        sb, ps, sem = sb_in(nc, st), ps_in(nc, st), sem_in(nc)
        rows = sb("out_rows", [P, NB * ST, D])
        pt = [ps(f"out_turned{i}", [P, D]) for i in range(8)]
        turned = sem("out_tile_turned")
        kept = [sem("out_kept_even"), sem("out_kept_odd")]
        stored = sem("out_stored")
        ov = out.rearrange("b (t p) d -> p (b t) d", p=P)
        block = st.enter_context(nc.Block())

        @block.tensor
        def _(e):
            for n in range(NB * ST):
                if n >= 8:
                    e.wait_ge(kept[n % 2], n // 2 - 3)
                for d in range(DT):
                    mm = e.transpose(pt[n % 8][:, d * P:(d + 1) * P], xt[:, d, n * P:(n + 1) * P], ident[:, :])
                mm.then_inc(turned, 1)

        def keep(e, n, op):
            e.wait_ge(turned, n + 1)
            op(rows[:, n], pt[n % 8][:, :]).then_inc(kept[n % 2], 1)

        @block.vector
        def _(e):
            for n in range(0, NB * ST, 2):
                keep(e, n, e.tensor_copy)

        @block.scalar
        def _(e):
            for n in range(1, NB * ST, 2):
                keep(e, n, e.copy)

        @block.sync
        def _(e):
            for n in range(0, NB * ST, 2):
                e.wait_ge(kept[0], n // 2 + 1)
                e.wait_ge(kept[1], n // 2 + 1)
                e.dma_start(ov[:, n:n + 2], rows[:, n:n + 2]).then_inc(stored, 16)
            e.wait_ge(stored, 16 * NB * ST // 2)


class Chain:

    def __init__(self, e, sem, before=0):
        self.e, self.sem, self.before, self.n = e, sem, before, 0

    def __call__(self, instruction):
        self.n += 1
        instruction.then_inc(self.sem, 1)
        self.e.wait_ge(self.sem, self.before + self.n)


def ffn(nc, tag, drams, xt, consts):
    c1_w, c2_w, w1, w2t = drams
    ident, identb, ones, rev = consts
    with ExitStack() as st:
        sb, ps, sem = sb_in(nc, st), ps_in(nc, st), sem_in(nc)
        with ExitStack() as early:
            w1_raw, w2_raw = sb_in(nc, early)(f"{tag}w1_raw", [P, DT, INTER]), sb_in(nc, early)(f"{tag}w2_raw", [P, IT, D])
        w1l, w2l = sb(f"{tag}w1_low", [P, DT, INTER], F32R), sb(f"{tag}w2_low", [P, IT, D], F32R)
        w1h, w2h = sb(f"{tag}w1_high", [P, DT, INTER], F32R), sb(f"{tag}w2_high", [P, IT, D], F32R)
        c1h, c1l = (sb(f"{tag}c1_{x}", [P, DT, CROWS], F32R) for x in ("high", "low"))
        c2s = sb(f"{tag}c2_stacked", [CROWS, INTER], F32R)
        zh, zl = (sb(f"{tag}z_{x}", [P, DT, S], F32R) for x in ("high", "low"))
        zf = sb(f"{tag}z", [P, DT, S])
        tmp = [sb(f"{tag}ln_tmp{i}", [P, S]) for i in range(3)]
        ts = sb(f"{tag}t_stacked", [CROWS, S], F32R)
        eq = sb(f"{tag}is_max", [P, CBLK, SPARSE], BF16)
        mx = sb(f"{tag}block_max", [P, CBLK])
        first = sb(f"{tag}first_max", [P, CBLK], BF16)
        mask = sb(f"{tag}mask", [P, 2, ST, CH], BF16)
        mts = sb(f"{tag}mask_turned", [P, 2, 2, S], BF16)
        hm = sb(f"{tag}hidden", [P, S])
        with ExitStack() as early:
            c2_raw = [sb_in(nc, early)(f"{tag}c2_raw{i}", [P, 2 * S]) for i in range(2)]
        hh, hl = (sb(f"{tag}hidden_{x}", [P, 2, S], F32R) for x in ("high", "low"))
        acc = ps(f"{tag}acc", [P, DT, S])
        hp = [ps(f"{tag}hidden_sum{i}", [P, S]) for i in range(2)]
        aux = [ps(f"{tag}aux{i}", [P, S]) for i in range(2)]
        HALF_IT = IT // 2
        c1r = hm[0:CROWS, :]
        c2r = [x[:, 0:HALF_IT * CROWS].rearrange("p (t r) -> p t r", t=HALF_IT) for x in c2_raw]
        banks = [acc[:, d] for d in range(DT)] + [x[:, :] for x in hp]
        groups = [(g, min(4, IT - g)) for g in range(0, IT, 4)]
        jobs = [("c1", 0, 0, DT)] + [("c2", 0, g, n) for g, n in groups] + \
               [("w1", d, g, n) for g, n in groups for d in range(DT)]
        ROUTER = range(1 + len(groups))
        W1 = [range(ROUTER.stop + DT * i, ROUTER.stop + DT * (i + 1)) for i in range(len(groups))]

        def places(j):
            (what, d, g, n), b = jobs[j], banks[j % len(banks)]
            cols = slice(g * P, (g + n) * P)
            if what == "c1":
                src = b[:, 0:DT * CROWS].rearrange("p (k r) -> p k r", k=DT)
                return src, c1h[:, :, :], src, c1l[:, :, :], c1h[:, :, :]
            if what == "c2":
                rest = c2s[64:CROWS, cols]
                return b[0:CROWS, 0:n * P], c2s[:, cols], b[64:CROWS, 0:n * P], rest, rest
            return b[:, 0:n * P], w1h[:, d, cols], b[:, 0:n * P], w1l[:, d, cols], w1h[:, d, cols]

        cleared, c_in = sem(f"{tag}c_rows_cleared"), sem(f"{tag}c_landed")
        w1_in = [sem(f"{tag}w1_landed{i}") for i in range(len(groups))]
        w2_in = [sem(f"{tag}w2_landed{i}") for i in range(NCH)]
        turned, w_high, w_low = (sem(f"{tag}weights_{x}") for x in ("turned", "high_ready", "low_ready"))
        w2_high, w2_low = sem(f"{tag}w2_high_ready"), sem(f"{tag}w2_low_ready")
        aux_full = [sem(f"{tag}aux_full{i}") for i in range(2)]
        aux_free = [sem(f"{tag}aux_free{i}") for i in range(2)]
        t_high = sem(f"{tag}t_high_written")
        dve_step, pool_step, act_step = sem(f"{tag}dve_step"), sem(f"{tag}pool_step"), sem(f"{tag}act_step")
        mask_ready = sem(f"{tag}mask_half_ready")
        h_full, h_masked = sem(f"{tag}hidden_sum_full"), sem(f"{tag}hidden_masked")
        hh_ready, hl_ready = sem(f"{tag}hidden_high_ready"), sem(f"{tag}hidden_low_ready")
        h_used, acc_added = sem(f"{tag}hidden_used"), sem(f"{tag}acc_added")
        x_summed, sq_ready, sq_added = sem(f"{tag}x_summed"), sem(f"{tag}square_ready"), sem(f"{tag}square_added")
        y0_ready, z_ready = sem(f"{tag}rsqrt_seed_ready"), sem(f"{tag}z_ready")
        zh_ready, zl_ready = sem(f"{tag}z_high_ready"), sem(f"{tag}z_low_ready")

        order = [("I", 0), ("I", 1)]
        for c in range(NCH):
            order += [("M", c)] + ([("I", 2 * c + 2), ("I", 2 * c + 3)] if c + 1 < NCH else [])
            order += [("mean", 0)] * (c == 1) + [("var", 0)] * (c == 4)
        order += [("T", 0)]
        BEFORE = ["mean", "var", "T"]
        HALF = len(order) // 2
        assert len(order) % 2 == 0

        def use(it, what, i=0):
            n = BEFORE.index(what) if it is None else order.index((what, i)) + len(BEFORE)
            return n % 2, (0 if it is None else it * HALF) + n // 2 + 1

        def aux_write(e, it, what, i=0):
            k, n = use(it, what, i)
            if not isinstance(n, int) or n > 1:
                e.wait_ge(aux_free[k], n - 1)
            return aux[k], aux_full[k]

        def aux_read(e, it, what, i=0):
            k, n = use(it, what, i)
            e.wait_ge(aux_full[k], n)
            return aux[k], aux_free[k]

        def aux_done(e, it, what, i=0):
            k, n = use(it, what, i)
            e.wait_ge(aux_free[k], n)

        def first_batch(it):
            return isinstance(it, int) and it == 0

        def of_ln(it, per):
            return 0 if it is None else (it + 1) * per

        def batch_after(it):
            return 0 if it is None else (it + 1) % NB

        def loop(e, body):
            body(0, True)
            with e.Fori(1, NB) as it:
                body(it, False)

        block = st.enter_context(nc.Block())

        @block.sync
        def _(e):
            e.wait_ge(cleared, 3)
            for r in range(CROWS // 32):
                rows = slice(32 * r, 32 * r + RANK)
                e.dma_start(c1r[rows, :], c1_w).then_inc(c_in, 16)
                for half in range(2):
                    e.dma_start(c2r[half][:, :, rows], c2_w.rearrange("(h t p) r -> h p t r", h=2, p=P)[half])\
                        .then_inc(c_in, 16)
            w1v = w1.rearrange("(t p) (d k) -> t p d k", p=P, k=P)
            for i, (g, n) in enumerate(groups):
                for t in range(g, g + n):
                    e.dma_start(w1_raw[:, :, t * P:(t + 1) * P], w1v[t]).then_inc(w1_in[i], 16)
            w2v = w2t.rearrange("(t p) d -> p t d", p=P)
            for i in range(NCH):
                e.dma_start(w2_raw[:, 2 * i:2 * i + 2], w2v[:, 2 * i:2 * i + 2]).then_inc(w2_in[i], 16)

        @block.tensor
        def _(e):
            def turn_weights(which):
                for j in which:
                    what, d, g, n = jobs[j]
                    if j == 0:
                        e.wait_ge(c_in, 16 * CROWS // 32 * 3)
                    if what == "w1" and d == 0:
                        e.wait_ge(w1_in[g // 4], 16 * n)
                    if j >= len(banks):
                        e.wait_ge(w_low, j - len(banks) + 1)
                    b = banks[j % len(banks)]
                    for k in range(n):
                        t = g + k
                        if what == "c1":
                            mm = e.transpose(b[:, k * CROWS:(k + 1) * CROWS], c1r[:, k * P:(k + 1) * P],
                                             ident[0:CROWS, 0:CROWS])
                        elif what == "c2":
                            mm = e.transpose(b[0:CROWS, k * P:(k + 1) * P], c2r[t // HALF_IT][:, t % HALF_IT, :],
                                             ident[:, :])
                        else:
                            mm = e.transpose(b[:, k * P:(k + 1) * P], w1_raw[:, d, t * P:(t + 1) * P], ident[:, :])
                    mm.then_inc(turned, 1)

            def mean(it):
                bank, full = aux_write(e, it, "mean")
                e.wait_ge(x_summed, of_ln(it, 1) + 1)
                e.matmul(bank[:, :], ones[:, :], tmp[2][:, :], start=True, stop=True).then_inc(full, 1)

            def var(it):
                bank, full = aux_write(e, it, "var")
                e.wait_ge(sq_added, of_ln(it, 3) + 3)
                e.matmul(bank[:, :], ones[:, :], tmp[2][:, :], start=True, stop=True).then_inc(full, 1)

            def router_first(it):
                e.wait_ge(zh_ready, of_ln(it, DT) + DT)
                e.wait_ge(zl_ready, of_ln(it, DT) + DT)
                bank, full = aux_write(e, it, "T")
                for n, (w, z) in enumerate([(c1h, zh), (c1h, zl), (c1l, zh)]):
                    for d in range(DT):
                        mm = e.matmul(bank[0:CROWS, :], w[:, d, :], z[:, d, :],
                                      start=n == 0 and d == 0, stop=n == 2 and d == DT - 1)
                mm.then_inc(full, 1)

            def router_scores(it, c, halves=(0, 1)):
                if c == 0:
                    aux_done(e, None if first_batch(it) else it - 1, "T")
                for half in halves:
                    bank, full = aux_write(e, it, "I", 2 * c + half)
                    for k in range(2):
                        t = 2 * half + k
                        mm = e.matmul(bank[:, k * CH:(k + 1) * CH], ts[:, t * P:(t + 1) * P],
                                      c2s[:, c * CH:(c + 1) * CH], start=True, stop=True)
                    mm.then_inc(full, 1)

            def turn_masks(it, c):
                e.wait_ge(mask_ready, it * 2 * NCH + 2 * c + 2)
                bank, full = aux_write(e, it, "M", c)
                turned = bank[:, :].bitcast(BF16).rearrange("p (j t) -> p j t", j=2)
                for j in range(2):
                    for t in range(ST):
                        mm = e.transpose(turned[:, j, t * P:(t + 1) * P],
                                         mask[:, c % 2, t, j * P:(j + 1) * P], identb[:, :])
                mm.then_inc(full, 1)

            def up(it, j):
                e.wait_ge(h_masked, it * IT + j + 1)
                for d in range(DT):
                    for n, (w, z) in enumerate([(w1h, zh), (w1h, zl), (w1l, zh)]):
                        mm = e.matmul(hp[j % 2][:, :], w[:, d, j * P:(j + 1) * P], z[:, d, :],
                                      start=d == 0 and n == 0, stop=d == DT - 1 and n == 2)
                mm.then_inc(h_full, 1)

            def down(it, j):
                if j == 0 and not first_batch(it):
                    e.wait_ge(acc_added, it)
                e.wait_ge(hh_ready, it * IT + j + 1)
                e.wait_ge(hl_ready, it * IT + j + 1)
                if first_batch(it):
                    e.wait_ge(w2_low, j // 2 + 1)
                for d in range(DT):
                    for n, (w, h) in enumerate([(w2h, hh), (w2h, hl), (w2l, hh)]):
                        mm = e.matmul(acc[:, d, :], w[:, j, d * P:(d + 1) * P], h[:, j % 2, :],
                                      start=j == 0 and n == 0, stop=j == IT - 1 and n == 2)
                mm.then_inc(h_used, 1)

            def body(it, first):
                router_scores(it, 0)
                for c in range(NCH):
                    up(it, 2 * c)
                    if c == 0:
                        up(it, 1)
                    else:
                        if c == 1:
                            router_scores(it, 1, [1])
                        down(it, 2 * c - 2)
                    turn_masks(it, c)
                    if c + 1 < NCH:
                        router_scores(it, c + 1, [0])
                    if c:
                        up(it, 2 * c + 1)
                        if c + 1 < NCH:
                            router_scores(it, c + 1, [1])
                        down(it, 2 * c - 1)
                    if c == 1:
                        mean(it)
                    if c == 4:
                        var(it)
                down(it, IT - 2)
                router_first(it)
                down(it, IT - 1)

            e.sem_inc(h_used, 2)
            mean(None)
            turn_weights(ROUTER)
            var(None)
            for i in range(3):
                turn_weights(W1[i])
            router_first(None)
            turn_weights(W1[3])
            e.wait_ge(w_low, len(jobs))
            loop(e, body)

        @block.vector
        def _(e):
            def centre(it):
                bank, free = aux_read(e, it, "mean")
                e.tensor_tensor(zf[:, :, :], xt[:, :, bass.ts(batch_after(it), S)],
                                bank[:, :].unsqueeze(1).broadcast_to([P, DT, S]), ALU.subtract).then_inc(free, 1)

            def variance(it):
                bank, free = aux_read(e, it, "var")
                e.tensor_scalar(tmp[0][:, :], bank[:, :], LN_EPS, None, ALU.add).then_inc(free, 1)

            def normalise(it, chain):
                e.wait_ge(y0_ready, of_ln(it, 1) + 1)
                chain(e.scalar_tensor_tensor(tmp[2][:, :], tmp[0][:, :], -0.5, tmp[1][:, :], ALU.mult, ALU.mult))
                chain(e.tensor_tensor(tmp[2][:, :], tmp[2][:, :], tmp[1][:, :], ALU.mult))
                chain(e.scalar_tensor_tensor(tmp[0][:, :], tmp[2][:, :], 1.5, tmp[1][:, :], ALU.add, ALU.mult))
                e.tensor_tensor(zf[:, :, :], zf[:, :, :], tmp[0][:, :].unsqueeze(1).broadcast_to([P, DT, S]),
                                ALU.mult).then_inc(z_ready, 1)

            def low_z(it):
                for d in range(DT):
                    e.wait_ge(zh_ready, of_ln(it, DT) + d + 1)
                    e.tensor_tensor(zl[:, d], zf[:, d], f32(zh[:, d]), ALU.subtract).then_inc(zl_ready, 1)

            def stack_t(it):
                e.wait_ge(t_high, of_ln(it, 1) + 1)
                bank, free = aux_read(e, it, "T")
                e.tensor_tensor(ts[32:64, :], bank[32:64, :], f32(ts[32:64, :]), ALU.subtract).then_inc(free, 1)

            def find_max(it, c, half, chain):
                bank, free = aux_read(e, it, "I", 2 * c + half)
                scores = bank[:, :].rearrange("p (g k) -> p g k", k=SPARSE)
                chain(e.tensor_reduce(mx[:, :], scores, AX.X, ALU.max))
                e.tensor_tensor(eq[:, :, :], scores, mx[:, :].unsqueeze(2).broadcast_to([P, CBLK, SPARSE]),
                                ALU.is_equal).then_inc(free, 1)
                aux_done(e, it, "I", 2 * c + half)
                chain(e.tensor_tensor(eq[:, :, :], eq[:, :, :],
                                      rev[:, :].unsqueeze(1).broadcast_to([P, CBLK, SPARSE]), ALU.mult))
                chain(e.tensor_reduce(first[:, :], eq[:, :, :], AX.X, ALU.max))
                if c >= 2:
                    k, n = use(it, "M", c - 2)
                    e.wait_ge(aux_full[k], n)
                out = mask[:, c % 2, 2 * half:2 * half + 2, :].rearrange("p t (g k) -> p (t g) k", k=SPARSE)
                e.tensor_tensor(out, eq[:, :, :], first[:, :].unsqueeze(2).broadcast_to([P, CBLK, SPARSE]),
                                ALU.is_equal).then_inc(mask_ready, 1)

            def keep_hidden(it, j):
                aux_done(e, it, "M", j // 2)
                e.wait_ge(h_full, it * IT + j + 1)
                e.wait_ge(hl_ready, it * IT + j)
                e.scalar_tensor_tensor(hm[:, :], hp[j % 2][:, :], 0.0, mts[:, j // 2 % 2, j % 2, :],
                                       ALU.max, ALU.mult).then_inc(h_masked, 1)

            def add_out(it):
                e.wait_ge(h_used, it * IT + IT + 2)
                here = xt[:, :, bass.ts(it, S)]
                e.tensor_tensor(here, here, acc[:, :, :], ALU.add).then_inc(acc_added, 1)

            def body(it, first):
                chain = Chain(e, dve_step, it * (3 * 2 * NCH + 3) + 3)
                find_max(it, 0, 0, chain)
                find_max(it, 0, 1, chain)
                if not first:
                    add_out(it - 1)
                for c in range(NCH):
                    if c == 2:
                        centre(it)
                    if c == 5:
                        variance(it)
                    for half in range(2):
                        keep_hidden(it, 2 * c + half)
                        if c + 1 < NCH:
                            find_max(it, c + 1, half, chain)
                    if c == 5:
                        normalise(it, chain)
                low_z(it)
                stack_t(it)

            def low_weights(which):
                for j in which:
                    _, _, src, lo, hi = places(j)
                    e.wait_ge(w_high, j + 1)
                    e.tensor_tensor(lo, src, f32(hi), ALU.subtract).then_inc(w_low, 1)

            e.sem_inc(h_masked, 2)
            e.memset(c1r, 0.0).then_inc(cleared, 1)
            for x in c2r:
                e.memset(x, 0.0).then_inc(cleared, 1)
            centre(None)
            low_weights(ROUTER)
            variance(None)
            low_weights(W1[0])
            normalise(None, Chain(e, dve_step))
            low_weights(W1[1])
            low_z(None)
            low_weights(W1[2])
            low_weights(W1[3])
            stack_t(None)
            loop(e, body)
            add_out(NB - 1)

        @block.scalar
        def _(e):
            def square(it, d):
                if d == 0:
                    aux_done(e, it, "mean")
                if d == 2:
                    e.wait_ge(sq_added, of_ln(it, 3) + 1)
                if d == 3:
                    e.wait_ge(sq_added, of_ln(it, 3) + 1)
                e.activation(tmp[d % 2][:, :], zf[:, d], ACT.Square).then_inc(sq_ready, 1)

            def seed(it):
                k, n = use(it, "var")
                aux_done(e, it, "var")
                e.activation(tmp[1][:, :], tmp[0][:, :], ACT.Ln).then_inc(act_step, 1)
                e.wait_ge(act_step, of_ln(it, 1) + 1)
                e.activation(tmp[1][:, :], tmp[1][:, :], ACT.Exp, scale=-0.5).then_inc(y0_ready, 1)

            def high_z(it):
                e.wait_ge(z_ready, of_ln(it, 1) + 1)
                if it is not None:
                    e.wait_ge(h_full, it * IT + IT)
                for d in range(DT):
                    e.copy(zh[:, d], zf[:, d]).then_inc(zh_ready, 1)

            def high_w2(i):
                e.wait_ge(w2_in[i], 16)
                e.copy(w2h[:, 2 * i:2 * i + 2], w2_raw[:, 2 * i:2 * i + 2]).then_inc(w2_high, 1)

            def high_t(it):
                bank, _ = aux_read(e, it, "T")
                e.copy(ts[:, :], bank[0:CROWS, :]).then_inc(t_high, 1)

            def body(it, first):
                for c in range(NCH):
                    e.wait_ge(h_masked, it * IT + max(2 * c, 0))
                    bank, free = aux_read(e, it, "M", c)
                    e.copy(mts[:, c % 2], bank[:, :].bitcast(BF16).rearrange("p (j t) -> p j t", j=2))\
                        .then_inc(free, 1)
                    for j in (2 * c, 2 * c + 1):
                        e.wait_ge(h_masked, it * IT + j + 3)
                        e.wait_ge(h_used, it * IT + j + 1)
                        e.copy(hh[:, j % 2], hm[:, :]).then_inc(hh_ready, 1)
                    if first and c + 1 < NCH:
                        high_w2(c + 1)
                    if c == 2:
                        square(it, 0)
                        square(it, 1)
                    if c == 3:
                        square(it, 2)
                        square(it, 3)
                    if c == 5:
                        seed(it)
                high_z(it)
                high_t(it)

            def high_weights(which):
                for j in which:
                    src, hi, _, _, _ = places(j)
                    e.wait_ge(turned, j + 1)
                    e.copy(hi, src).then_inc(w_high, 1)

            for d in range(DT):
                square(None, d)
            high_weights(ROUTER)
            seed(None)
            high_weights(W1[0])
            high_weights(W1[1])
            high_z(None)
            high_weights(W1[2])
            high_weights(W1[3])
            high_t(None)
            high_w2(0)
            loop(e, body)

        @block.gpsimd
        def _(e):
            def sum_x(it, chain):
                if it is not None:
                    e.wait_ge(z_ready, it + 1)
                    if not first_batch(it):
                        e.wait_ge(acc_added, it - 1)
                here = xt[:, :, bass.ts(batch_after(it), S)]
                chain(e.tensor_tensor(tmp[2][:, :], here[:, 0], here[:, 1], ALU.add))
                chain(e.tensor_tensor(tmp[2][:, :], tmp[2][:, :], here[:, 2], ALU.add))
                e.tensor_tensor(tmp[2][:, :], tmp[2][:, :], here[:, 3], ALU.add).then_inc(x_summed, 1)

            def sum_squares(it, n):
                e.wait_ge(sq_ready, of_ln(it, DT) + n + 2)
                if n:
                    e.wait_ge(sq_added, of_ln(it, 3) + n)
                e.tensor_tensor(tmp[2][:, :], tmp[0][:, :] if n == 0 else tmp[2][:, :], tmp[(n + 1) % 2][:, :],
                                ALU.add).then_inc(sq_added, 1)

            def low_hidden(it, j):
                e.wait_ge(hh_ready, it * IT + j + 1)
                e.tensor_tensor(hl[:, j % 2], hm[:, :], f32(hh[:, j % 2]), ALU.subtract).then_inc(hl_ready, 1)

            def body(it, first):
                sum_x(it, Chain(e, pool_step, it * 2 + 2))
                for c in range(NCH):
                    low_hidden(it, 2 * c)
                    low_hidden(it, 2 * c + 1)
                    if first and c + 1 < NCH:
                        low_w2(c + 1)
                    if c == 2:
                        sum_squares(it, 0)
                    if c == 3:
                        sum_squares(it, 1)
                        sum_squares(it, 2)

            def low_w2(i):
                e.wait_ge(w2_high, i + 1)
                two = slice(2 * i, 2 * i + 2)
                e.tensor_tensor(w2l[:, two], w2_raw[:, two], f32(w2h[:, two]), ALU.subtract).then_inc(w2_low, 1)

            sum_x(None, Chain(e, pool_step))
            for n in range(3):
                sum_squares(None, n)
            low_w2(0)
            loop(e, body)


AH, AD = 32, 16
PAIRS = AH // 2
HG = AH // 4
KV = 48
VROWS = 80
R_QHI, R_QLO, R_BIAS, R_MAX, R_QHI2, R_ZERO = 0, 16, 32, 38, 40, 56
LAG = 3


def unit_base(qt):
    return HG * qt * (qt + 1) // 2


def causal_attention(nc, drams, xt, consts, tables):
    ident, identb, ones = consts[:3]
    after, before, q_rows, k_rows = tables
    wqkv, wo = drams
    with ExitStack() as st:
        sb, ps, sem = sb_in(nc, st), ps_in(nc, st), sem_in(nc)
        q_dram = nc.dram_tensor("a_q_stacked", [2, 64, PAIRS, S], F32).ap()
        k_dram = nc.dram_tensor("a_k_stacked", [2, P, S], F32).ap()
        o_dram = nc.dram_tensor("a_out_parts", [NB, 2, AH * AD, S], F32).ap()
        sums_dram, inv_dram = (nc.dram_tensor(f"a_exp_{x}", [NB, AH, S], F32).ap() for x in ("sums", "inverses"))
        wh, wl = (sb(f"a_wq_{x}", [P, DT, AH * AD], F32R) for x in ("high", "low"))
        wkvh, wkvl = (sb(f"a_wkv_{x}", [P, DT, KV], F32R) for x in ("high", "low"))
        woh, wol = (sb(f"a_wo_{x}", [P, DT, D], F32R) for x in ("high", "low"))
        ka = [sb(f"a_keys{i}", [P, S], F32R) for i in range(2)]
        kan = [sb(f"a_keys_next{i}", [P, S], F32R) for i in range(2)]
        vs, vn = sb("a_values", [P, ST, VROWS], F32R), sb("a_values_next", [P, ST, VROWS], F32R)
        below, above = sb("a_below_mask", [P, P], BF16), sb("a_above_mask", [P, 4 * P], BF16)
        with ExitStack() as early:
            sbe = sb_in(nc, early)
            w_raw, wo_raw = sbe("a_wqkv_raw", [P, DT, AH * AD + 2 * AD]), sbe("a_wo_raw", [P, DT, D])
            below_raw, above_raw = sbe("a_below_raw", [P, P]), sbe("a_above_raw", [P, 4 * P])
        with ExitStack() as late:
            last_at = sb_in(nc, late)("a_last_out", [P, DT, 3, S])
        qa = sb("a_queries", [P, PAIRS, S], F32R)
        zh, zl = (sb(f"a_z_{x}", [P, DT, S], F32R) for x in ("high", "low"))
        zf = sb("a_z", [P, DT, S])
        tmp = [sb(f"a_ln_tmp{i}", [P, S]) for i in range(3)]
        pf = sb("a_probs", [P, 4, S])
        ph, pl = (sb(f"a_probs_{x}", [P, 4, S], F32R) for x in ("high", "low"))
        ot = sb("a_out", [VROWS, 2, 2, 4, P])
        qsh, qsl = (sb(f"a_q_part_{x}", [P, 2, S], F32R) for x in ("high", "low"))
        kxh, kxl = (sb(f"a_k_part_{x}", [KV, S], F32R) for x in ("high", "low"))
        vt = sb("a_v_by_dim", [AD, S])
        at = zf[:, 0:3]
        sums = sb("a_sums_tile", [P, AH * S // P])
        ath, atl = (sb(f"a_out_{x}", [P, DT, S], F32R) for x in ("high", "low"))
        mx = sb("a_max", [P, 2, AH])
        mh, ml = (sb(f"a_minus_max_{x}", [AH, 2, P], F32R) for x in ("high", "low"))

        mbank = [ps(f"a_max_scores{i}", [P, S]) for i in range(2)]
        sbank = [ps(f"a_scores{i}", [P, S]) for i in range(2)]
        obank = [ps(f"a_o_sum{i}", [P, S]) for i in range(2)]
        misc = [ps(f"a_misc{i}", [P, S]) for i in range(2)]

        names = ("max_full", "max_read", "scores_full", "exp_done", "low_by_vector", "low_by_pool", "pv_done", "o_copied",
                 "misc_used", "m_high", "m_low", "kv_high", "kv_low", "vt_copied", "v_high", "v_low", "q_high", "q_low",
                 "k_landed", "keys_kept", "x_summed", "sq_ready", "sq_added", "centred", "seed", "z_ready",
                 "zh_ready", "zl_ready",
                 "pool_step", "act_step", "dve_step", "at_ready", "at_high", "at_low", "wo_added", "out_landed",
                 "sums_landed", "inv_ready", "inv_stored",
                 "w_in", "wo_in", "q_rows_in", "k_rows_in", "k_rows_back", "cleared", "w_high", "w_low",
                 "masks_in", "masks_ready")
        s = {n: sem(f"a_{n}") for n in names}
        misc_full, misc_free = [sem(f"a_misc_full{i}") for i in range(2)], [sem(f"a_misc_free{i}") for i in range(2)]
        q_stored = [sem(f"a_q_stored{i}") for i in range(2)]
        last_landed = [sem(f"a_last_out_landed{m}") for m in range(DT)]
        q_landed = [sem(f"a_q_landed{t}") for t in range(ST)]
        m_landed, o_stored = [sem(f"a_m_landed{i}") for i in range(2)], [sem(f"a_o_stored{i}") for i in range(2)]

        MEAN, VAR, TURNS, KEYS, OUT, OUT_STEP = 1, 11, (18, 42, 57, 74), 23, 48, 5
        prepare = [("KV", 0), ("Vt", 0)] + [("Q", m) for m in range(DT)]
        small = {MEAN: ("mean", 0), VAR: ("var", 0)}
        small |= {KEYS + 2 * n: x for n, x in enumerate(prepare)}
        small |= {OUT + 18 + 3 * d: ("Wo", d) for d in range(DT)}
        small |= {n: ("mT", qt) for n, qt in zip(TURNS, range(2, ST + 2))}
        searches = [(0, 17, 2), (19, 41, 3), (43, 56, 4), (58, 73, 5)]
        assert len(small) == 8 + 2 * DT
        ahead_only = {("mean", 0), ("var", 0), ("mT", 4), ("mT", 5), *prepare}
        BEFORE = [("mean", 0), ("var", 0), *prepare, ("mT", 4), ("mT", 5)]

        NQ = AH * AD
        splits = [(w_raw[:, :, 0:NQ], wh[:, :, :], wl[:, :, :]),
                  (w_raw[:, :, NQ + AD:], wkvh[:, :, 0:AD], wkvl[:, :, 0:AD]),
                  (w_raw[:, :, NQ:NQ + AD], wkvh[:, :, 32:KV], wkvl[:, :, 32:KV]),
                  (wo_raw[:, :, :], woh[:, :, :], wol[:, :, :])]

        LARGE = ("KV", "Q", "Wo")

        class Batch:

            def __init__(self, it, first=False, last=False):
                self.it, self.first, self.last = it, first, last
                self.small = {k: x for k, x in sorted(small.items())
                              if not (first and x[0] == "Wo") and not (last and x in ahead_only)}
                self.order = list(self.small.values())

            def misc(self, x):
                if self.it is None:
                    n = BEFORE.index(x)
                    return n % 2, n // 2 + 1
                n = self.order.index(x) + (len(BEFORE) if self.first else len(BEFORE) - DT)
                full = len(small) // 2
                return n % 2, (0 if self.first else self.it * full) + n // 2 + 1

            def ahead(self):
                return 0 if self.it is None else self.it + 1

            def steps(self):
                for g in range(UB):
                    yield "scores", g
                    for since, until, tile in searches:
                        if since <= g < until and not (self.last and tile >= ST):
                            n = GROUPS[tile % ST]
                            for j in range(n * (g - since) // (until - since), n * (g + 1 - since) // (until - since)):
                                yield "max", tile, j
                    if g >= LAG:
                        yield "pv", g - LAG
                    if g - 1 in self.small and self.small[g - 1][0] in LARGE:
                        yield ("small", *self.small[g - 1], 1)
                    if g in self.small:
                        yield ("small", *self.small[g], 0 if self.small[g][0] in LARGE else None)
                    for n in (2, 1):
                        if g - n in self.small and (self.small[g - n][0] in LARGE) == (n == 2):
                            yield ("read", *self.small[g - n])
                for g in range(UB - LAG, UB):
                    yield "pv", g

        assert len(small) % 2 == 0

        UB = unit_base(ST)

        def place(g):
            qt = max(t for t in range(ST) if unit_base(t) <= g)
            return (qt, *divmod(g - unit_base(qt), qt + 1))

        def group_end(g):
            qt, hg, kt = place(g)
            return qt * HG + hg if kt == qt else None

        def split_by(b, g):
            on_vector = g % 4 == 1
            same = [x for x in range(UB) if (x % 4 == 1) == on_vector]
            return s["low_by_vector" if on_vector else "low_by_pool"], b.it * len(same) + same.index(g) + 1

        def wait(e, sem, value):
            if not (isinstance(value, int) and value <= 0):
                e.wait_ge(sem, value)

        def batches(e, body):
            body(Batch(0, first=True))
            with e.Fori(1, NB - 1) as it:
                body(Batch(it))
            body(Batch(NB - 1, last=True))

        class Finish(Batch):

            def __init__(self):
                self.it = NB

            def misc(self, x):
                n = NB * len(small) + len(BEFORE) - DT + x[1] - len(ahead_only)
                return n % 2, n // 2 + 1

        GROUPS = [AH * P * min(n, 4) // S if n < 3 else AH for n in range(1, ST + 1)]

        def heads_of(t, j):
            if GROUPS[t] == AH:
                return [(0, j % 2, j // 2)]
            n = PAIRS // GROUPS[t]
            return [((half * n + k) * (t + 1) * P, half, j * n + k) for half in range(2) for k in range(n)]

        def searched(b, qt):
            return (b.it if b.it is not None and qt < ST else b.ahead()) * sum(GROUPS) + sum(GROUPS[:qt % ST])

        def step_of(b, qt):
            base = -ST if b.it is None else b.it * ST
            return base + qt, qt % 2

        block = st.enter_context(nc.Block())

        @block.tensor
        def _(e):
            def three(out, w, z, first, last):
                for n, (x, y) in enumerate([(w[0], z[0]), (w[0], z[1]), (w[1], z[0])]):
                    mm = e.matmul(out, x, y, start=first and n == 0, stop=last and n == 2)
                return mm

            def small_product(b, kind, i, part=None):
                parts = range(DT) if part is None else range(part * DT // 2, (part + 1) * DT // 2)
                k, n = b.misc((kind, i))
                bank, full = misc[k], misc_full[k]
                if part != 1:
                    wait(e, misc_free[k], n - 1)
                if kind in ("mean", "var"):
                    wait(e, s["x_summed"] if kind == "mean" else s["sq_added"],
                         b.ahead() * (1 if kind == "mean" else 3) + (1 if kind == "mean" else 3))
                    mm = e.matmul(bank[:, :], ones[:, :], tmp[2][:, :], start=True, stop=True)
                elif kind in ("KV", "Q"):
                    e.wait_ge(s["zl_ready"], (b.ahead() + 1) * DT)
                    w = (wkvh, wkvl) if kind == "KV" else [x[:, :, i * P:(i + 1) * P] for x in (wh, wl)]
                    out = bank[0:KV, :] if kind == "KV" else bank[:, :]
                    for d in parts:
                        mm = three(out, [x[:, d, :] for x in w], [z[:, d, :] for z in (zh, zl)], d == 0, d == DT - 1)
                elif kind == "Vt":
                    e.wait_ge(s["vt_copied"], b.ahead() + 1)
                    for t in range(ST):
                        mm = e.matmul(bank[:, t * AD:(t + 1) * AD], vt[:, t * P:(t + 1) * P], ident[0:AD, 0:AD], start=True,
                                      stop=True)
                elif kind == "mT":
                    step, par = step_of(b, i)
                    e.wait_ge(s["max_read"], searched(b, i) + GROUPS[i % ST])
                    mm = e.transpose(bank[0:AH, 0:P], mx[:, par, :], ident[:, :])
                else:
                    e.wait_ge(s["at_low"], b.it * DT)
                    for m in parts:
                        mm = three(bank[:, :], [x[:, m, i * P:(i + 1) * P] for x in (woh, wol)],
                                   [x[:, m, :] for x in (ath, atl)], m == 0, m == DT - 1)
                if part != 0:
                    mm.then_inc(full, 1)

            def max_scores(b, qt, j):
                t, keys, bank = qt % ST, kan if qt >= ST else ka, mbank[j % 2]
                if j == 0:
                    e.wait_ge(q_landed[t], 16 * (b.ahead() + (1 if qt >= ST else 0)) if b.it is not None else 16)
                    if qt >= ST:
                        e.wait_ge(s["k_landed"], 96 * (b.ahead() + 1))
                wait(e, s["max_read"], searched(b, qt) + j - 1)
                n = (t + 1) * P
                for col, half, pair in heads_of(t, j):
                    e.matmul(bank[:, col:col + n], qa[:, pair, t * P:n], keys[half][:, 0:n], start=True, stop=False,
                             skip_group_check=True)
                    mm = e.matmul(bank[:, col + t * P:col + n], identb[:, :], below[:, :], start=False, stop=True,
                                  skip_group_check=True)
                mm.then_inc(s["max_full"], 1)

            def score(b, g):
                qt, hg, kt = place(g)
                if g == 0:
                    e.wait_ge(s["keys_kept"], (b.it + 1) * 3)
                if g == unit_base(qt):
                    e.wait_ge(m_landed[qt % 2], 64 * (b.it * 2 + qt // 2 + 1))
                wait(e, s["exp_done"], b.it * UB + g - 1)
                half, head = divmod(4 * hg, PAIRS)
                diagonal = kt == qt
                mm = e.matmul(sbank[g % 2][:, :], ka[half][:, kt * P:(kt + 1) * P],
                              qa[:, head:head + 4, qt * P:(qt + 1) * P], start=True, stop=not diagonal,
                              skip_group_check=True)
                if diagonal:
                    mm = e.matmul(sbank[g % 2][:, :], identb[:, :], above[:, :], start=False, stop=True,
                                  skip_group_check=True)
                mm.then_inc(s["scores_full"], 1)

            def weigh(b, g):
                qt, hg, kt = place(g)
                if kt == 0:
                    wait(e, s["o_copied"], b.it * ST * HG + qt * HG + hg - 1)
                e.wait_ge(*split_by(b, g))
                for x in (ph, pl):
                    mm = e.matmul(obank[hg % 2][0:VROWS, :], vs[:, kt, :], x[:, g % 4, :], start=kt == 0 and x is ph,
                                  stop=kt == qt and x is pl)
                mm.then_inc(s["pv_done"], 1)

            def body(b):
                for kind, *x in b.steps():
                    if kind != "read":
                        {"scores": score, "max": max_scores, "pv": weigh, "small": small_product}[kind](b, *x)

            first = Batch(None)
            for x in BEFORE:
                if x[0] == "KV":
                    e.wait_ge(s["w_low"], len(splits))
                    e.wait_ge(s["masks_ready"], 2)
                    e.wait_ge(s["cleared"], 2)
                for j in range(GROUPS[x[1] % ST]) if x[0] == "mT" else ():
                    max_scores(first, x[1], j)
                small_product(first, *x)
            batches(e, body)
            for d in range(DT):
                small_product(Finish(), "Wo", d)

        @block.vector
        def _(e):
            def read_small(b, kind, i):
                k, n = b.misc((kind, i))
                bank, free = misc[k], misc_free[k]
                if kind == "mean":
                    pass
                elif kind == "var":
                    e.wait_ge(misc_full[k], n)
                    e.tensor_scalar(tmp[0][:, :], bank[:, :], LN_EPS, None, ALU.add).then_inc(free, 1)
                elif kind == "KV":
                    e.wait_ge(s["kv_high"], b.ahead() + 1)
                    e.scalar_tensor_tensor(kxl[32:KV, :], bank[32:KV, :], AD ** -0.5, f32(kxh[32:KV, :]), ALU.mult,
                                           ALU.subtract).then_inc(s["kv_low"], 1)
                    e.wait_ge(s["kv_low"], b.ahead() + 1)
                    e.sem_inc(free, 1)
                elif kind == "Vt":
                    e.wait_ge(s["v_high"], b.ahead() + 1)
                    e.tensor_tensor(vn[:, :, 32:32 + AD], bank[:, 0:ST * AD].rearrange("p (t d) -> p t d", t=ST),
                                    f32(vn[:, :, 0:AD]), ALU.subtract).then_inc(s["v_low"], 1)
                    e.wait_ge(s["v_low"], b.ahead() + 1)
                    e.sem_inc(free, 1)
                elif kind == "Q":
                    e.wait_ge(s["q_high"], b.ahead() * DT + i + 1)
                    e.tensor_tensor(qsl[:, i % 2], bank[:, :], f32(qsh[:, i % 2]), ALU.subtract).then_inc(s["q_low"], 1)
                    e.wait_ge(s["q_low"], b.ahead() * DT + i + 1)
                    e.sem_inc(free, 1)
                elif kind == "mT":
                    step, par = step_of(b, i)
                    e.wait_ge(s["m_high"], step + 1)
                    e.scalar_tensor_tensor(ml[:, par], bank[0:AH, 0:P], -1.0, f32(mh[:, par]), ALU.mult,
                                           ALU.subtract).then_inc(s["m_low"], 1)
                    e.wait_ge(s["m_low"], step + 1)
                    e.sem_inc(free, 1)
                else:
                    e.wait_ge(misc_full[k], n)
                    here = xt[:, i, bass.ds((b.it - 1) * S, S)]
                    e.tensor_tensor(here, here, bank[:, :], ALU.add).then_inc(free, 1)

            def centre(b, d):
                k, n = b.misc(("mean", 0))
                if d == 0:
                    e.wait_ge(misc_full[k], n)
                    wait(e, s["zl_ready"], b.ahead() * DT)
                    if b.it is not None and not b.first:
                        e.wait_ge(s["at_low"], (b.it - 1) * DT)
                e.tensor_tensor(zf[:, d], xt[:, d, bass.ts(0 if b.it is None else b.it + 1, S)], misc[k][:, :],
                                ALU.subtract).then_inc(s["centred"], 1)
                if d == DT - 1:
                    e.wait_ge(s["centred"], (b.ahead() + 1) * DT)
                    e.sem_inc(misc_free[k], 1)

            def inverse_std(b, chain):
                e.wait_ge(s["seed"], b.ahead() + 1)
                chain(e.scalar_tensor_tensor(tmp[2][:, :], tmp[0][:, :], -0.5, tmp[1][:, :], ALU.mult, ALU.mult))
                chain(e.tensor_tensor(tmp[2][:, :], tmp[2][:, :], tmp[1][:, :], ALU.mult))
                chain(e.scalar_tensor_tensor(tmp[0][:, :], tmp[2][:, :], 1.5, tmp[1][:, :], ALU.add, ALU.mult))

            def normalise(b, d):
                e.tensor_tensor(zf[:, d], zf[:, d], tmp[0][:, :], ALU.mult).then_inc(s["z_ready"], 1)

            def find_max(b, qt, j):
                step, par = step_of(b, qt)
                t, bank = qt % ST, mbank[j % 2]
                e.wait_ge(s["max_full"], searched(b, qt) + j + 1)
                if j == 0:
                    wait(e, s["m_high"], step - 1)
                to = mx[:, par].rearrange("p (a h) -> p a h", a=2)
                if GROUPS[t] == AH:
                    to, scores = to[:, j % 2, j // 2:j // 2 + 1], bank[:, 0:(t + 1) * P]
                else:
                    n = PAIRS // GROUPS[t]
                    to = to[:, :, j * n:(j + 1) * n]
                    scores = bank[:, :].rearrange("p (a h k) -> p a h k", a=2, h=n)
                e.tensor_reduce(to, scores, AX.X, ALU.max).then_inc(s["max_read"], 1)

            def low_probs(b, g):
                e.wait_ge(s["exp_done"], b.it * UB + g + 1)
                e.tensor_tensor(pl[:, g % 4], pf[:, g % 4], f32(ph[:, g % 4]), ALU.subtract)\
                    .then_inc(s["low_by_vector"], 1)

            def low_weights(i):
                raw, hi, lo = splits[i]
                e.wait_ge(s["w_high"], i + 1)
                e.tensor_tensor(lo, raw, f32(hi), ALU.subtract).then_inc(s["w_low"], 1)

            def invert_sums(b):
                e.wait_ge(s["sums_landed"], 16 * (b + 1))
                e.reciprocal(sums[:, :], sums[:, :]).then_inc(s["inv_ready"], 1)

            def out_tile(count, chain, at=at, landed=None):
                e.wait_ge(landed or s["out_landed"], 32 * (1 if landed else count + 1))
                chain(e.tensor_tensor(at[:, 0], at[:, 0], at[:, 1], ALU.add))
                e.tensor_tensor(at[:, 0], at[:, 0], at[:, 2], ALU.mult).then_inc(s["at_ready"], 1)

            def low_out(m, count, at=at):
                e.wait_ge(s["at_high"], count + 1)
                e.tensor_tensor(atl[:, m], at[:, 0], f32(ath[:, m]), ALU.subtract).then_inc(s["at_low"], 1)

            def keep_keys(b):
                e.wait_ge(s["k_landed"], 96 * (b.it + 1))
                wait(e, s["pv_done"], b.it * UB)
                e.tensor_copy(ka[0][:, :], kan[0][:, :]).then_inc(s["keys_kept"], 1)
                e.tensor_copy(ka[1][:, :], kan[1][:, :]).then_inc(s["keys_kept"], 1)
                e.wait_ge(s["v_low"], b.it + 1)
                e.tensor_copy(vs[:, :, :], vn[:, :, :]).then_inc(s["keys_kept"], 1)

            def body(b):
                chain = Chain(e, s["dve_step"], 3 if b.first else b.it * 7 - 1)
                keep_keys(b)
                for kind, *x in b.steps():
                    if kind == "max":
                        find_max(b, *x)
                    elif kind == "scores":
                        g = x[0]
                        if not b.last:
                            if MEAN < g <= MEAN + DT:
                                centre(b, g - MEAN - 1)
                            if g == VAR + 4:
                                inverse_std(b, chain)
                            if VAR + 4 < g <= VAR + 4 + DT:
                                normalise(b, g - VAR - 5)
                        if not b.first:
                            if g == 8:
                                invert_sums(b.it - 1)
                            if OUT <= g < OUT + OUT_STEP * DT and (g - OUT) % OUT_STEP == 0:
                                out_tile((b.it - 1) * DT + (g - OUT) // OUT_STEP, chain)
                            if OUT < g <= OUT + OUT_STEP * DT and (g - OUT) % OUT_STEP == 1:
                                m = (g - OUT) // OUT_STEP
                                low_out(m, (b.it - 1) * DT + m)
                    elif kind == "read":
                        read_small(b, *x)
                    if kind == "scores" and x[0] % 4 == 2:
                        low_probs(b, x[0] - 1)

            first = Batch(None)
            chain = Chain(e, s["dve_step"])
            e.wait_ge(s["masks_in"], 32)
            e.tensor_copy(below[:, :], below_raw[:, :]).then_inc(s["masks_ready"], 1)
            e.tensor_copy(above[:, :], above_raw[:, :]).then_inc(s["masks_ready"], 1)
            for x in BEFORE:
                if x[0] == "Vt":
                    e.wait_ge(s["cleared"], 4)
                for j in range(GROUPS[x[1] % ST]) if x[0] == "mT" else ():
                    find_max(first, x[1], j)
                read_small(first, *x)
                if x[0] == "var":
                    for i in range(len(splits) - 1):
                        low_weights(i)
                for d in range(DT):
                    if x[0] == "mean":
                        centre(first, d)
                    if x[0] == "var":
                        if d == 0:
                            inverse_std(first, chain)
                        normalise(first, d)
                if x[0] == "var":
                    low_weights(3)
            batches(e, body)
            chain = Chain(e, s["dve_step"], 7 * NB - 4)
            invert_sums(NB - 1)
            for m in range(DT):
                out_tile((NB - 1) * DT + m, chain, last_at[:, m], last_landed[m])
            for m in range(DT):
                low_out(m, (NB - 1) * DT + m, last_at[:, m])
            for d in range(DT):
                read_small(Finish(), "Wo", d)

        @block.scalar
        def _(e):
            def read_small(b, kind, i):
                k, n = b.misc((kind, i))
                bank = misc[k]
                if kind == "var":
                    e.wait_ge(misc_free[k], n)
                    e.activation(tmp[1][:, :], tmp[0][:, :], ACT.Ln).then_inc(s["act_step"], 1)
                    e.wait_ge(s["act_step"], b.ahead() + 1)
                    e.activation(tmp[1][:, :], tmp[1][:, :], ACT.Exp, scale=-0.5).then_inc(s["seed"], 1)
                elif kind == "KV":
                    e.wait_ge(misc_full[k], n)
                    wait(e, s["k_landed"], 96 * b.ahead())
                    e.copy(vt[:, :], bank[0:AD, :]).then_inc(s["vt_copied"], 1)
                    e.activation(kxh[32:KV, :], bank[32:KV, :], ACT.Copy, scale=AD ** -0.5).then_inc(s["kv_high"], 1)
                elif kind == "Vt":
                    e.wait_ge(misc_full[k], n)
                    wait(e, s["keys_kept"], 3 * b.ahead())
                    e.copy(vn[:, :, 0:AD], bank[:, 0:ST * AD].rearrange("p (t d) -> p t d", t=ST)).then_inc(s["v_high"], 1)
                elif kind == "Q":
                    e.wait_ge(misc_full[k], n)
                    wait(e, q_stored[i % 2], 48 * (DT // 2 * b.ahead() + i // 2))
                    e.copy(qsh[:, i % 2], bank[:, :]).then_inc(s["q_high"], 1)
                elif kind == "mT":
                    step, par = step_of(b, i)
                    e.wait_ge(misc_full[k], n)
                    wait(e, m_landed[par], 64 * (((-1 if b.it is None else b.it) * 2) + i // 2))
                    e.activation(mh[:, par], bank[0:AH, 0:P], ACT.Copy, scale=-1.0).then_inc(s["m_high"], 1)

            def square(b, d):
                e.wait_ge(s["centred"], b.ahead() * DT + d + 1)
                if d >= 2:
                    e.wait_ge(s["sq_added"], b.ahead() * 3 + 1)
                e.activation(tmp[d % 2][:, :], zf[:, d], ACT.Square).then_inc(s["sq_ready"], 1)

            def high_z(b, d):
                e.wait_ge(s["z_ready"], b.ahead() * DT + d + 1)
                e.copy(zh[:, d], zf[:, d]).then_inc(s["zh_ready"], 1)

            def exps(b, g):
                e.wait_ge(s["scores_full"], b.it * UB + g + 1)
                if g >= 4 or not b.first:
                    before = (b, g - 4) if g >= 4 else (Batch(b.it - 1), g - 4 + UB)
                    e.wait_ge(*split_by(*before))
                e.activation(pf[:, g % 4], sbank[g % 2][:, :], ACT.Exp)
                wait(e, s["pv_done"], b.it * UB + g - 3)
                e.activation(ph[:, g % 4], sbank[g % 2][:, :], ACT.Exp).then_inc(s["exp_done"], 1)

            def copy_out(b, g):
                hg = place(g)[1]
                e.wait_ge(s["pv_done"], b.it * UB + g + 1)
                if hg % 2 == 0:
                    wait(e, o_stored[hg // 2 % 2], 48 * (b.it * 2 * ST + group_end(g) // 4))
                e.copy(ot[:, hg // 2 % 2, hg % 2], obank[hg % 2][0:VROWS, :].rearrange("p (h q) -> p h q", h=4))\
                    .then_inc(s["o_copied"], 1)

            def high_weights(i):
                raw, hi, _ = splits[i]
                e.wait_ge(s["wo_in" if i == 3 else "w_in"], 16)
                e.copy(hi, raw).then_inc(s["w_high"], 1)

            def high_out(m, count, at=at):
                e.wait_ge(s["at_ready"], count + 1)
                e.copy(ath[:, m], at[:, 0]).then_inc(s["at_high"], 1)

            def body(b):
                for kind, *x in b.steps():
                    if kind == "scores":
                        g = x[0]
                        exps(b, g)
                        if not b.last:
                            if MEAN + 1 < g <= MEAN + 1 + DT:
                                square(b, g - MEAN - 2)
                            if VAR + 5 < g <= VAR + 5 + DT:
                                high_z(b, g - VAR - 6)
                        if not b.first and OUT <= g < OUT + OUT_STEP * DT and (g - OUT) % OUT_STEP == 0:
                            m = (g - OUT) // OUT_STEP
                            high_out(m, (b.it - 1) * DT + m)
                    elif kind == "pv" and group_end(x[0]) is not None:
                        copy_out(b, x[0])
                    elif kind == "small" and x[2] != 0:
                        read_small(b, *x[:2])

            first = Batch(None)
            for x in BEFORE:
                if x[0] == "Vt":
                    e.wait_ge(s["cleared"], 4)
                if x[0] == "var":
                    for i in range(len(splits) - 1):
                        high_weights(i)
                read_small(first, *x)
                if x[0] == "var":
                    high_weights(3)
                for d in range(DT):
                    if x[0] == "mean":
                        square(first, d)
                    if x[0] == "var":
                        high_z(first, d)
            batches(e, body)
            for m in range(DT):
                high_out(m, (NB - 1) * DT + m, last_at[:, m])

        @block.gpsimd
        def _(e):
            def sum_x(b, chain):
                wait(e, s["z_ready"], b.ahead() * DT)
                here = xt[:, :, bass.ts(0 if b.it is None else b.it + 1, S)]
                chain(e.tensor_tensor(tmp[2][:, :], here[:, 0], here[:, 1], ALU.add))
                chain(e.tensor_tensor(tmp[2][:, :], tmp[2][:, :], here[:, 2], ALU.add))
                e.tensor_tensor(tmp[2][:, :], tmp[2][:, :], here[:, 3], ALU.add).then_inc(s["x_summed"], 1)

            def sum_squares(b, n):
                e.wait_ge(s["sq_ready"], b.ahead() * DT + n + 2)
                if n:
                    e.wait_ge(s["sq_added"], b.ahead() * 3 + n)
                e.tensor_tensor(tmp[2][:, :], tmp[0][:, :] if n == 0 else tmp[2][:, :], tmp[(n + 1) % 2][:, :],
                                ALU.add).then_inc(s["sq_added"], 1)

            def low_z(b, d):
                e.wait_ge(s["zh_ready"], b.ahead() * DT + d + 1)
                e.tensor_tensor(zl[:, d], zf[:, d], f32(zh[:, d]), ALU.subtract).then_inc(s["zl_ready"], 1)

            def low_probs(b, g):
                e.wait_ge(s["exp_done"], b.it * UB + g + 1)
                e.tensor_tensor(pl[:, g % 4], pf[:, g % 4], f32(ph[:, g % 4]), ALU.subtract)\
                    .then_inc(s["low_by_pool"], 1)

            def body(b):
                if not b.last:
                    sum_x(b, Chain(e, s["pool_step"], b.it * 2 + 2))
                for kind, *x in b.steps():
                    if kind == "scores":
                        g = x[0]
                        if g % 4 != 1:
                            low_probs(b, g)
                        if b.last:
                            continue
                        if g in (MEAN + 4, MEAN + 6, MEAN + 7):
                            sum_squares(b, (MEAN + 4, MEAN + 6, MEAN + 7).index(g))
                        if VAR + 6 < g <= VAR + 6 + DT:
                            low_z(b, g - VAR - 7)

            first = Batch(None)
            for x in (wkvh, wkvl):
                e.memset(f32(x[:, :, AD:32]), 0.0).then_inc(s["cleared"], 1)
            sum_x(first, Chain(e, s["pool_step"]))
            for n in range(3):
                sum_squares(first, n)
            e.memset(f32(vn[:, :, 0:64]), 0.0).then_inc(s["cleared"], 1)
            e.memset(f32(vn[:, :, 64:VROWS]), 1.0).then_inc(s["cleared"], 1)
            for d in range(DT):
                low_z(first, d)
            batches(e, body)

        @block.sync
        def _(e):
            def send_keys(b):
                e.wait_ge(s["kv_low"], b.ahead() + 1)
                wait(e, s["keys_kept"], 3 * b.ahead())
                for half in range(2):
                    for row, part in ((R_QHI, kxh), (R_QLO, kxh), (R_QHI2, kxl)):
                        r = 64 * half + row
                        e.dma_start(f32(kan[half][r:r + AD, :]), f32(part[32:KV, :])).then_inc(s["k_landed"], 16)

            def send_queries(b, m):
                if m == 0:
                    for t in range(ST):
                        wait(e, q_landed[t], 16 * b.ahead())
                e.wait_ge(s["q_low"], b.ahead() * DT + m + 1)
                half, head = divmod(8 * m, PAIRS)
                for row, part in ((R_QHI, qsh), (R_QLO, qsl), (R_QHI2, qsh)):
                    to = q_dram[half, row:row + AD, head:head + 8, :].rearrange("d h t -> h d t")
                    e.dma_start(to, f32(part[:, m % 2])).then_inc(q_stored[m % 2], 16)

            def load_queries(b, t, used=True):
                if used:
                    e.wait_ge(s["scores_full"], b.it * UB + unit_base(t + 1))
                e.dma_start(f32(qa[:, :, t * P:(t + 1) * P]),
                            q_dram[:, :, :, t * P:(t + 1) * P].rearrange("a r h t -> (a r) h t")).then_inc(q_landed[t], 16)

            def queries_stored(b):
                for k in range(2):
                    e.wait_ge(q_stored[k], 48 * DT // 2 * (b.ahead() + 1))

            def send_max(b, i):
                step, par = step_of(b, i)
                e.wait_ge(s["m_low"], step + 1)
                t = i % ST * P
                for half in range(2):
                    for row, part in ((R_MAX, mh), (R_MAX + 1, ml)):
                        r = 64 * half + row
                        e.dma_start(f32(qa[r:r + 1, :, t:t + P]), f32(part[half * PAIRS:(half + 1) * PAIRS, par, :]))\
                            .then_inc(m_landed[par], 16)

            def store_out(b, g):
                qt, hg, _ = place(g)
                tile = hg // 2
                e.wait_ge(s["o_copied"], b.it * ST * HG + group_end(g) + 1)
                for c in range(2):
                    to = o_dram[bass.ds(b.it, 1), c, tile * P:(tile + 1) * P, qt * P:(qt + 1) * P]\
                        .rearrange("b (h d) q -> d (b h) q", d=AD)
                    e.dma_start(to, ot[32 * c:32 * c + AD, tile % 2].rearrange("p a h q -> p (a h) q"))\
                        .then_inc(o_stored[tile % 2], 16)
                e.dma_start(sums_dram[bass.ds(b.it, 1), 8 * tile:8 * tile + 8, qt * P:(qt + 1) * P],
                            ot[64:65, tile % 2].rearrange("p a h q -> p (a h) q")).then_inc(o_stored[tile % 2], 16)

            def load_sums(b):
                for k in range(2):
                    e.wait_ge(o_stored[k], 48 * 2 * ST * (b + 1))
                e.dma_start(sums[:, :], sums_dram[bass.ds(b, 1)].rearrange("b h (c q) -> (b h c) q", c=ST))\
                    .then_inc(s["sums_landed"], 16)

            def store_inverses(b):
                e.wait_ge(s["inv_ready"], b + 1)
                e.dma_start(inv_dram[bass.ds(b, 1)].rearrange("b h (c q) -> (b h c) q", c=ST), sums[:, :])\
                    .then_inc(s["inv_stored"], 16)

            def load_out(b, m, at=at, landed=s["out_landed"]):
                if m == 0:
                    e.wait_ge(s["inv_stored"], 16 * (b + 1))
                elif not isinstance(b, int) or b < NB - 1:
                    wait(e, s["at_low"], b * DT + m)
                e.dma_start(at[:, 0:2, :], o_dram[bass.ds(b, 1), :, m * P:(m + 1) * P, :].rearrange("b c p t -> p (b c) t"))\
                    .then_inc(landed, 16)
                heads = P // AD
                e.dma_start(at[:, 2, :], inv_dram[bass.ds(b, 1), heads * m:heads * (m + 1)].rearrange("b h t -> (b h) t")
                            .unsqueeze(1).broadcast_to([heads, AD, S])).then_inc(landed, 16)

            def body(b):
                for kind, *x in b.steps():
                    if kind == "scores" and not b.first:
                        g = x[0]
                        if g == 2:
                            load_sums(b.it - 1)
                        if g == 14:
                            store_inverses(b.it - 1)
                        if OUT - 6 <= g < OUT + OUT_STEP * DT - 6 and (g - OUT + 6) % OUT_STEP == 0:
                            load_out(b.it - 1, (g - OUT + 6) // OUT_STEP)
                    if kind == "scores" and x[0] == unit_base(3) + 1 and not b.last:
                        load_queries(b, 2)
                    if kind == "pv" and group_end(x[0]) is not None and group_end(x[0]) % 2:
                        store_out(b, x[0])
                    if kind != "small" or x[2] == 0:
                        continue
                    if x[0] == "mT":
                        send_max(b, x[1])
                    if x[0] == "KV":
                        send_keys(b)
                    if x[0] == "Q":
                        send_queries(b, x[1])
                        if x[1] == DT - 1:
                            queries_stored(b)
                            load_queries(b, 0)
                            load_queries(b, 1)
                if not b.last:
                    load_queries(b, 3)

            first = Batch(None)
            e.dma_start(below_raw[:, :], after).then_inc(s["masks_in"], 16)
            e.dma_start(above_raw[:, :], before).then_inc(s["masks_in"], 16)
            e.dma_start(w_raw[:, :, :], wqkv.rearrange("(t p) n -> p t n", p=P)).then_inc(s["w_in"], 16)
            e.dma_start(k_dram, k_rows).then_inc(s["k_rows_in"], 16)
            e.dma_start(wo_raw[:, :, :], wo.rearrange("(t p) n -> p t n", p=P)).then_inc(s["wo_in"], 16)
            e.dma_start(q_dram[:, R_BIAS:R_QHI2], q_rows[:, 0:8]).then_inc(s["q_rows_in"], 16)
            e.dma_start(q_dram[:, R_ZERO:64], q_rows[:, 8:16]).then_inc(s["q_rows_in"], 16)
            e.wait_ge(s["k_rows_in"], 16)
            for half in range(2):
                e.dma_start(f32(kan[half][:, :]), k_dram[half]).then_inc(s["k_rows_back"], 16)
            e.wait_ge(s["k_rows_back"], 32)
            send_keys(first)
            e.wait_ge(s["q_rows_in"], 32)
            for m in range(DT):
                send_queries(first, m)
            queries_stored(first)
            for t in range(ST):
                load_queries(first, t, used=False)
            send_max(first, ST)
            send_max(first, ST + 1)
            batches(e, body)
            load_sums(NB - 1)
            store_inverses(NB - 1)
            for m in range(DT):
                load_out(NB - 1, m, last_at[:, m], last_landed[m])


QH, KVH, HD = 32, 8, 128
GRP = QH // KVH
SM_SCALE = HD ** -0.5
HALF = HD // 2
UNITS = 2 * GRP
BELOW_ALL = -3.0e38


def window_attention(nc, drams, xt, consts, tables):
    ident, ones = consts[0], consts[2]
    wq, wk, wv, wo = drams
    with ExitStack() as st:
        sb, ps, sem = sb_in(nc, st), ps_in(nc, st), sem_in(nc)
        yh, yl = (sb(f"y_{x}", [P, DT, 2 * S], F32R) for x in ("high", "low"))
        wqh, wql = (sb(f"wq_{x}", [P, DT, GRP * HD], F32R) for x in ("high", "low"))
        wkvh, wkvl = (sb(f"wkv_{x}", [P, 2, DT, HD], F32R) for x in ("high", "low"))
        woh, wol = (sb(f"wo_{x}", [P, GRP, D], F32R) for x in ("high", "low"))
        wq_raw, wkv_raw = sb("wq_raw", [P, DT, 2 * HD]), sb("wkv_raw", [P, 2, DT, HD])
        wo_raw = sb("wo_raw", [P, GRP, D])
        qh, ql = (sb(f"q_{x}", [P, 2, S], F32R) for x in ("high", "low"))
        kh, kl = (sb(f"k_{x}", [P, 2, S], F32R) for x in ("high", "low"))
        vh, vl = (sb(f"v_{x}", [P, 2, ST, HD], F32R) for x in ("high", "low"))
        vt = sb("v_by_dim", [P, S])
        ra, rb = sb("rope_straight", [P, 2, S]), sb("rope_crossed", [P, 2, S])
        probs = sb("probs", [P, 2, ST, 2 * P])
        top, bias = sb("score_max", [P, 2, ST]), sb("exp_bias", [P, 2, ST])
        cos, sin, mask = sb("cos_table", [P, S]), sb("sin_table", [P, S]), sb("window_mask", [P, 2 * P])
        nothing = sb("nothing", [1, 1])
        total, share = sb("exp_sum", [P, 2, ST]), sb("exp_sum_inverse", [P, 2, ST])
        with ExitStack() as early:
            sbe = sb_in(nc, early)
            zf, sq = sbe("y_centred", [P, 2, DT, S]), sbe("y_squares", [P, DT, S])
            tmp = [[sbe(f"y_tmp{half}_{i}", [P, S]) for i in range(3)] for half in range(2)]
        oh, ol = (sb(f"o_{x}", [P, 2, GRP, S], F32R) for x in ("high", "low"))
        pth, ptl = (sb(f"probs_turned_{x}", [P, ST * 2 * P - P], F32R) for x in ("high", "low"))

        ring = [ps(f"proj{i}", [P, S]) for i in range(2)]
        scores = ps("scores", [P, ST, 2 * P])
        pt = ps("probs_turned", [P, 2 * S])
        obank, wbank = ps("o_sum", [P, S]), ps("w_sum", [P, S])

        mean_bank = [ring[0][:, :], scores[:, 0:2].rearrange("p t k -> p (t k)")]
        var_bank = [ring[1][:, :], scores[:, 2:4].rearrange("p t k -> p (t k)")]

        ring_full, ring_free = [sem(f"b_proj_full{i}") for i in range(2)], [sem(f"b_proj_free{i}") for i in range(2)]
        o_full, w_full, w_free = (sem(f"b_{n}") for n in ("o_full", "w_full", "w_free"))
        ln_mean, ln_centred, ln_squared, ln_summed, ln_vare, ln_seed, ln_z, ln_yh, ln_yl = (
            sem(f"b_ln_{n}") for n in ("mean", "centred", "squared", "summed", "var_read", "seed", "z", "yh", "yl"))
        act_step, dve_step = sem("b_act_step"), sem("b_dve_step")
        tables_in = sem("b_tables_landed")
        raw_in = {n: sem(f"b_{n}_raw_landed") for n in ("wo", "wkv", "wq")}
        w_high, w_low = ({n: sem(f"b_{n}_{x}_ready") for n in ("wo", "wkv", "wq")} for x in ("high", "low"))
        roped, rope_high, rope_low = (sem(f"b_{n}") for n in ("roped", "rope_high", "rope_low"))
        vt_ready, v_high, v_low = sem("b_v_by_dim"), sem("b_v_high"), sem("b_v_low")
        s_full, s_max, bias_ready, exp_done, p_ready = (
            sem(f"b_{n}") for n in ("scores_full", "scores_max", "bias_ready", "exp_done", "probs_ready"))
        pt_full, pt_high, pt_low = (sem(f"b_{n}") for n in ("turned_full", "turned_high", "turned_low"))
        o_high, o_low = sem("b_o_high"), sem("b_o_low")

        proj = [("Q", 2), ("Q", 3), ("Q", 4), ("K", 1), ("Q", 5), ("V", 1), ("N", 1), ("Q", 6), ("Q", 7),
                ("Q", 8), ("K", 2), ("Q", 9), ("V", 2), ("N", 2)]
        ropes = [x for x in proj if x[0] in "QK"]
        FIRST = proj[-5:]
        AHEAD, AHEAD_R = 5, 3

        def bank_of(it, kind, n):
            i = proj.index((kind, n)) + AHEAD
            return i % 2, it * (len(proj) // 2) + i // 2 + 1

        def rope_of(it, kind, n):
            i = ropes.index((kind, n)) + AHEAD_R
            return i % 2, it * len(ropes) + i + 1

        def quarter_of(it, u):
            return it * UNITS + u - GRP, (u // GRP - 1) % 2, u % GRP

        def groups(e, before, body, after=None):
            with e.Fori(0, NB // 2) as pair:
                before(pair)
                body(pair, 0, pair * KVH, True, False)
                with e.Fori(1, KVH - 1) as g:
                    body(pair, g, pair * KVH + g, False, False)
                body(pair, KVH - 1, pair * KVH + (KVH - 1), False, True)
                if after:
                    after(pair, pair * KVH + KVH)

        def head(i):
            return slice(i * HD, (i + 1) * HD)

        def prepare(u, last):
            steps = {0: [("Q", 2)], 1: [("Q", 3)], 2: [("Q", 4), ("K", 1)], 3: [("Q", 5), ("V", 1), ("N", 1)],
                     4: [("Q", 6)], 5: [("Q", 7)], 6: [("Q", 8), ("K", 2)], 7: [("Q", 9), ("V", 2), ("N", 2)]}[u]
            return [x for x in steps if not (last and u >= 6)]

        block = st.enter_context(nc.Block())

        @block.sync
        def _(e):
            def load_qkv(g, it):
                e.wait_ge(w_low["wkv"], it)
                cols = bass.ds(g * HD, HD)
                for i, w in enumerate((wk, wv)):
                    e.dma_start(wkv_raw[:, i], w[:, cols].rearrange("(t p) n -> p t n", p=P)).then_inc(raw_in["wkv"], 16)
                for two in range(GRP // 2):
                    e.wait_ge(w_low["wq"], it * GRP + 2 * two)
                    e.dma_start(wq_raw[:, :, :], wq[:, bass.ds((g * GRP + 2 * two) * HD, 2 * HD)]
                                .rearrange("(t p) n -> p t n", p=P)).then_inc(raw_in["wq"], 16)

            def load_wo(g, it):
                e.wait_ge(w_low["wo"], it * DT)
                e.dma_start(wo_raw[:, :, :], wo[bass.ds(g * GRP * HD, GRP * HD), :]
                            .rearrange("(t p) n -> p t n", p=P)).then_inc(raw_in["wo"], 16)

            def before(pair):
                load_qkv(0, pair * KVH)
                load_wo(0, pair * KVH)

            def body(pair, g, it, first, last):
                if not last:
                    load_qkv(g + 1, it + 1)
                    load_wo(g + 1, it + 1)

            for to, table in zip((cos, sin, mask), tables):
                e.dma_start(to[:, :], table).then_inc(tables_in, 16)
            groups(e, before, body)

        @block.tensor
        def _(e):
            def layernorm_sums(pair):
                for half in range(2):
                    for d in range(DT):
                        mm = e.matmul(mean_bank[half], ones[:, :], xt[:, d, bass.ts(pair * 2 + half, S)],
                                      start=d == 0, stop=d == DT - 1)
                    mm.then_inc(ln_mean, 1)
                for half in range(2):
                    for d in range(DT):
                        e.wait_ge(ln_squared, pair * 2 * DT + half * DT + d + 1)
                        e.matmul(var_bank[half], ones[:, :], sq[:, d, :], start=d == 0, stop=d == DT - 1)\
                            .then_inc(ln_summed, 1)

            def three(out, w, z, first, last, **kw):
                for n, (a, b) in enumerate([(w[0], z[0]), (w[0], z[1]), (w[1], z[0])]):
                    mm = e.matmul(out, a, b, start=first and n == 0, stop=last and n == 2, **kw)
                return mm

            def project(it, kind, n):
                k, count = bank_of(it, kind, n)
                e.wait_ge(ring_free[k], count - 1)
                if kind == "Q":
                    i, b = n % GRP, n // GRP % 2
                    e.wait_ge(w_low["wq"], it * GRP + (GRP if n >= UNITS else 0) + i + 1)
                    w = [x[:, :, head(i)] for x in (wqh, wql)]
                elif kind in "KV":
                    b = n % 2
                    e.wait_ge(w_low["wkv"], it + (1 if n >= 2 else 0) + 1)
                    w = [x[:, 0 if kind == "K" else 1] for x in (wkvh, wkvl)]
                if kind == "N":
                    e.wait_ge(vt_ready, it * 2 + n + 1)
                    for t in range(ST):
                        mm = e.transpose(ring[k][:, t * HD:(t + 1) * HD], vt[:, t * P:(t + 1) * P], ident[:, :])
                else:
                    for d in range(DT):
                        mm = three(ring[k][:, :], [x[:, d, :] for x in w],
                                   [y[:, d, b * S:(b + 1) * S] for y in (yh, yl)], d == 0, d == DT - 1)
                mm.then_inc(ring_full[k], 1)

            def score(it, n):
                before = rope_of(it, "Q", n) if n > 1 else rope_of(it - 1, "Q", 9)
                e.wait_ge(rope_low, before[1] + 2)
                if n % GRP == 0:
                    e.wait_ge(rope_low, rope_of(it, "K", n // GRP)[1] + 2)
                e.wait_ge(s_max, (it * UNITS + n) * ST)
                for t in range(ST):
                    keys = slice(max(t - 1, 0) * P, (t + 1) * P)
                    mm = three(scores[:, t, (P if t == 0 else 0):], [x[:, n % 2, t * P:(t + 1) * P] for x in (qh, ql)],
                               [x[:, n // GRP % 2, keys] for x in (kh, kl)], True, True)
                mm.then_inc(s_full, 1)

            def turn(it, u):
                e.wait_ge(p_ready, it * UNITS + u + 1)
                e.wait_ge(pt_low, it * UNITS + u)
                for k in range(ST):
                    mm = e.transpose(pt[:, 2 * k * P:(2 * k + 1) * P], probs[:, u % 2, k, P:2 * P], ident[:, :])
                    if k + 1 < ST:
                        e.transpose(pt[:, (2 * k + 1) * P:(2 * k + 2) * P], probs[:, u % 2, k + 1, 0:P], ident[:, :])
                mm.then_inc(pt_full, 1)

            def weigh(it, u):
                b = u // GRP
                e.wait_ge(pt_low, it * UNITS + u + 1)
                e.wait_ge(v_low, it * 2 + b + 1)
                e.wait_ge(o_low, it * UNITS + u)
                for k in range(ST):
                    q = slice(k * P, min(k + 2, ST) * P)
                    cols = slice(2 * k * P, min(2 * k + 2, 2 * ST - 1) * P)
                    mm = three(obank[:, q], [x[:, b, k, :] for x in (vh, vl)], [x[:, cols] for x in (pth, ptl)],
                               k == 0, k == ST - 1, skip_group_check=True)
                mm.then_inc(o_full, 1)

            def project_out(it, u):
                n, half, d = quarter_of(it, u)
                if d == 0:
                    e.wait_ge(o_low, n + GRP)
                if half == 0:
                    e.wait_ge(w_low["wo"], it * DT + d + 1)
                e.wait_ge(w_free, n)
                for i in range(GRP):
                    mm = three(wbank[:, :], [x[:, i, d * P:(d + 1) * P] for x in (woh, wol)],
                               [x[:, half, i, :] for x in (oh, ol)], i == 0, i == GRP - 1)
                mm.then_inc(w_full, 1)

            def before(pair):
                for k in range(2):
                    e.wait_ge(ring_free[k], pair * KVH * (len(proj) // 2))
                e.wait_ge(s_max, pair * (KVH * UNITS * ST))
                layernorm_sums(pair)
                e.wait_ge(ln_yl, pair * 2 * DT + DT)
                for kind, n in FIRST:
                    project(pair * KVH - 1, kind, n)
                e.wait_ge(ln_yl, pair * 2 * DT + 2 * DT)
                e.wait_ge(ln_vare, pair * 2 + 2)
                score(pair * KVH - 1, UNITS)

            def body(pair, g, it, first, last):
                for u in range(UNITS):
                    steps = prepare(u, last)
                    for kind, n in steps[:1]:
                        project(it, kind, n)
                    turn(it, u)
                    if not (last and u == UNITS - 1):
                        score(it, u + 1)
                    if not (first and u < GRP):
                        project_out(it, u)
                    for kind, n in steps[1:]:
                        if kind != "N":
                            project(it, kind, n)
                    weigh(it, u)
                    for kind, n in steps[1:]:
                        if kind == "N":
                            project(it, kind, n)

            def after(pair, it):
                for u in range(GRP):
                    project_out(it, u)

            groups(e, before, body, after)

        @block.vector
        def _(e):
            def centre(pair, half):
                e.wait_ge(ln_mean, pair * 2 + half + 1)
                for d in range(DT):
                    e.tensor_tensor(zf[:, half, d], xt[:, d, bass.ts(pair * 2 + half, S)], mean_bank[half],
                                    ALU.subtract).then_inc(ln_centred, 1)

            def normalise_rows(pair, half, chain):
                t = tmp[half]
                e.wait_ge(ln_summed, (pair * 2 + half + 1) * DT)
                e.tensor_scalar(t[0][:, :], var_bank[half], LN_EPS, None, ALU.add).then_inc(ln_vare, 1)
                e.wait_ge(ln_seed, pair * 2 + half + 1)
                chain(e.scalar_tensor_tensor(t[2][:, :], t[0][:, :], -0.5, t[1][:, :], ALU.mult, ALU.mult))
                chain(e.tensor_tensor(t[2][:, :], t[2][:, :], t[1][:, :], ALU.mult))
                chain(e.scalar_tensor_tensor(t[0][:, :], t[2][:, :], 1.5, t[1][:, :], ALU.add, ALU.mult))
                for d in range(DT):
                    e.tensor_tensor(zf[:, half, d], zf[:, half, d], t[0][:, :], ALU.mult).then_inc(ln_z, 1)
                for d in range(DT):
                    e.wait_ge(ln_yh, (pair * 2 + half) * DT + d + 1)
                    e.tensor_tensor(yl[:, d, half * S:(half + 1) * S], zf[:, half, d],
                                    f32(yh[:, d, half * S:(half + 1) * S]), ALU.subtract).then_inc(ln_yl, 1)

            def find_max(it, n):
                e.wait_ge(s_full, it * UNITS + n + 1)
                e.memset(nothing[:, :], 0.0)
                for t in range(ST):
                    k = slice(P if t == 0 else 0, 2 * P)
                    e.tensor_tensor_reduce(probs[:, n % 2, t, k], scores[:, t, k], mask[:, k], 1.0, BELOW_ALL,
                                           ALU.add, ALU.max, top[:, n % 2, t:t + 1]).then_inc(s_max, 1)
                e.wait_ge(s_max, (it * UNITS + n + 1) * ST)
                e.tensor_scalar(bias[:, n % 2], top[:, n % 2], -SM_SCALE, None, ALU.mult).then_inc(bias_ready, 1)

            def normalise(it, n, chain):
                e.wait_ge(exp_done, (it * UNITS + n + 1) * ST)
                chain(e.reciprocal(share[:, n % 2], total[:, n % 2]))
                for t in range(ST):
                    part = probs[:, n % 2, t, (P if t == 0 else 0):]
                    last = e.tensor_scalar(part, part, share[:, n % 2, t:t + 1], None, ALU.mult)
                last.then_inc(p_ready, 1)

            def rope(it, kind, n):
                k, count = bank_of(it, kind, n)
                slot, r = rope_of(it, kind, n)
                e.wait_ge(ring_full[k], count)
                e.wait_ge(rope_low, r)
                e.tensor_tensor(ra[:, slot], ring[k][:, :], cos[:, :], ALU.mult)
                e.tensor_tensor(rb[0:HALF, slot], ring[k][HALF:, :], sin[HALF:, :], ALU.mult)
                e.tensor_tensor(rb[HALF:, slot], ring[k][0:HALF, :], sin[0:HALF, :], ALU.mult).then_inc(ring_free[k], 1)

            def low_values(it, n):
                k, count = bank_of(it, "N", n)
                e.wait_ge(v_high, it * 2 + n + 1)
                bank = ring[k][:, :].rearrange("p (t d) -> p t d", t=ST)
                e.tensor_tensor(vl[:, n % 2], bank, f32(vh[:, n % 2]), ALU.subtract).then_inc(v_low, 1)
                e.wait_ge(v_low, it * 2 + n + 1)
                e.sem_inc(ring_free[k], 1)

            def low_probs(it, u):
                e.wait_ge(pt_high, it * UNITS + u + 1)
                e.tensor_tensor(ptl[:, :], pt[:, 0:(2 * ST - 1) * P], f32(pth[:, :]), ALU.subtract).then_inc(pt_low, 1)

            def low_out(it, u):
                e.wait_ge(o_high, it * UNITS + u + 1)
                slot = u // GRP, u % GRP
                e.tensor_tensor(ol[:, slot[0], slot[1]], obank[:, :], f32(oh[:, slot[0], slot[1]]), ALU.subtract)\
                    .then_inc(o_low, 1)

            def add_out(pair, it, u):
                n, half, d = quarter_of(it, u)
                here = xt[:, d, bass.ds((pair * 2 + half) * S, S)]
                e.wait_ge(w_full, n + 1)
                e.tensor_tensor(here, here, wbank[:, :], ALU.add).then_inc(w_free, 1)

            def before(pair):
                for half in range(2):
                    centre(pair, half)
                for half in range(2):
                    normalise_rows(pair, half, Chain(e, dve_step, pair * (6 + KVH * UNITS) + 3 * half))
                it = pair * KVH - 1
                e.wait_ge(tables_in, 48)
                for kind, n in FIRST:
                    if kind in "QK":
                        rope(it, kind, n)
                    if kind == "N":
                        low_values(it, n)
                find_max(it, UNITS)
                normalise(it, UNITS, Chain(e, dve_step, pair * (6 + KVH * UNITS) + 6))

            def body(pair, g, it, first, last):
                chain = Chain(e, dve_step, pair * (6 + KVH * UNITS) + 7 + g * UNITS)
                for u in range(UNITS):
                    more = not (last and u == UNITS - 1)
                    steps = prepare(u, last)
                    for kind, n in steps[:1]:
                        rope(it, kind, n)
                    low_probs(it, u)
                    if more:
                        find_max(it, u + 1)
                    if not (first and u < GRP):
                        add_out(pair, it, u)
                    for kind, n in steps[1:]:
                        if kind == "K":
                            rope(it, kind, n)
                    if more:
                        normalise(it, u + 1, chain)
                    low_out(it, u)
                    for kind, n in steps[1:]:
                        if kind == "N":
                            low_values(it, n)

            def after(pair, it):
                for u in range(GRP):
                    add_out(pair, it, u)

            groups(e, before, body, after)

        @block.scalar
        def _(e):
            def square(pair, half):
                for d in range(DT):
                    n = (pair * 2 + half) * DT + d
                    e.wait_ge(ln_centred, n + 1)
                    if half:
                        e.wait_ge(ln_summed, n + 1 - DT)
                    e.activation(sq[:, d], zf[:, half, d], ACT.Square).then_inc(ln_squared, 1)

            def seed_and_high(pair, half):
                t = tmp[half]
                b = pair * 2 + half
                e.wait_ge(ln_vare, b + 1)
                e.activation(t[1][:, :], t[0][:, :], ACT.Ln).then_inc(act_step, 1)
                e.wait_ge(act_step, b + 1)
                e.activation(t[1][:, :], t[1][:, :], ACT.Exp, scale=-0.5).then_inc(ln_seed, 1)
                for d in range(DT):
                    e.wait_ge(ln_z, b * DT + d + 1)
                    e.copy(yh[:, d, half * S:(half + 1) * S], zf[:, half, d]).then_inc(ln_yh, 1)

            def exps(it, n):
                e.wait_ge(bias_ready, it * UNITS + n + 1)
                for t in range(ST):
                    part = probs[:, n % 2, t, (P if t == 0 else 0):]
                    e.activation(part, part, ACT.Exp, bias=bias[:, n % 2, t:t + 1], scale=SM_SCALE,
                                 accum_out=total[:, n % 2, t:t + 1]).then_inc(exp_done, 1)

            def high_rope(it, kind, n):
                slot, r = rope_of(it, kind, n)
                e.wait_ge(roped, r)
                to = (qh if kind == "Q" else kh)[:, n % 2]
                e.copy(to, ra[:, slot]).then_inc(rope_high, 1)

            def keep_values(it, n):
                k, count = bank_of(it, "V", n)
                e.wait_ge(ring_full[k], count)
                e.copy(vt[:, :], ring[k][:, :]).then_inc(vt_ready, 1)
                e.wait_ge(vt_ready, it * 2 + n + 1)
                e.sem_inc(ring_free[k], 1)

            def high_values(it, n):
                k, count = bank_of(it, "N", n)
                e.wait_ge(ring_full[k], count)
                e.copy(vh[:, n % 2], ring[k][:, :].rearrange("p (t d) -> p t d", t=ST)).then_inc(v_high, 1)

            def split_wkv(it):
                e.wait_ge(raw_in["wkv"], 32 * it + 32)
                e.copy(wkvh[:, :], wkv_raw[:, :]).then_inc(w_high["wkv"], 1)

            def split_wq(it, i):
                if i % 2 == 0:
                    e.wait_ge(raw_in["wq"], 32 * it + 8 * i + 16)
                e.copy(wqh[:, :, head(i)], wq_raw[:, :, head(i % 2)]).then_inc(w_high["wq"], 1)

            def split_wo(it, d, first):
                if d == 0:
                    e.wait_ge(raw_in["wo"], 16 * it + 16)
                if not first:
                    e.wait_ge(w_full, quarter_of(it, d)[0] + 1)
                cols = slice(d * P, (d + 1) * P)
                e.copy(woh[:, :, cols], wo_raw[:, :, cols]).then_inc(w_high["wo"], 1)

            def before(pair):
                split_wkv(pair * KVH)
                for i in range(2):
                    split_wq(pair * KVH, i)
                for half in range(2):
                    square(pair, half)
                for half in range(2):
                    seed_and_high(pair, half)
                for i in range(2, GRP):
                    split_wq(pair * KVH, i)
                it = pair * KVH - 1
                for kind, n in FIRST:
                    if kind in "QK":
                        high_rope(it, kind, n)
                    elif kind == "V":
                        keep_values(it, n)
                    else:
                        high_values(it, n)
                exps(it, UNITS)

            def body(pair, g, it, first, last):
                for u in range(UNITS):
                    e.wait_ge(pt_full, it * UNITS + u + 1)
                    e.copy(pth[:, :], pt[:, 0:(2 * ST - 1) * P]).then_inc(pt_high, 1)
                    steps = prepare(u, last)
                    for kind, n in steps[:1]:
                        high_rope(it, kind, n)
                    if not (last and u == UNITS - 1):
                        exps(it, u + 1)
                    for kind, n in steps[1:]:
                        if kind == "K":
                            high_rope(it, kind, n)
                        elif kind == "V":
                            keep_values(it, n)
                    if u < DT:
                        split_wo(it, u, first)
                    if u == 4 and not last:
                        split_wkv(it + 1)
                    e.wait_ge(o_full, it * UNITS + u + 1)
                    if u == 0:
                        e.wait_ge(w_full, it * UNITS - (0 if first else GRP))
                    e.copy(oh[:, u // GRP, u % GRP], obank[:, :]).then_inc(o_high, 1)
                    for kind, n in steps[1:]:
                        if kind == "N":
                            high_values(it, n)
                    if 3 <= u <= 6 and not last:
                        split_wq(it + 1, u - 3)

            groups(e, before, body)

        @block.gpsimd
        def _(e):
            def rope(it, kind, n):
                slot, r = rope_of(it, kind, n)
                k, count = bank_of(it, kind, n)
                e.wait_ge(ring_free[k], count)
                e.tensor_tensor(ra[:, slot], ra[:, slot], rb[:, slot], ALU.add).then_inc(roped, 1)
                e.wait_ge(rope_high, r)
                hi, lo = [x[:, n % 2] for x in ((qh, ql) if kind == "Q" else (kh, kl))]
                e.tensor_tensor(lo, ra[:, slot], f32(hi), ALU.subtract).then_inc(rope_low, 1)

            def split(name, it, lo, raw, hi):
                e.wait_ge(w_high[name], it + 1)
                e.tensor_tensor(lo, raw, f32(hi), ALU.subtract).then_inc(w_low[name], 1)

            def split_wq(it, i):
                split("wq", it * GRP + i, wql[:, :, head(i)], wq_raw[:, :, head(i % 2)], wqh[:, :, head(i)])

            def before(pair):
                split("wkv", pair * KVH, wkvl[:, :], wkv_raw[:, :], wkvh[:, :])
                for i in range(GRP):
                    split_wq(pair * KVH, i)
                for kind, n in FIRST:
                    if kind in "QK":
                        rope(pair * KVH - 1, kind, n)

            def body(pair, g, it, first, last):
                for u in range(UNITS):
                    for kind, n in prepare(u, last):
                        if kind in "QK":
                            rope(it, kind, n)
                    if u < DT:
                        cols = slice(u * P, (u + 1) * P)
                        split("wo", it * DT + u, wol[:, :, cols], wo_raw[:, :, cols], woh[:, :, cols])
                    if u == 4 and not last:
                        split("wkv", it + 1, wkvl[:, :], wkv_raw[:, :], wkvh[:, :])
                    if 3 <= u <= 6 and not last:
                        split_wq(it + 1, u - 3)

            e.sem_inc(rope_low, 2)
            groups(e, before, body)


def rounded(x):
    bits = x.astype(np.float32).view(np.int32)
    return ((bits + 0x7FF + ((bits >> 12) & 1)) & ~0xFFF).view(np.float32)


def alibi_rows():
    slope = ((2.0 ** -0.25) ** np.arange(1, AH + 1, dtype=np.float64)).astype(np.float32).reshape(2, PAIRS, 1)
    pos = np.arange(S, dtype=np.float32)
    high = rounded(slope)
    low = slope - high
    q = np.zeros((2, 16, PAIRS, S), np.float32)
    q[:, 0], q[:, 3] = high, low
    for row, part in ((1, -high * pos), (4, -low * pos)):
        q[:, row] = rounded(part)
        q[:, row + 1] = rounded(part - q[:, row])
    k = np.zeros((2, P, S), np.float32)
    for half in range(2):
        r = 64 * half + R_BIAS
        k[half, r], k[half, r + 3] = pos, pos
        k[half, [r + 1, r + 2, r + 4, r + 5, r + 6, r + 7]] = 1.0
    return q, k


def constants():
    eye = np.eye(P, dtype=np.float32)
    rank = np.broadcast_to(np.arange(SPARSE, 0, -1, dtype=np.float32), (P, SPARSE))
    inv_freq = np.float32(10000.0) ** (-np.arange(HALF, dtype=np.float32) / np.float32(HALF))
    angle = inv_freq[:, None] * np.arange(S, dtype=np.float32)[None, :]
    cos, sin = np.cos(angle), np.sin(angle)
    q, k = np.arange(P)[:, None], np.arange(P)[None, :]
    window = np.where(np.concatenate([k > q, k <= q], axis=1), 0.0, -1.0e30).astype(np.float32)
    after = np.where(k > q, -1.0e30, 0.0).astype(np.float32)
    q_rows, k_rows = alibi_rows()
    return {"q_rows": q_rows, "k_rows": k_rows, "after": after, "before": np.tile(after.T, (1, 4)),
            "cos": np.concatenate([cos, cos]), "sin": np.concatenate([sin, -sin]), "window": window, "eye": eye,
            "ones": np.full((P, P), 1.0 / D, np.float32), "rank": np.ascontiguousarray(rank)}


def program(nc, ins, out):
    with ExitStack() as st:
        sb = sb_in(nc, st)
        ident, ones = sb("ident", [P, P]), sb("ones", [P, P])
        consts = ident, sb("identb", [P, P], BF16), ones, sb("rankb", [P, SPARSE], BF16)
        xt = st.enter_context(nc.sbuf_tensor("xt", [P, DT, TOK], F32))
        ffn_w = [ins[f"L0_ffn_{n}"] for n in ("c1_w", "c2_w", "w1", "w2t")]
        with nc.cleanup_on_exit():
            load_x(nc, ins, ins["L0_attn_a_hidden_states"], xt, consts)
        with nc.cleanup_on_exit():
            causal_attention(nc, [ins[f"L0_attn_a_{n}"] for n in ("Wqkv", "Wo")], xt, consts,
                             [ins[n] for n in ("after", "before", "q_rows", "k_rows")])
        with nc.cleanup_on_exit():
            ffn(nc, "f1_", ffn_w, xt, consts)
        with nc.cleanup_on_exit():
            window_attention(nc, [ins[f"L0_attn_b_{n}"] for n in ("wq", "wk", "wv", "wo")], xt, consts,
                             [ins[n] for n in ("cos", "sin", "window")])
        with nc.cleanup_on_exit():
            ffn(nc, "f2_", ffn_w, xt, consts)
        with nc.cleanup_on_exit():
            store_x(nc, out, xt, consts[0])


_INS = ["L0_attn_a_hidden_states", "L0_attn_a_Wqkv", "L0_attn_a_Wo", "L0_attn_b_wq", "L0_attn_b_wk",
        "L0_attn_b_wv", "L0_attn_b_wo", "L0_ffn_c1_w", "L0_ffn_c2_w", "L0_ffn_w1", "L0_ffn_w2t"]


def kernel(**inputs):
    import concourse.bacc as _bacc
    from concourse.bass_utils import run_bass_kernel_spmd as _run

    nc = _bacc.Bacc("TRN2", target_bir_lowering=False, num_devices=1)
    arrays, aps = {}, {}
    for name, a in [(n, inputs[n]) for n in _INS] + list(constants().items()):
        a = np.ascontiguousarray(a)
        arrays[f"in_{name}"] = a
        aps[name] = nc.dram_tensor(f"in_{name}", a.shape, mybir.dt.from_np(a.dtype), kind="ExternalInput").ap()
    out = nc.dram_tensor("out", (NB, S, D), F32, kind="ExternalOutput").ap()
    program(nc, aps, out)
    r = _run(nc, [arrays], core_ids=[0])
    return r.results[0]["out"]
```
